# Optimizing a Trainium2 kernel written in Bass

```python
import numpy as np
import jax
import jax.numpy as jnp

def _softmax(x, axis=-1):
    return jax.nn.softmax(x, axis=axis)

def _gelu(x):
    return jax.nn.gelu(x, approximate=True)

def _silu(x):
    return jax.nn.silu(x)

def _sigmoid(x):
    return jax.nn.sigmoid(x)

def _layernorm(x, axis=-1, eps=1e-05):
    m = jnp.mean(x, axis=axis, keepdims=True)
    v = jnp.var(x, axis=axis, keepdims=True)
    return (x - m) / jnp.sqrt(v + eps)

def _scatter_add(tgt, idx, src, axis=0):
    return tgt.at[idx].add(src)

def _segment_sum(src, seg, n):
    return jax.ops.segment_sum(src, seg, n)
kernel_name = 'mk_adaln_d2_jaxref_r8_0a7223'

def setup_inputs(seed: int=0):
    np.random.seed(seed)
    _w = jnp.asarray

    def _L0_attn_setup():
        import jax, jax.numpy as jnp
        import numpy as np
        import math
        D_MODEL = 256
        N_HEADS = 16
        HEAD_DIM = D_MODEL // N_HEADS
        key = jax.random.key(seed)
        k1, k2, k3, k4 = jax.random.split(key, 4)
        bs, seq = (2, 256)
        x = jax.random.normal(k1, (bs, seq, D_MODEL), dtype=jnp.float32)
        scale_q = 1.0 / math.sqrt(D_MODEL)
        Wq = jax.random.uniform(k2, (D_MODEL, D_MODEL), jnp.float32, -scale_q, scale_q)
        Wkv = jax.random.uniform(k3, (2 * HEAD_DIM, D_MODEL), jnp.float32, -scale_q, scale_q)
        Wo = jax.random.uniform(k4, (D_MODEL, D_MODEL), jnp.float32, -scale_q, scale_q)
        return {'x': x, 'Wq': Wq, 'Wkv': Wkv, 'Wo': Wo}
    _L0_attn_in = _L0_attn_setup()

    def _L0_ffn_setup():
        import jax, jax.numpy as jnp
        import numpy as np
        TOP_K = 8
        key = jax.random.key(seed)
        k1, k2, k3 = jax.random.split(key, 3)
        B, S, H, E = (4, 512, 256, 64)
        hidden_states = jax.random.normal(k1, (B, S, H), dtype=jnp.float32)
        router_weight = jax.random.normal(k2, (E, H), dtype=jnp.float32)
        router_bias = jnp.zeros((E,), dtype=jnp.float32)
        expert_bias = jax.random.normal(k3, (E, H), dtype=jnp.float32) * 0.1
        return {'hidden_states': hidden_states, 'router_weight': router_weight, 'router_bias': router_bias, 'expert_bias': expert_bias}
    _L0_ffn_in = _L0_ffn_setup()
    _L0_c = _w((lambda *s: np.random.randn(*s).astype(np.float32) * 0.05)(4, 256))
    _L0_wmod = _w((lambda *s: np.random.randn(*s).astype(np.float32) * 0.05)(256, 6 * 256) * 256 ** (-0.5))

    def _L1_attn_setup():
        import jax, jax.numpy as jnp
        import numpy as np
        N_HEADS = 16
        HEAD_DIM = 128
        D_MODEL = 256
        EPS = 1e-05

        def _rmsnorm(x, w):
            rms = jnp.sqrt(jnp.mean(x * x, axis=-1, keepdims=True) + EPS)
            return x / rms * w
        key = jax.random.key(seed)
        ks = jax.random.split(key, 8)
        B, T = (4, 256)
        s = D_MODEL ** (-0.5)
        return {'x': jax.random.normal(ks[0], (B, T, D_MODEL), dtype=jnp.float32), 'Wq': jax.random.normal(ks[1], (N_HEADS * HEAD_DIM, D_MODEL), dtype=jnp.float32) * s, 'Wk': jax.random.normal(ks[2], (N_HEADS * HEAD_DIM, D_MODEL), dtype=jnp.float32) * s, 'Wv': jax.random.normal(ks[3], (N_HEADS * HEAD_DIM, D_MODEL), dtype=jnp.float32) * s, 'Wo': jax.random.normal(ks[4], (D_MODEL, N_HEADS * HEAD_DIM), dtype=jnp.float32) * s, 'gq': jnp.ones((HEAD_DIM,), dtype=jnp.float32), 'gk': jnp.ones((HEAD_DIM,), dtype=jnp.float32)}
    _L1_attn_in = _L1_attn_setup()

    def _L1_ffn_setup():
        import jax, jax.numpy as jnp
        import numpy as np
        HIDDEN = 256
        INTER = 688
        LUT_SIZE = 16

        def _ghost_linear(x, idx, lut):
            w = lut[idx]
            return jnp.einsum('bsh,oh->bso', x, w)
        key = jax.random.key(seed)
        k_x, k_lut, k_g, k_u, k_d = jax.random.split(key, 5)
        x = jax.random.normal(k_x, (2, 512, HIDDEN), dtype=jnp.float32)
        lut = jax.random.normal(k_lut, (LUT_SIZE,), dtype=jnp.float32) * 0.02
        gate_idx = jax.random.randint(k_g, (INTER, HIDDEN), 0, LUT_SIZE, dtype=jnp.int32)
        up_idx = jax.random.randint(k_u, (INTER, HIDDEN), 0, LUT_SIZE, dtype=jnp.int32)
        down_idx = jax.random.randint(k_d, (HIDDEN, INTER), 0, LUT_SIZE, dtype=jnp.int32)
        return {'x': x, 'lut': lut, 'gate_idx': gate_idx, 'up_idx': up_idx, 'down_idx': down_idx}
    _L1_ffn_in = _L1_ffn_setup()
    _L1_c = _w((lambda *s: np.random.randn(*s).astype(np.float32) * 0.05)(4, 256))
    _L1_wmod = _w((lambda *s: np.random.randn(*s).astype(np.float32) * 0.05)(256, 6 * 256) * 256 ** (-0.5))
    _d = {'L0_attn_x': _L0_attn_in['x'], 'L0_attn_Wq': _L0_attn_in['Wq'], 'L0_attn_Wkv': _L0_attn_in['Wkv'], 'L0_attn_Wo': _L0_attn_in['Wo'], 'L0_ffn_router_weight': _L0_ffn_in['router_weight'], 'L0_ffn_router_bias': _L0_ffn_in['router_bias'], 'L0_ffn_expert_bias': _L0_ffn_in['expert_bias'], 'L0_c': _L0_c, 'L0_wmod': _L0_wmod, 'L1_attn_Wq': _L1_attn_in['Wq'], 'L1_attn_Wk': _L1_attn_in['Wk'], 'L1_attn_Wv': _L1_attn_in['Wv'], 'L1_attn_Wo': _L1_attn_in['Wo'], 'L1_attn_gq': _L1_attn_in['gq'], 'L1_attn_gk': _L1_attn_in['gk'], 'L1_ffn_lut': _L1_ffn_in['lut'], 'L1_ffn_gate_idx': _L1_ffn_in['gate_idx'], 'L1_ffn_up_idx': _L1_ffn_in['up_idx'], 'L1_ffn_down_idx': _L1_ffn_in['down_idx'], 'L1_c': _L1_c, 'L1_wmod': _L1_wmod}
    _x0 = _d['L0_attn_x']
    _d['L0_attn_x'] = jax.random.normal(jax.random.fold_in(jax.random.key(seed), 1), (4, 512, 256), dtype=_x0.dtype)
    del _x0
    return _d

def reference(L0_attn_x, L0_attn_Wq, L0_attn_Wkv, L0_attn_Wo, L0_ffn_router_weight, L0_ffn_router_bias, L0_ffn_expert_bias, L0_c, L0_wmod, L1_attn_Wq, L1_attn_Wk, L1_attn_Wv, L1_attn_Wo, L1_attn_gq, L1_attn_gk, L1_ffn_lut, L1_ffn_gate_idx, L1_ffn_up_idx, L1_ffn_down_idx, L1_c, L1_wmod):

    def _L0_attn_ref(x, Wq, Wkv, Wo):
        import jax, jax.numpy as jnp
        import numpy as np
        import math
        D_MODEL = 256
        N_HEADS = 16
        HEAD_DIM = D_MODEL // N_HEADS
        bs, seq, _ = x.shape
        q = x @ Wq.T
        kv = x @ Wkv.T
        k, v = jnp.split(kv, 2, axis=-1)
        q = q.reshape(bs, seq, N_HEADS, HEAD_DIM).transpose(0, 2, 1, 3)
        attn = jnp.einsum('bhqd,bkd->bhqk', q, k) / math.sqrt(HEAD_DIM)
        causal = jnp.tril(jnp.ones((seq, seq), dtype=bool))
        attn = jnp.where(causal[None, None], attn, jnp.float32(-1000000000.0))
        attn = jax.nn.softmax(attn, axis=-1)
        out = jnp.einsum('bhqk,bkd->bhqd', attn, v)
        out = out.transpose(0, 2, 1, 3).reshape(bs, seq, D_MODEL)
        return out @ Wo.T

    def _L0_ffn_ref(hidden_states, router_weight, router_bias, expert_bias):
        import jax, jax.numpy as jnp
        import numpy as np
        TOP_K = 8
        B, S, H = hidden_states.shape
        flat = hidden_states.reshape(B * S, H)
        logits = jnp.einsum('th,eh->te', flat, router_weight) + router_bias
        scores = jax.nn.softmax(logits, axis=-1)
        topk_w, topk_idx = jax.lax.top_k(scores, TOP_K)
        gathered_bias = expert_bias[topk_idx]
        out = flat * jnp.sum(topk_w, axis=-1, keepdims=True) + jnp.einsum('tk,tkh->th', topk_w, gathered_bias)
        return out.reshape(B, S, H)

    def _L1_attn_ref(x, Wq, Wk, Wv, Wo, gq, gk):
        import jax, jax.numpy as jnp
        import numpy as np
        N_HEADS = 16
        HEAD_DIM = 128
        D_MODEL = 256
        EPS = 1e-05

        def _rmsnorm(x, w):
            rms = jnp.sqrt(jnp.mean(x * x, axis=-1, keepdims=True) + EPS)
            return x / rms * w
        B, T, _ = x.shape
        H, hd = (N_HEADS, HEAD_DIM)
        q = (x @ Wq.T).reshape(B, T, H, hd)
        k = (x @ Wk.T).reshape(B, T, H, hd)
        v = (x @ Wv.T).reshape(B, T, H, hd)
        q = _rmsnorm(q, gq)
        k = _rmsnorm(k, gk)
        q = q.transpose(0, 2, 1, 3)
        k = k.transpose(0, 2, 1, 3)
        v = v.transpose(0, 2, 1, 3)
        scale = hd ** (-0.5)
        scores = jnp.einsum('bhqd,bhkd->bhqk', q, k) * scale
        q_idx = jnp.arange(T)[:, None]
        k_idx = jnp.arange(T)[None, :]
        mask = k_idx > q_idx
        scores = jnp.where(mask[None, None], -jnp.inf, scores)
        attn = jax.nn.softmax(scores.astype(jnp.float32), axis=-1).astype(q.dtype)
        out = jnp.einsum('bhqk,bhkd->bhqd', attn, v)
        out = out.transpose(0, 2, 1, 3).reshape(B, T, H * hd)
        return out @ Wo.T

    def _L1_ffn_ref(x, lut, gate_idx, up_idx, down_idx):
        import jax, jax.numpy as jnp
        import numpy as np
        HIDDEN = 256
        INTER = 688
        LUT_SIZE = 16

        def _ghost_linear(x, idx, lut):
            w = lut[idx]
            return jnp.einsum('bsh,oh->bso', x, w)
        gate = _ghost_linear(x, gate_idx, lut)
        up = _ghost_linear(x, up_idx, lut)
        h = jax.nn.silu(gate) * up
        return _ghost_linear(h, down_idx, lut)
    x = L0_attn_x
    mod = (_silu(L0_c) @ L0_wmod).reshape(L0_c.shape[0], 6, 1, -1)
    sa, ca, ga, sb, cb, gb = (mod[:, 0], mod[:, 1], mod[:, 2], mod[:, 3], mod[:, 4], mod[:, 5])
    ga = (2 * (ga >= 0) - 1) * jnp.maximum(jnp.abs(ga), 0.25)
    gb = (2 * (gb >= 0) - 1) * jnp.maximum(jnp.abs(gb), 0.25)
    h = _layernorm(x, axis=-1) * (1 + ca) + sa
    x = x + ga * _L0_attn_ref(h, L0_attn_Wq, L0_attn_Wkv, L0_attn_Wo)
    h = _layernorm(x, axis=-1) * (1 + cb) + sb
    x = x + gb * _L0_ffn_ref(h, L0_ffn_router_weight, L0_ffn_router_bias, L0_ffn_expert_bias)
    mod = (_silu(L1_c) @ L1_wmod).reshape(L1_c.shape[0], 6, 1, -1)
    sa, ca, ga, sb, cb, gb = (mod[:, 0], mod[:, 1], mod[:, 2], mod[:, 3], mod[:, 4], mod[:, 5])
    ga = (2 * (ga >= 0) - 1) * jnp.maximum(jnp.abs(ga), 0.25)
    gb = (2 * (gb >= 0) - 1) * jnp.maximum(jnp.abs(gb), 0.25)
    h = _layernorm(x, axis=-1) * (1 + ca) + sa
    x = x + ga * _L1_attn_ref(h, L1_attn_Wq, L1_attn_Wk, L1_attn_Wv, L1_attn_Wo, L1_attn_gq, L1_attn_gk)
    h = _layernorm(x, axis=-1) * (1 + cb) + sb
    x = x + gb * _L1_ffn_ref(h, L1_ffn_lut, L1_ffn_gate_idx, L1_ffn_up_idx, L1_ffn_down_idx)
    return x

_drawn_inputs = setup_inputs


def setup_inputs(seed=0):
    import zlib

    import numpy as np

    out = dict(_drawn_inputs(seed))
    spreads = {'L0_ffn_router_bias': (0.0, 2.0), 'L1_attn_gq': (1.0, 0.6), 'L1_attn_gk': (1.0, 0.6)}
    factors = {'L0_attn_Wq': 8.0,
     'L0_attn_Wkv': 4.256,
     'L0_attn_Wo': 4.024,
     'L1_ffn_lut': 5.586,
     'L0_ffn_router_weight': 2.878,
     'L0_ffn_expert_bias': 2.845}
    for name, (base, spread) in spreads.items():
        noise = np.random.default_rng([zlib.crc32(name.encode()), seed]).standard_normal(out[name].shape)
        drawn = base * np.exp(spread * noise) if base else spread * noise
        out[name] = jnp.asarray(drawn.astype(out[name].dtype))
    for name, factor in factors.items():
        out[name] = (out[name] * factor).astype(out[name].dtype)
    return out
```

```python
from contextlib import ExitStack

import concourse.bass as bass
from concourse import mybir

F32 = mybir.dt.float32
F32R = mybir.dt.float32r
BF16 = mybir.dt.bfloat16
I32 = mybir.dt.int32
ALU = mybir.AluOpType
ACT = mybir.ActivationFunctionType
AX = mybir.AxisListType

P = 128
NB = 4
SEQ = 512
QT = SEQ // P
D = 256
KT = D // P
NH = 16
HD0 = 16
HD1 = 128
HG = 4
NG = NH // HG
ITEMS = HG * QT
NE = 64
TOPK = 8
INTER = 688
MT = -(-INTER // P)
LAST = INTER - (MT - 1) * P
LUT = 16
NMOD = 6
SA, CA, GA, SB, CB, GB = range(NMOD)
EPS = 1e-5
NEG = -1e30
Q_SLOT = (0, 0, 0, 1, 1, 2, 2, 1)
K_SLOT = (0, 1, 2, 0, 1, 0, 1, 2)
SLOTS = len(Q_SLOT)
LAG = 2
LAG1 = 3
SCORE_BANKS = (3, 4, 2)
ORDER = (0, 3, 1, 2)


class Chain:

    def __init__(self, eng, sem):
        self.eng, self.sem, self.base, self.n = eng, sem, 0, 0

    def begin(self, base):
        self.base, self.n = base, 0

    def step(self, ins):
        self.n += 1
        ins.then_inc(self.sem, 1)
        self.eng.wait_ge(self.sem, self.base + self.n)


def f32(ap):
    return ap.bitcast(F32)


def build(nc, a, out):
    x_v = a["x"].rearrange("b (t p) d -> p (b t) d", p=P)
    out_v = out.rearrange("b (t p) d -> p (b t) d", p=P)
    q_parts = nc.dram_tensor("q_parts", (3, D, NB * SEQ), BF16).ap()
    h1_saved = nc.dram_tensor("h1_saved", (NB, P, 2 * KT * SEQ), F32).ap()
    wffn_saved = nc.dram_tensor("wffn_saved", (P, 2 * KT * INTER + MT * D), F32).ap()

    with ExitStack() as top:
        sems = {}

        def sem(name):
            if name not in sems:
                sems[name] = top.enter_context(nc.semaphore(name))
            return sems[name]

        def sb(stack, name, shape, dt=F32):
            return stack.enter_context(nc.sbuf_tensor(name, shape, dt))

        bank = [top.enter_context(nc.psum_tensor(f"bank{i}", [P, 512], F32)) for i in range(8)]

        x = sb(top, "x", [P, NB * QT, D])
        mod1 = sb(top, "mod1", [P, NB, NMOD, D])
        identf = sb(top, "identf", [P, P])
        identb = sb(top, "identb", [P, P], BF16)
        maskb = sb(top, "maskb", [P, P], BF16)
        pad = sb(top, "pad", [P, 32])
        hN = sb(top, "hN", [P, QT, D])
        hH = sb(top, "hH", [P, KT, SEQ], F32R)
        hL = sb(top, "hL", [P, KT, SEQ], F32R)
        stats = sb(top, "stats", [P, QT, 6])
        mv = sb(top, "mv", [P, QT, 2])
        sm = sb(top, "sm", [P, 4, 2 * ITEMS])
        negmax = sb(top, "negmax", [P, ITEMS])
        sums = sb(top, "sums", [P, ITEMS])
        rsum = sb(top, "rsum", [P, ITEMS])
        probs = sb(top, "probs", [P, 4, SEQ])
        ytmp = sb(top, "ytmp", [P, 2, D])

        s0 = ExitStack()
        mod = [sb(s0, "mod0", [P, NB, NMOD, D]), mod1]
        cT = sb(s0, "cT", [P, 2, KT, NB])
        sc = sb(s0, "sc", [P, 2, KT, NB])
        ones = sb(s0, "ones", [P, P])
        cB = sb(s0, "cB", [P, 2, KT, NB, P])
        wmod = sb(s0, "wmod", [P, 2, KT, NMOD * D])
        W0N = D + P + HD0 + D + NE
        w0 = sb(s0, "w0", [P, KT, W0N])
        w0H = sb(s0, "w0H", [P, KT, W0N], F32R)
        w0L = sb(s0, "w0L", [P, KT, W0N], F32R)
        WQ, WK, WV, WO, WR = (slice(o, o + n) for o, n in
                              ((0, D), (D, P), (D + P, HD0), (D + P + HD0, D), (2 * D + P + HD0, NE)))
        ebias = sb(s0, "ebias", [NE, D])
        rbias = sb(s0, "rbias", [P, NE])
        kmask = sb(s0, "kmask", [P, 3])
        q32 = sb(s0, "q32", [P, SEQ])
        qhi = sb(s0, "qhi", [P, 2, SEQ], BF16)
        qmi = sb(s0, "qmi", [P, 2, SEQ], BF16)
        qlo = sb(s0, "qlo", [P, 2, SEQ], BF16)
        kst = sb(s0, "kst", [P, NB * SEQ], BF16)
        v0 = sb(s0, "v0", [P, NB * QT, HD0])
        qst = sb(s0, "qst", [P, NH * SEQ], BF16)
        pT0 = sb(s0, "pT0", [P, 2, SEQ])
        oTok = sb(s0, "oTok", [P, QT, D])
        oH0 = sb(s0, "oH0", [P, KT, SEQ], F32R)
        oL0 = sb(s0, "oL0", [P, KT, SEQ], F32R)
        lg = sb(s0, "lg", [P, QT, NE])
        ex = sb(s0, "ex", [P, QT, NE])
        rest = sb(s0, "rest", [P, QT, NE])
        top8 = sb(s0, "top8", [P, QT, TOPK])
        rsm = sb(s0, "rsm", [P, 4, QT])
        wT = sb(s0, "wT", [NE, SEQ])
        lut = sb(s0, "lut", [P, LUT])
        idx = sb(s0, "idx", [P, MT * D], I32)
        wf = sb(s0, "wf", [P, MT * D])
        wft = sb(s0, "wft", [P, MT * D])
        s0.close()

        s1 = ExitStack()
        wg = sb(s1, "wg", [P, 3 * KT, HG * HD1])
        wgH = sb(s1, "wgH", [P, 3 * KT, HG * HD1], F32R)
        wgL = sb(s1, "wgL", [P, 3 * KT, HG * HD1], F32R)
        wo = sb(s1, "wo", [P, HG, D])
        woH = sb(s1, "woH", [P, HG, D], F32R)
        woL = sb(s1, "woL", [P, HG, D], F32R)
        gqk = sb(s1, "gqk", [P, 3])
        qk = sb(s1, "qk", [P, QT, 2, HG * HD1])
        qkst = sb(s1, "qkst", [P, QT * 2 * HG, 6])
        qT = sb(s1, "qT", [P, HG, SEQ])
        kT = sb(s1, "kT", [P, HG, SEQ])
        v1 = sb(s1, "v1", [P, QT, HG * HD1])
        pT1 = sb(s1, "pT1", [P, 2, QT, SEQ])
        oH1 = sb(s1, "oH1", [P, HG, SEQ], F32R)
        oL1 = sb(s1, "oL1", [P, HG, SEQ], F32R)
        s1.close()

        s2 = ExitStack()
        wgu = sb(s2, "wgu", [P, 2 * KT, INTER])
        wguH = sb(s2, "wguH", [P, 2, KT, MT * P], F32R)
        wguL = sb(s2, "wguL", [P, 2, KT, MT * P], F32R)
        wd = sb(s2, "wd", [P, MT, D])
        wdH = sb(s2, "wdH", [P, MT, D], F32R)
        wdL = sb(s2, "wdL", [P, MT, D], F32R)
        sg = sb(s2, "sg", [P, 2, SEQ])
        hf = sb(s2, "hf", [P, 2, SEQ])
        hmH = sb(s2, "hmH", [P, MT, SEQ], F32R)
        hmL = sb(s2, "hmL", [P, MT, SEQ], F32R)
        s2.close()

        def xb(b, t, n=1):
            return x[:, bass.ds(b * QT + t, n), :]

        def modb(l, b, c):
            return mod[l][:, bass.ds(b, 1), c, :]

        def mm3(pe, o, wH, wL, mH, mL, start, stop):
            pe.matmul(o, wL, mH, start=start, stop=False)
            pe.matmul(o, wH, mL, start=False, stop=False)
            return pe.matmul(o, wH, mH, start=False, stop=stop)

        class Norm:
            def __init__(self, name, layer, c, s):
                self.layer, self.c, self.s = layer, c, s
                self.var, self.rs, self.h, self.tp, self.hi, self.lo = (
                    sem(f"{name}_{w}") for w in ("var", "rs", "h", "tp", "hi", "lo"))
                self.act_sem = sem(f"{name}_act")

            def dve(self, dve, ch, b, r):
                vector_carrier(dve)
                for t in range(QT):
                    last = dve.bn_stats(stats[:, t, :], xb(b, t))
                ch.step(last)
                vector_carrier(dve)
                for t in range(QT):
                    last = dve.bn_aggr(mv[:, t, :], stats[:, t, :])
                ch.step(last)
                v, y, w = sm[:, 0, 0:QT], sm[:, 1, 0:QT], sm[:, 2, 0:QT]
                ins = dve.tensor_scalar(v, mv[:, :, 1], EPS, None, ALU.add)
                ins.then_inc(self.var, 1)
                dve.wait_ge(self.var, r + 1)
                dve.wait_ge(self.rs, r + 1)
                ch.step(dve.tensor_tensor(w, y, y, ALU.mult))
                ch.step(dve.tensor_tensor(w, w, v, ALU.mult))
                ch.step(dve.tensor_scalar(w, w, -0.5, 1.5, ALU.mult, ALU.add))
                ch.step(dve.tensor_tensor(w, w, y, ALU.mult))
                for t in range(QT):
                    last = dve.tensor_scalar(hN[:, t, :], xb(b, t), mv[:, t, 0:1], sm[:, 2, t:t + 1],
                                             ALU.subtract, ALU.mult)
                ch.step(last)
                m, s = modb(self.layer, b, self.c), modb(self.layer, b, self.s)
                ch.step(dve.tensor_tensor(hN[:, :, :], hN[:, :, :], m.to_broadcast([P, QT, D]), ALU.mult))
                dve.tensor_tensor(hN[:, :, :], hN[:, :, :], s.to_broadcast([P, QT, D]),
                                  ALU.add).then_inc(self.h, 1)
                for k in range(KT):
                    dve.wait_ge(self.hi, r * KT + k + 1)
                    dve.tensor_tensor(hL[:, k, :], bank[6 + k][:, :], f32(hH[:, k, :]),
                                      ALU.subtract).then_inc(self.lo, 1)

            def act(self, act, r, free):
                act.wait_ge(self.var, r + 1)
                act.activation(sm[:, 3, 0:QT], sm[:, 0, 0:QT], ACT.Ln).then_inc(self.act_sem, 1)
                act.wait_ge(self.act_sem, r + 1)
                act.activation(sm[:, 1, 0:QT], sm[:, 3, 0:QT], ACT.Exp, scale=-0.5).then_inc(self.rs, 1)
                free()
                for k in range(KT):
                    act.wait_ge(self.tp, r * KT + k + 1)
                    act.activation(hH[:, k, :], bank[6 + k][:, :], ACT.Copy).then_inc(self.hi, 1)

            def pe(self, pe, r):
                pe.wait_ge(self.h, r + 1)
                for k in range(KT):
                    for t in range(QT):
                        last = pe.transpose(bank[6 + k][:, t * P:(t + 1) * P], hN[:, t, k * P:(k + 1) * P],
                                            identf[:, :])
                    last.then_inc(self.tp, 1)

            def wait_ready(self, pe, r):
                pe.wait_ge(self.lo, (r + 1) * KT)

        norm_a0 = Norm("norm_a0", 0, CA, SA)
        norm_f0 = Norm("norm_f0", 0, CB, SB)
        norm_a1 = Norm("norm_a1", 1, CA, SA)
        norm_f1 = Norm("norm_f1", 1, CB, SB)

        loaded_c, loaded_w0, loaded_x, loaded_idx, loaded_misc = map(
            sem, ("loaded_c", "loaded_w0", "loaded_x", "loaded_idx", "loaded_misc"))
        consts, consts_v = sem("consts"), sem("consts_v")
        silu_c, cb_ready, mod_pe, mod_raw, mod_done = map(
            sem, ("silu_c", "cb_ready", "mod_pe", "mod_raw", "mod_done"))
        w0_hi, w0_lo = sem("w0_hi"), sem("w0_lo")
        qkv_pe, q_scaled, q_split, q_stored, k_read, v_read = map(
            sem, ("qkv_pe", "q_scaled", "q_split", "q_stored", "k_read", "v_read"))
        dchain = [sem(f"dve_chain{i}") for i in range(6)]
        q_loaded = sem("q_loaded")
        s0_pe, max0, exp0, t0_pe, ev0, pv0, oev0 = map(
            sem, ("scores0", "max0", "exp0", "turned0", "pT0_ready", "pv0", "o0_ready"))
        ot_pe, ot_hi, ot_lo, y0_pe, x0_add = map(sem, ("oT_pe", "oT_hi", "oT_lo", "y0_pe", "x0_added"))
        r_pe, r_nmax, r_exp, r_w, r_tp, r_wT, r_y, r_done = map(
            sem, ("route_pe", "route_max", "route_exp", "route_w", "route_tp", "route_wT", "route_y", "route_done"))
        h1_stored = sem("h1_stored")
        gat, gat_dma = sem("gathered"), sem("gathered_dma")
        w1_loaded, w1_hi, w1_lo, h1_loaded, gqk_ready = map(
            sem, ("w1_loaded", "w1_hi", "w1_lo", "h1_loaded", "gqk_ready"))
        p1_pe, p1_act, p1_dve, rs_v, rs_a, rs_s, qk_norm = map(
            sem, ("proj1", "proj1_copied", "proj1_stats", "rms_v", "rms_first", "rms_act", "qk_normed"))
        tr_pe, tr_act = sem("qkT_pe"), sem("qkT_ready")
        s1_pe, max1, exp1, nrm1, t1_pe, ev1, pv1, o1_hi, o1_lo, y1_pe, x1_add = map(
            sem, ("scores1", "max1", "exp1", "normed1", "turned1", "pT1_ready", "pv1", "o1_hi", "o1_lo",
                  "y1_pe", "x1_added"))
        y1_gated, rsum1 = sem("y1_gated"), sem("rsum1")
        f_loaded, f_zero, f_hi, f_lo = map(sem, ("f_loaded", "f_zero", "f_hi", "f_lo"))
        gu_pe, f_silu, f_h, f_hhi, f_hlo, y2_pe, x2_add, stored = map(
            sem, ("gateup_pe", "silu", "f_h", "f_h_hi", "f_h_lo", "y2_pe", "x2_added", "stored"))

        carriers = [0]

        def vector_carrier(dve):
            dve.memset(pad[:, carriers[0]:carriers[0] + 1], 0.0)
            carriers[0] += 1

        def tensor_carrier(pe, o):
            pe.matmul(o, identb[:, :], identb[:, :], start=True, stop=True)

        block = top.enter_context(nc.Block())

        @block.sync
        def _(sp):
            sp.dma_start(cT[:, :, :, :], a["cT"]).then_inc(loaded_c, 16)
            for l in range(2):
                sp.dma_start(wmod[:, l, :, :], a[f"wmod{l}"].rearrange("(k p) n -> p k n", p=P)).then_inc(loaded_c, 16)
            for b in range(NB):
                sp.dma_start(x[:, b * QT:(b + 1) * QT, :], x_v[:, b * QT:(b + 1) * QT, :]).then_inc(loaded_x, 16)
            for name, cols in (("wq0", WQ), ("wk0", WK), ("wv0", WV), ("wo0", WO), ("wr", WR)):
                sp.dma_start(w0[:, :, cols], a[name].rearrange("(k p) n -> p k n", p=P)).then_inc(loaded_w0, 16)
            sp.dma_start(ebias[:, :], a["ebias"]).then_inc(loaded_misc, 16)
            sp.dma_start(rbias[:, :], a["rbias"].to_broadcast([P, NE])).then_inc(loaded_misc, 16)
            sp.dma_start(kmask[:, :], a["kmask"]).then_inc(loaded_misc, 16)
            with sp.Fori(0, NB) as b:
                for m in range(KT):
                    sp.wait_ge(q_split, (b * KT + m + 1) * 3)
                    for i, part in enumerate((qhi, qmi, qlo)):
                        sp.dma_start(q_parts[i, m * P:(m + 1) * P, bass.ds(b * SEQ, SEQ)],
                                     part[:, m, :]).then_inc(q_stored, 16)
            sp.wait_ge(k_read, NB)
            sp.wait_ge(q_stored, NB * KT * 3 * 16)
            with sp.Fori(0, NB) as b:
                sp.wait_ge(s0_pe, b * NH * QT)
                for s, part in enumerate(Q_SLOT):
                    sp.dma_start(qst[s * HD0:(s + 1) * HD0, :].rearrange("d (h t) -> d h t", h=NH),
                                 q_parts[part].rearrange("(h d) t -> d h t", d=HD0)[:, :, bass.ds(b * SEQ, SEQ)]
                                 ).then_inc(q_loaded, 16)
                sp.wait_ge(norm_a1.lo, (b + 1) * KT)
                sp.dma_start(h1_saved[b, :, 0:KT * SEQ], f32(hH[:, :, :]).rearrange("p k t -> p (k t)")).then_inc(h1_stored, 16)
                sp.dma_start(h1_saved[b, :, KT * SEQ:], f32(hL[:, :, :]).rearrange("p k t -> p (k t)")).then_inc(h1_stored, 16)
            sp.wait_ge(h1_stored, NB * 32)
            sp.wait_ge(gat_dma, 4 * 16)
            sp.dma_start(gqk[:, 0:2], a["gqk"]).then_inc(gqk_ready, 16)
            with sp.Fori(0, NG) as g:
                sp.wait_ge(w1_lo, g * (3 * KT + HG))
                sp.wait_ge(w1_hi, g * (3 * KT + HG))
                sp.dma_start(wg[:, :, :], a["wqkv"][g].rearrange("p (k n) -> p k n", k=3 * KT)).then_inc(w1_loaded, 16)
                sp.dma_start(wo[:, :, :], a["wo1"][g].rearrange("(h p) n -> p h n", p=P)).then_inc(w1_loaded, 16)
                with sp.Fori(0, NB) as b:
                    it = g * NB + b
                    sp.wait_ge(p1_pe, it * 3 * QT)
                    sp.dma_start(f32(hH[:, :, :]).rearrange("p k t -> p (k t)"), h1_saved[b, :, 0:KT * SEQ]).then_inc(h1_loaded, 16)
                    sp.dma_start(f32(hL[:, :, :]).rearrange("p k t -> p (k t)"), h1_saved[b, :, KT * SEQ:]).then_inc(h1_loaded, 16)
            sp.wait_ge(x1_add, NG * NB * 2)
            sp.dma_start(wgu[:, :, :].rearrange("p k n -> p (k n)"), wffn_saved[:, 0:2 * KT * INTER]).then_inc(f_loaded, 16)
            sp.dma_start(wd[:, :, :].rearrange("p k n -> p (k n)"), wffn_saved[:, 2 * KT * INTER:]).then_inc(f_loaded, 16)
            with sp.Fori(0, NB) as b:
                for t2 in range(2):
                    sp.wait_ge(x2_add, b * 2 + t2 + 1)
                    sp.dma_start(out_v[:, bass.ds(b * QT + 2 * t2, 2), :], xb(b, 2 * t2, 2)).then_inc(stored, 16)
            sp.wait_ge(stored, NB * 2 * 16)

        @block.gpsimd
        def _(pool):
            pool.memset(identf[:, :], 0.0).then_inc(consts, 1)
            pool.memset(ones[:, :], 0.0).then_inc(consts, 1)
            pool.wait_ge(consts, 2)
            pool.affine_select(out=identf[:, :], in_=identf[:, :], compare_op=ALU.not_equal, fill=1.0, base=0,
                               pattern=[[-1, P]], channel_multiplier=1).then_inc(consts, 1)
            pool.affine_select(out=maskb[:, :], in_=ones[:, :], compare_op=ALU.is_ge, fill=NEG, base=0,
                               pattern=[[-1, P]], channel_multiplier=1).then_inc(consts, 1)
            pool.wait_ge(consts, 4)
            pool.tensor_copy(identb[:, :], identf[:, :]).then_inc(consts, 1)
            pool.memset(ones[:, :], 1.0).then_inc(consts, 1)
            n = [0]

            def link(ins):
                n[0] += 1
                ins.then_inc(gat, 1)
                pool.wait_ge(gat, n[0])

            pool.dma_start(lut[:, :], a["lut"].to_broadcast([P, LUT])).then_inc(loaded_idx, 16)
            jobs = [(a[f"idx_{w}"].rearrange("(k p) n -> p k n", p=P), P, 0, KT * INTER, n * KT * INTER)
                    for n, w in enumerate(("gate", "up"))]
            jobs += [(a["idx_down"][0:(MT - 1) * P, :].rearrange("(m p) n -> p m n", p=P), P, 0, (MT - 1) * D,
                      2 * KT * INTER),
                     (a["idx_down"][(MT - 1) * P:, :], LAST, (MT - 1) * D, D, 2 * KT * INTER + (MT - 1) * D)]
            link(pool.memset(wf[:, :], 0.0))
            for i, (src, rows, o, cols, at) in enumerate(jobs):
                part = idx[0:rows, o:o + cols]
                if len(src.shape) == 3:
                    part = part.rearrange("p (k n) -> p k n", k=src.shape[1])
                pool.dma_start(part, src).then_inc(loaded_idx, 16)
                pool.wait_ge(loaded_idx, (i + 2) * 16)
                if i:
                    pool.wait_ge(gat_dma, i * 16)
                if i == 3:
                    link(pool.memset(wf[:, o:o + cols], 0.0))
                part, acc, tmp = idx[0:rows, o:o + cols], wf[0:rows, o:o + cols], wft[0:rows, o:o + cols]
                for j in range(LUT):
                    link(pool.tensor_scalar(tmp if j else acc, part, float(j), lut[0:rows, j:j + 1],
                                            ALU.is_equal, ALU.mult))
                    if j:
                        link(pool.tensor_tensor(acc, acc, tmp, ALU.add))
                pool.dma_start(wffn_saved[:, at:at + cols], wf[:, o:o + cols]).then_inc(gat_dma, 16)

        @block.scalar
        def _(act):
            act.wait_ge(loaded_c, 48)
            act.activation(sc[:, :, :, :], cT[:, :, :, :], ACT.Silu).then_inc(silu_c, 1)
            act.wait_ge(loaded_w0, 5 * 16)
            act.activation(w0H[:, :, :], w0[:, :, :], ACT.Copy).then_inc(w0_hi, 1)

            with act.Fori(0, NB) as b:
                norm_a0.act(act, b, lambda: act.wait_ge(qkv_pe, b * (KT + 2)))
                for m in range(KT):
                    act.wait_ge(qkv_pe, b * (KT + 2) + m + 1)
                    act.wait_ge(q_split, (b * KT + m) * 3)
                    act.activation(q32[:, :], bank[m][:, :], ACT.Copy, scale=HD0 ** -0.5).then_inc(q_scaled, 1)
                act.wait_ge(qkv_pe, (b + 1) * (KT + 2))
                act.activation(v0[:, bass.ds(b * QT, QT), :], bank[3][:, 0:QT * HD0].rearrange("p (t d) -> p t d", d=HD0),
                               ACT.Copy).then_inc(v_read, 1)

            with act.Fori(0, NB) as b:
                with act.Fori(0, NG) as g:
                    it = b * NG + g
                    for i in range(ITEMS):
                        n = (i % QT + 1) * P
                        act.wait_ge(max0, it * ITEMS + i + 1)
                        act.wait_ge(t0_pe, it * ITEMS + max(i - 2, 0))
                        act.activation(probs[:, i % 3, 0:n], bank[i % 3][:, 0:n], ACT.Exp,
                                       bias=negmax[:, i:i + 1], accum_out=sums[:, i:i + 1]).then_inc(exp0, 1)
                for k in range(KT):
                    act.wait_ge(ot_pe, b * KT + k + 1)
                    act.wait_ge(y0_pe, b * 2)
                    act.activation(oH0[:, k, :], bank[k][:, :], ACT.Copy).then_inc(ot_hi, 1)
                norm_f0.act(act, b, lambda: act.wait_ge(h1_stored, b * 32))
                act.wait_ge(r_nmax, b + 1)
                for t in range(QT):
                    act.activation(ex[:, t, :], lg[:, t, :], ACT.Exp, bias=rsm[:, 0, t:t + 1],
                                   accum_out=rsm[:, 1, t:t + 1]).then_inc(r_exp, 1)
                act.wait_ge(r_tp, b + 1)
                act.activation(wT[:, :], bank[5][0:NE, :], ACT.Copy).then_inc(r_wT, 1)
                norm_a1.act(act, b, lambda: act.wait_ge(r_pe, b + 1))

            act.wait_ge(h1_stored, NB * 32)
            act.wait_ge(gqk_ready, 16)
            act.activation(gqk[:, 2:3], gqk[:, 0:1], ACT.Copy, scale=gqk[:, 1:2]).then_inc(gqk_ready, 1)
            act.wait_ge(gqk_ready, 17)
            act.activation(gqk[:, 2:3], gqk[:, 2:3], ACT.Copy, scale=HD1 ** -0.5).then_inc(gqk_ready, 1)
            act.wait_ge(gqk_ready, 18)
            with act.Fori(0, NG) as g:
                act.wait_ge(w1_loaded, (g + 1) * 32)
                act.wait_ge(p1_pe, g * NB * 3 * QT)
                for c in range(3 * KT):
                    act.activation(wgH[:, c, :], wg[:, c, :], ACT.Copy).then_inc(w1_hi, 1)
                act.wait_ge(y1_pe, g * NB * 2)
                for c in range(HG):
                    act.activation(woH[:, c, :], wo[:, c, :], ACT.Copy).then_inc(w1_hi, 1)
                with act.Fori(0, NB) as b:
                    it = g * NB + b
                    act.wait_ge(tr_pe, it * 2 * QT)
                    act.wait_ge(pv1, it * HG)
                    for u in range(3 * QT):
                        act.wait_ge(p1_pe, it * 3 * QT + u + 1)
                        dst = qk[:, u // 2, u % 2, :] if u < 2 * QT else v1[:, u - 2 * QT, :]
                        act.activation(dst, bank[u % 3][:, :], ACT.Copy).then_inc(p1_act, 1)
                        if u == 2 * QT + 1:
                            act.wait_ge(rs_v, it + 1)
                            act.activation(sm[:, 3, :], sm[:, 0, :], ACT.Ln).then_inc(rs_s, 1)
                            act.wait_ge(rs_s, it + 1)
                            act.activation(sm[:, 1, :], sm[:, 3, :], ACT.Exp, scale=-0.5).then_inc(rs_a, 1)
                    for u in range(2 * QT):
                        act.wait_ge(tr_pe, it * 2 * QT + u + 1)
                        t = u // 2
                        dst = (qT, kT)[u % 2][:, :, t * P:(t + 1) * P]
                        act.activation(dst, bank[u % 3][:, :].rearrange("p (h t) -> p h t", h=HG), ACT.Copy,
                                       scale=1.0 if u % 2 else gqk[:, 2:3]).then_inc(tr_act, 1)
                    for s in range(ITEMS + LAG1 + 2):
                        if s < ITEMS:
                            i = s
                            n = (ORDER[i % QT] + 1) * P
                            act.wait_ge(max1, it * ITEMS + i + 1)
                            act.wait_ge(t1_pe, it * ITEMS + max(i - 3, 0))
                            act.activation(probs[:, i % 4, 0:n], bank[SCORE_BANKS[i % 3]][:, 0:n], ACT.Exp,
                                           bias=negmax[:, i:i + 1], accum_out=sums[:, i:i + 1]).then_inc(exp1, 1)
                        i = s - LAG1
                        if 0 <= i < ITEMS:
                            h, t = i // QT, ORDER[i % QT]
                            act.wait_ge(t1_pe, it * ITEMS + i + 1)
                            act.wait_ge(pv1, it * HG + max(h - 1, 0))
                            act.activation(pT1[:, h % 2, 0:t + 1, t * P:(t + 1) * P],
                                           bank[5 + i % 2][:, 0:(t + 1) * P].rearrange("p (k q) -> p k q", q=P),
                                           ACT.Copy).then_inc(ev1, 1)
                        i = s - LAG1 - 2
                        if i >= 0 and i % QT == QT - 1:
                            h = i // QT
                            act.wait_ge(pv1, it * HG + h + 1)
                            act.wait_ge(y1_pe, it * 2)
                            act.activation(oH1[:, h, :], bank[7][:, :], ACT.Copy).then_inc(o1_hi, 1)

            act.wait_ge(f_loaded, 32)
            act.wait_ge(f_zero, 2)
            for w in range(2):
                for k in range(KT):
                    act.activation(wguH[:, w, k, 0:INTER], wgu[:, w * KT + k, :], ACT.Copy).then_inc(f_hi, 1)
            act.activation(wdH[:, :, :], wd[:, :, :], ACT.Copy).then_inc(f_hi, 1)
            with act.Fori(0, NB) as b:
                norm_f1.act(act, b, lambda: act.wait_ge(gu_pe, b * MT))
                for m in range(MT):
                    act.wait_ge(gu_pe, b * MT + m + 1)
                    act.wait_ge(f_h, b * MT + max(m - 1, 0))
                    act.activation(sg[:, m % 2, :], bank[2 * (m % 2)][:, :], ACT.Silu).then_inc(f_silu, 1)
                    act.wait_ge(f_h, b * MT + m + 1)
                    act.wait_ge(y2_pe, b * 2)
                    act.activation(hmH[:, m, :], hf[:, m % 2, :], ACT.Copy).then_inc(f_hhi, 1)

        @block.vector
        def _(dve):
            chains = [Chain(dve, s) for s in dchain]
            ch = chains[0]
            dve.wait_ge(consts, 6)
            dve.wait_ge(silu_c, 1)
            for l in range(2):
                for k in range(KT):
                    for b in range(NB):
                        last = dve.tensor_scalar(cB[:, l, k, b, :], ones[:, :], sc[:, l, k, b:b + 1], None, ALU.mult)
            last.then_inc(cb_ready, 1)
            u = 0
            for l in range(2):
                for b in range(NB):
                    for c in range(NMOD * D // 512):
                        dve.wait_ge(mod_pe, u + 1)
                        dve.tensor_copy(mod[l][:, b, 2 * c:2 * c + 2, :].rearrange("p c d -> p (c d)"),
                                        bank[u % 2][:, :]).then_inc(mod_raw, 1)
                        u += 1
            dve.wait_ge(mod_raw, u)
            for l in range(2):
                for c in (CA, CB):
                    ch.step(dve.tensor_scalar(mod[l][:, :, c, :], mod[l][:, :, c, :], 1.0, None, ALU.add))
                for c in (GA, GB):
                    g, sgn, mag = mod[l][:, :, c, :], probs[:, 0:2, :], hN[:, :, :]
                    sgn = sgn.rearrange("p a n -> p (a n)").rearrange("p (b d) -> p b d", d=D)
                    ch.step(dve.tensor_scalar(sgn, g, 0.0, 2.0, ALU.is_ge, ALU.mult))
                    ch.step(dve.tensor_scalar(mag, g, -1.0, None, ALU.mult))
                    ch.step(dve.tensor_tensor(mag, mag, g, ALU.max))
                    ch.step(dve.tensor_scalar(mag, mag, 0.25, None, ALU.max))
                    ch.step(dve.tensor_scalar(sgn, sgn, -1.0, None, ALU.add))
                    ch.step(dve.tensor_tensor(g, sgn, mag, ALU.mult))
            dve.wait_ge(w0_hi, 1)
            dve.tensor_tensor(w0L[:, :, :], w0[:, :, :], f32(w0H[:, :, :]), ALU.subtract).then_inc(w0_lo, 1)
            dve.wait_ge(loaded_x, NB * 16)
            dve.wait_ge(loaded_misc, 48)

            ch = chains[1]
            with dve.Fori(0, NB) as b:
                ch.begin(b * NA_STEPS)
                norm_a0.dve(dve, ch, b, b)
                for m in range(KT):
                    dve.wait_ge(q_scaled, b * KT + m + 1)
                    dve.wait_ge(q_stored, (b * KT + m) * 3 * 16 if m == 0 else b * KT * 3 * 16)
                    dve.tensor_copy(qhi[:, m, :], q32[:, :]).then_inc(q_split, 1)
                    dve.wait_ge(q_split, (b * KT + m) * 3 + 1)
                    ch.step(dve.tensor_tensor(q32[:, :], q32[:, :], qhi[:, m, :], ALU.subtract))
                    dve.tensor_copy(qmi[:, m, :], q32[:, :]).then_inc(q_split, 1)
                    dve.wait_ge(q_split, (b * KT + m) * 3 + 2)
                    dve.tensor_tensor(qlo[:, m, :], q32[:, :], qmi[:, m, :], ALU.subtract).then_inc(q_split, 1)
                dve.wait_ge(qkv_pe, b * (KT + 2) + KT + 1)
                kb = bank[2][:, :]
                hi, mi, lo = probs[:, 0, :], probs[:, 1, :], probs[:, 2, :]
                hb, mb = qst[:, 0:SEQ], qst[:, SEQ:2 * SEQ]
                ch.step(dve.tensor_copy(hb, kb))
                ch.step(dve.tensor_tensor(lo, kb, hb, ALU.subtract))
                ch.step(dve.tensor_copy(mb, lo))
                ch.step(dve.tensor_tensor(lo, lo, mb, ALU.subtract))
                ch.step(dve.tensor_scalar(lo, lo, kmask[:, 2:3], None, ALU.mult))
                ch.step(dve.scalar_tensor_tensor(out=lo, in0=mb, scalar=kmask[:, 1:2], in1=lo, op0=ALU.mult, op1=ALU.add))
                dve.scalar_tensor_tensor(out=kst[:, bass.ds(b * SEQ, SEQ)], in0=hb, scalar=kmask[:, 0:1], in1=lo,
                                         op0=ALU.mult, op1=ALU.add).then_inc(k_read, 1)
            assert ch.n == NA_STEPS, ch.n

            ch = chains[2]
            with dve.Fori(0, NB) as b:
                with dve.Fori(0, NG) as g:
                    it = b * NG + g
                    for s in range(ITEMS + LAG):
                        if s < ITEMS:
                            i, n = s, (s % QT + 1) * P
                            dve.wait_ge(s0_pe, it * ITEMS + i + 1)
                            dve.tensor_reduce(negmax[:, i:i + 1], bank[i % 3][:, 0:n], AX.X, ALU.max,
                                              negate=True).then_inc(max0, 1)
                        i = s - LAG
                        if i >= 0:
                            n = (i % QT + 1) * P
                            dve.wait_ge(t0_pe, it * ITEMS + i + 1)
                            dve.wait_ge(pv0, it * ITEMS + max(i - 1, 0))
                            dve.tensor_copy(pT0[:, i % 2, 0:n], bank[3 + i % 2][:, 0:n]).then_inc(ev0, 1)
                    dve.wait_ge(exp0, (it + 1) * ITEMS)
                    dve.reciprocal(rsum[:, :], sums[:, :]).then_inc(oev0, 1)
                    dve.wait_ge(oev0, it * 2 + 1)
                    dve.wait_ge(pv0, (it + 1) * ITEMS)
                    dve.wait_ge(ot_pe, b * KT)
                    dve.tensor_tensor(
                        oTok[:, :, bass.ds(g * HG * HD0, HG * HD0)].rearrange("p t (h d) -> p h t d", d=HD0),
                        bank[5][:, 0:ITEMS * HD0].rearrange("p (h t d) -> p h t d", h=HG, d=HD0),
                        rsum[:, :].rearrange("p (h t one) -> p h t one", h=HG, one=1).to_broadcast([P, HG, QT, HD0]),
                        ALU.mult).then_inc(oev0, 1)
                ch.begin(b * NB0_STEPS)
                for k in range(KT):
                    dve.wait_ge(ot_hi, b * KT + k + 1)
                    dve.tensor_tensor(oL0[:, k, :], bank[k][:, :], f32(oH0[:, k, :]), ALU.subtract).then_inc(ot_lo, 1)
                for t2 in range(2):
                    dve.wait_ge(y0_pe, b * 2 + t2 + 1)
                    ch.step(dve.tensor_tensor(ytmp[:, :, :], bank[2 + t2][:, :].rearrange("p (t d) -> p t d", d=D),
                                              modb(0, b, GA).to_broadcast([P, 2, D]), ALU.mult))
                    ch.step(dve.tensor_tensor(xb(b, 2 * t2, 2), xb(b, 2 * t2, 2), ytmp[:, :, :], ALU.add))
                norm_f0.dve(dve, ch, b, b)
                dve.wait_ge(r_pe, b + 1)
                ch.step(dve.tensor_tensor(lg[:, :, :], bank[4][:, 0:QT * NE].rearrange("p (t e) -> p t e", e=NE),
                                          rbias[:, :].rearrange("p (one e) -> p one e", one=1).to_broadcast([P, QT, NE]), ALU.add))
                dve.tensor_reduce(rsm[:, 0, :], lg[:, :, :], AX.X, ALU.max, negate=True).then_inc(r_nmax, 1)
                dve.wait_ge(r_exp, (b + 1) * QT)
                vector_carrier(dve)
                for t in range(QT):
                    last = dve.max(top8[:, t, :], ex[:, t, :])
                ch.step(last)
                vector_carrier(dve)
                for t in range(QT):
                    last = dve.match_replace(rest[:, t, :], top8[:, t, :], ex[:, t, :], 0.0)
                ch.step(last)
                ch.step(dve.tensor_tensor(ex[:, :, :], ex[:, :, :], rest[:, :, :], ALU.subtract))
                ch.step(dve.reciprocal(rsm[:, 2, :], rsm[:, 1, :]))
                ch.step(dve.tensor_reduce(rsm[:, 3, :], ex[:, :, :], AX.X, ALU.add))
                ch.step(dve.tensor_tensor(rsm[:, 3, :], rsm[:, 3, :], rsm[:, 2, :], ALU.mult))
                dve.tensor_tensor(ex[:, :, :], ex[:, :, :], rsm[:, 2, :].rearrange("p (t one) -> p t one", one=1).to_broadcast([P, QT, NE]),
                                  ALU.mult).then_inc(r_w, 1)
                dve.wait_ge(r_y, b + 1)
                for t in range(QT):
                    y = bank[t // 2][:, (t % 2) * D:(t % 2 + 1) * D]
                    ch.step(dve.scalar_tensor_tensor(out=hN[:, t, :], in0=hN[:, t, :], scalar=rsm[:, 3, t:t + 1], in1=y,
                                                     op0=ALU.mult, op1=ALU.add))
                ch.step(dve.tensor_tensor(hN[:, :, :], hN[:, :, :], modb(0, b, GB).to_broadcast([P, QT, D]), ALU.mult))
                dve.tensor_tensor(xb(b, 0, QT), xb(b, 0, QT), hN[:, :, :], ALU.add).then_inc(r_done, 1)
                dve.wait_ge(r_done, b + 1)
                norm_a1.dve(dve, ch, b, b)
            assert ch.n == NB0_STEPS, ch.n

            ch = chains[3]

            def add_y1(it, b):
                for t2 in range(2):
                    dve.wait_ge(y1_pe, it * 2 + t2 + 1)
                    dve.tensor_tensor(ytmp[:, :, :], bank[5 + t2][:, :].rearrange("p (t d) -> p t d", d=D),
                                      modb(1, b, GA).to_broadcast([P, 2, D]), ALU.mult).then_inc(y1_gated, 1)
                    dve.wait_ge(y1_gated, it * 2 + t2 + 1)
                    dve.tensor_tensor(xb(b, 2 * t2, 2), xb(b, 2 * t2, 2), ytmp[:, :, :], ALU.add).then_inc(x1_add, 1)
                    dve.wait_ge(x1_add, it * 2 + t2 + 1)

            def round1(it, before):
                ch.begin(it * N1_STEPS)
                for u in range(2 * QT):
                    dve.wait_ge(p1_act, it * 3 * QT + u + 1)
                    vector_carrier(dve)
                    for h in range(HG):
                        last = dve.bn_stats(qkst[:, u * HG + h, :], qk[:, u // 2, u % 2, h * HD1:(h + 1) * HD1])
                    last.then_inc(p1_dve, 1)
                dve.wait_ge(p1_dve, (it + 1) * 2 * QT)
                v, y, w = sm[:, 0, :], sm[:, 1, :], sm[:, 2, :]
                me, mo = qkst[:, :, 1], qkst[:, :, 4]
                ch.step(dve.tensor_tensor(v, me, me, ALU.mult))
                ch.step(dve.tensor_tensor(w, mo, mo, ALU.mult))
                ch.step(dve.tensor_tensor(v, v, w, ALU.add))
                ch.step(dve.tensor_tensor(w, qkst[:, :, 2], qkst[:, :, 5], ALU.add))
                ch.step(dve.scalar_tensor_tensor(out=v, in0=w, scalar=2.0 / HD1, in1=v, op0=ALU.mult, op1=ALU.add))
                dve.tensor_scalar(v, v, 0.5, EPS, ALU.mult, ALU.add).then_inc(rs_v, 1)
                dve.wait_ge(rs_v, it + 1)
                dve.wait_ge(rs_a, it + 1)
                ch.step(dve.tensor_tensor(w, y, y, ALU.mult))
                ch.step(dve.tensor_tensor(w, w, v, ALU.mult))
                ch.step(dve.tensor_scalar(w, w, -0.5, 1.5, ALU.mult, ALU.add))
                ch.step(dve.tensor_tensor(w, w, y, ALU.mult))
                for u in range(2 * QT):
                    rows = qk[:, u // 2, u % 2, :].rearrange("p (h d) -> p h d", d=HD1)
                    r = sm[:, 2, u * HG:(u + 1) * HG].rearrange("p (h one) -> p h one", one=1)
                    dve.tensor_tensor(rows, rows, r.to_broadcast([P, HG, HD1]), ALU.mult).then_inc(qk_norm, 1)
                if before is not None:
                    add_y1(it - 1, before)
                for s in range(ITEMS + LAG1 + 3):
                    if s < ITEMS:
                        i, n = s, (ORDER[s % QT] + 1) * P
                        dve.wait_ge(s1_pe, it * ITEMS + i + 1)
                        dve.tensor_reduce(negmax[:, i:i + 1], bank[SCORE_BANKS[i % 3]][:, 0:n], AX.X, ALU.max,
                                          negate=True).then_inc(max1, 1)
                    i = s - 1
                    if 0 <= i < ITEMS:
                        dve.wait_ge(exp1, it * ITEMS + i + 1)
                        dve.reciprocal(rsum[:, i:i + 1], sums[:, i:i + 1]).then_inc(rsum1, 1)
                    i = s - 2
                    if 0 <= i < ITEMS:
                        n = (ORDER[i % QT] + 1) * P
                        dve.wait_ge(rsum1, it * ITEMS + i + 1)
                        dve.tensor_scalar(probs[:, i % 4, 0:n], probs[:, i % 4, 0:n], rsum[:, i:i + 1], None,
                                          ALU.mult).then_inc(nrm1, 1)
                    i = s - LAG1 - 3
                    if i >= 0 and i % QT == QT - 1:
                        h = i // QT
                        dve.wait_ge(o1_hi, it * HG + h + 1)
                        dve.tensor_tensor(oL1[:, h, :], bank[7][:, :], f32(oH1[:, h, :]),
                                          ALU.subtract).then_inc(o1_lo, 1)
                assert ch.n == N1_STEPS, ch.n

            with dve.Fori(0, NG) as g:
                for c in range(3 * KT):
                    dve.wait_ge(w1_hi, g * (3 * KT + HG) + c + 1)
                    dve.tensor_tensor(wgL[:, c, :], wg[:, c, :], f32(wgH[:, c, :]), ALU.subtract).then_inc(w1_lo, 1)
                for c in range(HG):
                    dve.wait_ge(w1_hi, g * (3 * KT + HG) + 3 * KT + c + 1)
                    dve.tensor_tensor(woL[:, c, :], wo[:, c, :], f32(woH[:, c, :]), ALU.subtract).then_inc(w1_lo, 1)
                round1(g * NB, None)
                with dve.Fori(1, NB) as b:
                    round1(g * NB + b, b - 1)
                add_y1(g * NB + NB - 1, NB - 1)

            ch = chains[4]
            dve.memset(f32(wguH[:, :, :, :]), 0.0).then_inc(f_zero, 1)
            dve.memset(f32(wguL[:, :, :, :]), 0.0).then_inc(f_zero, 1)
            dve.wait_ge(f_zero, 2)
            for w in range(2):
                for k in range(KT):
                    dve.wait_ge(f_hi, w * KT + k + 1)
                    dve.tensor_tensor(wguL[:, w, k, 0:INTER], wgu[:, w * KT + k, :], f32(wguH[:, w, k, 0:INTER]),
                                      ALU.subtract).then_inc(f_lo, 1)
            dve.wait_ge(f_hi, 2 * KT + 1)
            dve.tensor_tensor(wdL[:, :, :], wd[:, :, :], f32(wdH[:, :, :]), ALU.subtract).then_inc(f_lo, 1)
            with dve.Fori(0, NB) as b:
                ch.begin(b * N2_STEPS)
                norm_f1.dve(dve, ch, b, b)
                for m in range(MT):
                    dve.wait_ge(f_silu, b * MT + m + 1)
                    dve.wait_ge(f_hlo, b * MT + max(m - 1, 0))
                    dve.tensor_tensor(hf[:, m % 2, :], bank[2 * (m % 2) + 1][:, :], sg[:, m % 2, :], ALU.mult).then_inc(f_h, 1)
                    dve.wait_ge(f_hhi, b * MT + m + 1)
                    dve.tensor_tensor(hmL[:, m, :], hf[:, m % 2, :], f32(hmH[:, m, :]), ALU.subtract).then_inc(f_hlo, 1)
                for t2 in range(2):
                    dve.wait_ge(y2_pe, b * 2 + t2 + 1)
                    ch.step(dve.tensor_tensor(ytmp[:, :, :], bank[4 + t2][:, :].rearrange("p (t d) -> p t d", d=D),
                                              modb(1, b, GB).to_broadcast([P, 2, D]), ALU.mult))
                    dve.tensor_tensor(xb(b, 2 * t2, 2), xb(b, 2 * t2, 2), ytmp[:, :, :], ALU.add).then_inc(x2_add, 1)
                    dve.wait_ge(x2_add, b * 2 + t2 + 1)
            assert ch.n == N2_STEPS, ch.n

        @block.tensor
        def _(pe):
            pe.wait_ge(cb_ready, 1)
            pe.wait_ge(loaded_c, 48)
            u = 0
            for l in range(2):
                for b in range(NB):
                    for c in range(NMOD * D // 512):
                        if u >= 2:
                            pe.wait_ge(mod_raw, u - 1)
                        for k in range(KT):
                            last = pe.matmul(bank[u % 2][:, :], cB[:, l, k, b, :], wmod[:, l, k, c * 512:(c + 1) * 512],
                                             start=(k == 0), stop=(k == KT - 1))
                        last.then_inc(mod_pe, 1)
                        u += 1
            pe.wait_ge(mod_raw, u)
            pe.wait_ge(w0_lo, 1)

            with pe.Fori(0, NB) as b:
                norm_a0.pe(pe, b)
                norm_a0.wait_ready(pe, b)
                for m in range(KT + 1):
                    if m < KT:
                        pe.wait_ge(q_scaled, b * KT)
                    else:
                        pe.wait_ge(k_read, b)
                    cols = slice(m * P, (m + 1) * P)
                    for k in range(KT):
                        last = mm3(pe, bank[m][:, :], w0H[:, k, cols], w0L[:, k, cols], hH[:, k, :], hL[:, k, :],
                                   k == 0, k == KT - 1)
                    last.then_inc(qkv_pe, 1)
                pe.wait_ge(v_read, b)
                for t in range(QT):
                    rows = slice(t * P, (t + 1) * P)
                    for k in range(KT):
                        last = mm3(pe, bank[3][:, t * HD0:(t + 1) * HD0], hH[:, k, rows], hL[:, k, rows],
                                   w0H[:, k, WV], w0L[:, k, WV], k == 0, k == KT - 1)
                last.then_inc(qkv_pe, 1)
            pe.wait_ge(k_read, NB)
            pe.wait_ge(v_read, NB)

            with pe.Fori(0, NB) as b:
                with pe.Fori(0, NG) as g:
                    it = b * NG + g
                    pe.wait_ge(q_loaded, (b + 1) * SLOTS * 16)
                    pe.wait_ge(r_done, b)
                    for s in range(ITEMS + 3):
                        if s < ITEMS:
                            i, h, t = s, s // QT, s % QT
                            n = (t + 1) * P
                            pe.wait_ge(exp0, it * ITEMS + max(i - 2, 0))
                            pe.matmul(bank[i % 3][:, 0:n], qst[:, bass.ds((g * HG + h) * SEQ + t * P, P)],
                                      kst[:, bass.ds(b * SEQ, n)], start=True, stop=False)
                            pe.matmul(bank[i % 3][:, t * P:n], identb[:, :], maskb[:, :], start=False,
                                      stop=True).then_inc(s0_pe, 1)
                        i = s - LAG
                        if 0 <= i < ITEMS:
                            t = i % QT
                            pe.wait_ge(exp0, it * ITEMS + i + 1)
                            pe.wait_ge(ev0, it * ITEMS + max(i - 1, 0))
                            for k in range(t + 1):
                                last = pe.transpose(bank[3 + i % 2][:, k * P:(k + 1) * P],
                                                    probs[:, i % 3, k * P:(k + 1) * P], identf[:, :])
                            last.then_inc(t0_pe, 1)
                        i = s - LAG - 1
                        if i >= 0:
                            t = i % QT
                            pe.wait_ge(ev0, it * ITEMS + i + 1)
                            if i == 0:
                                pe.wait_ge(oev0, it * 2)
                            for k in range(t + 1):
                                last = pe.matmul(bank[5][:, i * HD0:(i + 1) * HD0], pT0[:, i % 2, k * P:(k + 1) * P],
                                                 v0[:, bass.ds(b * QT + k, 1), :], start=(k == 0), stop=(k == t))
                            last.then_inc(pv0, 1)
                pe.wait_ge(oev0, (b + 1) * NG * 2)
                for k in range(KT):
                    for t in range(QT):
                        last = pe.transpose(bank[k][:, t * P:(t + 1) * P], oTok[:, t, k * P:(k + 1) * P], identf[:, :])
                    last.then_inc(ot_pe, 1)
                pe.wait_ge(ot_lo, (b + 1) * KT)
                for t in range(QT):
                    rows = slice(t * P, (t + 1) * P)
                    for k in range(KT):
                        last = mm3(pe, bank[2 + t // 2][:, (t % 2) * D:(t % 2 + 1) * D], oH0[:, k, rows], oL0[:, k, rows],
                                   w0H[:, k, WO], w0L[:, k, WO], k == 0, k == KT - 1)
                    if t % 2:
                        last.then_inc(y0_pe, 1)
                norm_f0.pe(pe, b)
                norm_f0.wait_ready(pe, b)
                for t in range(QT):
                    rows = slice(t * P, (t + 1) * P)
                    for k in range(KT):
                        last = mm3(pe, bank[4][:, t * NE:(t + 1) * NE], hH[:, k, rows], hL[:, k, rows],
                                   w0H[:, k, WR], w0L[:, k, WR], k == 0, k == KT - 1)
                last.then_inc(r_pe, 1)
                pe.wait_ge(r_w, b + 1)
                tensor_carrier(pe, bank[5][:, 0:P])
                for t in range(QT):
                    last = pe.transpose(bank[5][0:NE, t * P:(t + 1) * P], ex[:, t, :], identf[:, :])
                last.then_inc(r_tp, 1)
                pe.wait_ge(r_wT, b + 1)
                for t in range(QT):
                    last = pe.matmul(bank[t // 2][:, (t % 2) * D:(t % 2 + 1) * D], wT[:, t * P:(t + 1) * P], ebias[:, :],
                                     start=True, stop=True)
                last.then_inc(r_y, 1)
                norm_a1.pe(pe, b)
                norm_a1.wait_ready(pe, b)

            def out_proj1(it):
                pe.wait_ge(o1_lo, (it + 1) * HG)
                for t in range(QT):
                    rows = slice(t * P, (t + 1) * P)
                    for h in range(HG):
                        last = mm3(pe, bank[5 + t // 2][:, (t % 2) * D:(t % 2 + 1) * D], oH1[:, h, rows], oL1[:, h, rows],
                                   woH[:, h, :], woL[:, h, :], h == 0, h == HG - 1)
                    if t % 2:
                        last.then_inc(y1_pe, 1)

            def round1(g, it, first):
                pe.wait_ge(w1_lo, g * (3 * KT + HG) + (3 * KT if first else 3 * KT + HG))
                pe.wait_ge(h1_loaded, (it + 1) * 32)
                pe.wait_ge(exp1, it * ITEMS)
                for u in range(3 * QT):
                    t, c = (u // 2, u % 2) if u < 2 * QT else (u - 2 * QT, 2)
                    if u >= 3:
                        pe.wait_ge(p1_act, it * 3 * QT + u - 2)
                    else:
                        pe.wait_ge(tr_act, it * 2 * QT)
                    rows = slice(t * P, (t + 1) * P)
                    for k in range(KT):
                        w = c * KT + k
                        last = mm3(pe, bank[u % 3][:, :], hH[:, k, rows], hL[:, k, rows], wgH[:, w, :], wgL[:, w, :],
                                   k == 0, k == KT - 1)
                    last.then_inc(p1_pe, 1)
                if not first:
                    out_proj1(it - 1)
                pe.wait_ge(p1_act, (it + 1) * 3 * QT)
                for u in range(2 * QT):
                    pe.wait_ge(qk_norm, it * 2 * QT + u + 1)
                    if u >= 3:
                        pe.wait_ge(tr_act, it * 2 * QT + u - 2)
                    for h in range(HG):
                        last = pe.transpose(bank[u % 3][:, h * P:(h + 1) * P],
                                            qk[:, u // 2, u % 2, h * HD1:(h + 1) * HD1], identf[:, :])
                    last.then_inc(tr_pe, 1)
                for s in range(ITEMS + LAG1 + 1):
                    if s < ITEMS:
                        i, h, t = s, s // QT, ORDER[s % QT]
                        n = (t + 1) * P
                        if i < QT:
                            pe.wait_ge(tr_act, it * 2 * QT + 2 * (t + 1))
                        pe.wait_ge(exp1, it * ITEMS + max(i - 2, 0))
                        pe.matmul(bank[SCORE_BANKS[i % 3]][:, 0:n], qT[:, h, t * P:n], kT[:, h, 0:n], start=True, stop=False)
                        pe.matmul(bank[SCORE_BANKS[i % 3]][:, t * P:n], identb[:, :], maskb[:, :], start=False,
                                  stop=True).then_inc(s1_pe, 1)
                    i = s - LAG1
                    if 0 <= i < ITEMS:
                        t = ORDER[i % QT]
                        if i == 0:
                            pe.wait_ge(x1_add, it * 2)
                        pe.wait_ge(nrm1, it * ITEMS + i + 1)
                        pe.wait_ge(ev1, it * ITEMS + max(i - 1, 0))
                        for k in range(t + 1):
                            last = pe.transpose(bank[5 + i % 2][:, k * P:(k + 1) * P],
                                                probs[:, i % 4, k * P:(k + 1) * P], identf[:, :])
                        last.then_inc(t1_pe, 1)
                    i = s - LAG1 - 1
                    if 0 <= i and i % QT == QT - 1:
                        h = i // QT
                        pe.wait_ge(ev1, it * ITEMS + i + 1)
                        pe.wait_ge(o1_lo, it * HG + h)
                        for k in range(QT):
                            last = pe.matmul(bank[7][:, k * P:], v1[:, k, h * HD1:(h + 1) * HD1],
                                             pT1[:, h % 2, k, k * P:], start=(k == 0), stop=(k == QT - 1))
                        last.then_inc(pv1, 1)

            with pe.Fori(0, NG) as g:
                round1(g, g * NB, True)
                with pe.Fori(1, NB) as b:
                    round1(g, g * NB + b, False)
                out_proj1(g * NB + NB - 1)

            pe.wait_ge(f_lo, 2 * KT + 1)
            with pe.Fori(0, NB) as b:
                norm_f1.pe(pe, b)
                norm_f1.wait_ready(pe, b)
                for m in range(MT):
                    pe.wait_ge(f_h, b * MT + max(m - 1, 0))
                    for w in range(2):
                        for k in range(KT):
                            last = mm3(pe, bank[2 * (m % 2) + w][:, :], wguH[:, w, k, m * P:(m + 1) * P],
                                       wguL[:, w, k, m * P:(m + 1) * P], hH[:, k, :], hL[:, k, :], k == 0, k == KT - 1)
                    last.then_inc(gu_pe, 1)
                pe.wait_ge(f_hlo, (b + 1) * MT)
                pe.wait_ge(x2_add, b * 2)
                for t in range(QT):
                    rows = slice(t * P, (t + 1) * P)
                    for m in range(MT):
                        last = mm3(pe, bank[4 + t // 2][:, (t % 2) * D:(t % 2 + 1) * D], hmH[:, m, rows], hmL[:, m, rows],
                                   wdH[:, m, :], wdL[:, m, :], m == 0, m == MT - 1)
                    if t % 2:
                        last.then_inc(y2_pe, 1)


NORM_STEPS = 2 + 4 + 1 + 1
NA_STEPS = NORM_STEPS + KT + 6
NB0_STEPS = 4 + NORM_STEPS + 1 + 2 + 4 + QT + 1 + NORM_STEPS
N1_STEPS = 5 + 4
N2_STEPS = NORM_STEPS + 2


def kernel(**inputs):
    import numpy as np
    import concourse.bacc as bacc
    from concourse.bass_utils import run_bass_kernel_spmd

    i = {k: np.asarray(v) for k, v in inputs.items()}
    kmask = np.zeros((P, 3), np.float32)
    for s, part in enumerate(K_SLOT):
        kmask[s * HD0:(s + 1) * HD0, part] = 1
    wk, wv = i["L0_attn_Wkv"][:HD0], i["L0_attn_Wkv"][HD0:]
    wqkv = np.stack([i[f"L1_attn_W{c}"].T for c in "qkv"]).reshape(3, KT, P, NG, HG * HD1)
    arrays = {
        "x": i["L0_attn_x"],
        "cT": np.stack([i[f"L{l}_c"].T for l in range(2)]).reshape(2, KT, P, NB).transpose(2, 0, 1, 3),
        "wmod0": i["L0_wmod"],
        "wmod1": i["L1_wmod"],
        "wq0": i["L0_attn_Wq"].T,
        "wk0": np.tile(wk.T, (1, SLOTS)),
        "wv0": wv.T,
        "wo0": i["L0_attn_Wo"].T,
        "wr": i["L0_ffn_router_weight"].T,
        "ebias": i["L0_ffn_expert_bias"],
        "rbias": i["L0_ffn_router_bias"].reshape(1, NE),
        "kmask": kmask,
        "wqkv": wqkv.transpose(3, 2, 0, 1, 4).reshape(NG, P, 3 * KT * HG * HD1),
        "wo1": i["L1_attn_Wo"].T.reshape(NG, HG * HD1, D),
        "gqk": np.stack([i["L1_attn_gq"], i["L1_attn_gk"]], axis=1),
        "lut": i["L1_ffn_lut"].reshape(1, LUT),
        "idx_gate": i["L1_ffn_gate_idx"].T,
        "idx_up": i["L1_ffn_up_idx"].T,
        "idx_down": i["L1_ffn_down_idx"].T,
    }
    arrays = {k: np.ascontiguousarray(v) for k, v in arrays.items()}
    nc = bacc.Bacc("TRN2", target_bir_lowering=False, num_devices=1)
    aps = {k: nc.dram_tensor(f"in_{k}", v.shape, mybir.dt.from_np(v.dtype), kind="ExternalInput").ap()
           for k, v in arrays.items()}
    out = nc.dram_tensor("out", (NB, SEQ, D), F32, kind="ExternalOutput").ap()
    build(nc, aps, out)
    r = run_bass_kernel_spmd(nc, [{f"in_{k}": v for k, v in arrays.items()}], core_ids=[0])
    return r.results[0]["out"]
```

```python
from contextlib import ExitStack

import concourse.bass as bass
from concourse import mybir

F32 = mybir.dt.float32
F32R = mybir.dt.float32r
BF16 = mybir.dt.bfloat16
I32 = mybir.dt.int32
ALU = mybir.AluOpType
ACT = mybir.ActivationFunctionType
AX = mybir.AxisListType

P = 128
NB = 4
SEQ = 512
QT = SEQ // P
D = 256
KT = D // P
NH = 16
HD0 = 16
HD1 = 128
HG = 4
NG = NH // HG
ITEMS = HG * QT
ITEMS0 = NH * QT
NE = 64
TOPK = 8
INTER = 688
MT = -(-INTER // P)
LAST = INTER - (MT - 1) * P
LUT = 16
NMOD = 6
SA, CA, GA, SB, CB, GB = range(NMOD)
LATER_MODS = ((0, 1), (0, 2), (1, 0), (1, 1), (1, 2))
NEWTON = 3
NORM_PARTS = 11 + NEWTON
EPS = 1e-5
NEG = -1e30
Q_SLOT = (0, 0, 0, 1, 1, 2, 2, 1)
K_SLOT = (0, 1, 2, 0, 1, 0, 1, 2)
SLOTS = len(Q_SLOT)
LAG = 3
LAG1 = 3
SCORE_BANKS = (3, 4, 2)
ORDER = (0, 3, 1, 2)


class Chain:

    def __init__(self, eng, sem):
        self.eng, self.sem, self.base, self.n = eng, sem, 0, 0

    def begin(self, base):
        self.base, self.n = base, 0

    def mark(self, ins):
        self.n += 1
        ins.then_inc(self.sem, 1)

    def wait(self):
        self.eng.wait_ge(self.sem, self.base + self.n)

    def step(self, ins):
        self.mark(ins)
        self.wait()


def rsqrt_seed(dve, ch, y, t, v):
    ch.step(dve.tensor_scalar(t.bitcast(I32), v.bitcast(I32), 1, None, ALU.arith_shift_right))
    ch.mark(dve.tensor_scalar(y.bitcast(I32), t.bitcast(I32), -1.0, float(0x5F3759DF), ALU.mult, ALU.add))


def rsqrt_newton(dve, ch, y, t, v):
    ch.wait()
    ch.step(dve.tensor_tensor(t, y, y, ALU.mult))
    ch.step(dve.scalar_tensor_tensor(out=t, in0=t, scalar=-0.5, in1=v, op0=ALU.mult, op1=ALU.mult))
    ch.mark(dve.scalar_tensor_tensor(out=y, in0=t, scalar=1.5, in1=y, op0=ALU.add, op1=ALU.mult))


def f32(ap):
    return ap.bitcast(F32)


def build(nc, a, out):
    x_v = a["x"].rearrange("b (t p) d -> p (b t) d", p=P)
    out_v = out.rearrange("b (t p) d -> p (b t) d", p=P)
    q_parts = nc.dram_tensor("q_parts", (3, D, NB * SEQ), BF16).ap()
    h1_saved = nc.dram_tensor("h1_saved", (NB, P, 2 * KT * SEQ), F32).ap()
    wffn_saved = nc.dram_tensor("wffn_saved", (P, 2 * KT * INTER + MT * D), F32).ap()

    with ExitStack() as top:
        sems = {}

        def sem(name):
            if name not in sems:
                sems[name] = top.enter_context(nc.semaphore(name))
            return sems[name]

        def sb(stack, name, shape, dt=F32):
            return stack.enter_context(nc.sbuf_tensor(name, shape, dt))

        bank = [top.enter_context(nc.psum_tensor(f"bank{i}", [P, 512], F32)) for i in range(8)]

        x = sb(top, "x", [P, NB * QT, D])
        mod1 = sb(top, "mod1", [P, NB, NMOD, D])
        identf = sb(top, "identf", [P, P])
        identb = sb(top, "identb", [P, P], BF16)
        maskb = sb(top, "maskb", [P, P], BF16)
        pad = sb(top, "pad", [P, 64])
        hN = sb(top, "hN", [P, QT, D])
        hH = sb(top, "hH", [P, KT, SEQ], F32R)
        hL = sb(top, "hL", [P, KT, SEQ], F32R)
        gqk = sb(top, "gqk", [P, 3])
        stats = sb(top, "stats", [P, QT, 6])
        mv = sb(top, "mv", [P, QT, 2])
        sm = sb(top, "sm", [P, 4, 2 * ITEMS])
        negmax = sb(top, "negmax", [P, ITEMS0])
        sums = sb(top, "sums", [P, ITEMS0])
        rsum = sb(top, "rsum", [P, ITEMS0])
        probs = sb(top, "probs", [P, 4, SEQ])
        ytmp = sb(top, "ytmp", [P, 2, D])

        s0 = ExitStack()
        wmod = sb(s0, "wmod", [P, 2, KT, NMOD * D])
        qhi = sb(s0, "qhi", [P, 2, SEQ], BF16)
        qmi = sb(s0, "qmi", [P, 2, SEQ], BF16)
        qlo = sb(s0, "qlo", [P, 2, SEQ], BF16)
        cB = sb(s0, "cB", [P, 2, KT, 1, P])
        qst = sb(s0, "qst", [P, NH * SEQ], BF16)
        mod = [sb(s0, "mod0", [P, NB, NMOD, D]), mod1]
        cT = sb(s0, "cT", [P, 2, KT, NB])
        sc = sb(s0, "sc", [P, 2, KT, NB])
        ones = sb(s0, "ones", [P, P])
        cB0 = sb(s0, "cB0", [P, KT, NB, P])
        W0N = D + P + HD0 + D + NE
        w0 = sb(s0, "w0", [P, KT, W0N])
        w0H = sb(s0, "w0H", [P, KT, W0N], F32R)
        w0L = sb(s0, "w0L", [P, KT, W0N], F32R)
        WQ, WK, WV, WO, WR = (slice(o, o + n) for o, n in
                              ((0, D), (D, P), (D + P, HD0), (D + P + HD0, D), (2 * D + P + HD0, NE)))
        ebias = sb(s0, "ebias", [NE, D])
        rbias = sb(s0, "rbias", [P, NE])
        kmask = sb(s0, "kmask", [P, 3])
        q32 = probs[:, 0:KT, :]
        sgn = hN[:, 0:2, :]
        kst = sb(s0, "kst", [P, NB * SEQ], BF16)
        v0 = sb(s0, "v0", [P, NB * QT, 2 * HD0])
        rsum0_t = sb(s0, "rsum0_t", [P, ITEMS, 1])
        pT0 = sb(s0, "pT0", [P, 2, SEQ])
        oTok = sb(s0, "oTok", [P, QT, D])
        oH0 = sb(s0, "oH0", [P, KT, SEQ], F32R)
        oL0 = sb(s0, "oL0", [P, KT, SEQ], F32R)
        lg = sb(s0, "lg", [P, QT, NE])
        ex = sb(s0, "ex", [P, QT, NE])
        rest = sb(s0, "rest", [P, QT, NE])
        top8 = sb(s0, "top8", [P, QT, TOPK])
        rsm = sb(s0, "rsm", [P, 4, QT])
        wT = sb(s0, "wT", [NE, SEQ])
        lut = sb(s0, "lut", [P, LUT])
        idx = sb(s0, "idx", [P, MT * D], I32)
        wf = sb(s0, "wf", [P, MT * D])
        wft = sb(s0, "wft", [P, MT * D])
        hH2, hL2 = (w[:, 0:KT * SEQ].bitcast(F32R).rearrange("p (k t) -> p k t", k=KT) for w in (wf, wft))
        s0.close()

        s1 = ExitStack()
        wgH = sb(s1, "wgH", [P, 3 * KT, HG * HD1], F32R)
        wgL = sb(s1, "wgL", [P, 3 * KT, HG * HD1], F32R)
        woH = sb(s1, "woH", [P, HG, D], F32R)
        woL = sb(s1, "woL", [P, HG, D], F32R)
        wo = sb(s1, "wo", [P, HG, D])
        wg = sb(s1, "wg", [P, 3 * KT, HG * HD1])
        qk = sb(s1, "qk", [P, QT, 2, HG * HD1])
        qkst = sb(s1, "qkst", [P, QT * 2 * HG, 6])
        qT = sb(s1, "qT", [P, HG, SEQ])
        kT = sb(s1, "kT", [P, HG, SEQ])
        v1 = sb(s1, "v1", [P, QT, HG * HD1])
        pT1 = sb(s1, "pT1", [P, 2, QT * (QT + 1) // 2 * P])
        oH1 = sb(s1, "oH1", [P, HG, SEQ], F32R)
        oL1 = sb(s1, "oL1", [P, HG, SEQ], F32R)
        wguH = sb(s1, "wguH", [P, 2, KT, MT * P], F32R)
        wdH = sb(s1, "wdH", [P, MT, D], F32R)
        wdL = sb(s1, "wdL", [P, MT, D], F32R)
        wraw = sb(s1, "wraw", [P, max(INTER, MT * D // 2)])
        s1.close()

        s2 = ExitStack()
        sg = sb(s2, "sg", [P, 2, SEQ])
        hf = sb(s2, "hf", [P, 2, SEQ])
        hmH = sb(s2, "hmH", [P, MT, SEQ], F32R)
        hmL = sb(s2, "hmL", [P, MT, SEQ], F32R)
        sb(s2, "as_wo", [P, HG, D])
        wguL = sb(s2, "wguL", [P, 2, KT, MT * P], F32R)
        s2.close()

        def xb(b, t, n=1):
            return x[:, bass.ds(b * QT + t, n), :]

        def modb(l, b, c):
            return mod[l][:, bass.ds(b, 1), c, :]

        def mm3(pe, o, wH, wL, mH, mL, start, stop):
            pe.matmul(o, wL, mH, start=start, stop=False)
            pe.matmul(o, wH, mL, start=False, stop=False)
            return pe.matmul(o, wH, mH, start=False, stop=stop)

        class Norm:
            def __init__(self, name, layer, c, s):
                self.layer, self.c, self.s = layer, c, s
                self.h, self.tp, self.hi, self.lo = (sem(f"{name}_{w}") for w in ("h", "tp", "hi", "lo"))

            def dve(self, dve, ch, b, r):
                for part in range(NORM_PARTS):
                    self.dve_part(part, dve, ch, b, r)

            def dve_part(self, part, dve, ch, b, r, high=hH, low=hL):
                m, s = modb(self.layer, b, self.c), modb(self.layer, b, self.s)
                v, t, y = sm[:, 0, 0:QT], sm[:, 1, 0:QT], sm[:, 2, 0:QT]
                half = lambda i: slice(i * QT // 2, (i + 1) * QT // 2)
                if part < 2:
                    vector_carrier(dve)
                    for i in range(QT)[half(part)]:
                        last = dve.bn_stats(stats[:, i, :], xb(b, i))
                    ch.mark(last)
                elif part == 2:
                    ch.wait()
                    vector_carrier(dve)
                    for i in range(QT):
                        last = dve.bn_aggr(mv[:, i, :], stats[:, i, :])
                    ch.step(last)
                    ch.mark(dve.tensor_scalar(v, mv[:, :, 1], EPS, None, ALU.add))
                elif part == 3:
                    ch.wait()
                    rsqrt_seed(dve, ch, y, t, v)
                elif part < 4 + NEWTON:
                    rsqrt_newton(dve, ch, y, t, v)
                elif part < 6 + NEWTON:
                    ch.wait()
                    for i in range(QT)[half(part - 4 - NEWTON)]:
                        last = dve.tensor_scalar(hN[:, i, :], xb(b, i), mv[:, i, 0:1], sm[:, 2, i:i + 1],
                                                 ALU.subtract, ALU.mult)
                    ch.mark(last)
                elif part < 8 + NEWTON:
                    ch.wait()
                    h = hN[:, half(part - 6 - NEWTON), :]
                    ch.mark(dve.tensor_tensor(h, h, m.to_broadcast([P, QT // 2, D]), ALU.mult))
                elif part < 10 + NEWTON:
                    ch.wait()
                    h = hN[:, half(part - 8 - NEWTON), :]
                    ins = dve.tensor_tensor(h, h, s.to_broadcast([P, QT // 2, D]), ALU.add)
                    ins.then_inc(self.h, 1)
                else:
                    for k in range(KT):
                        dve.wait_ge(self.hi, r * KT + k + 1)
                        dve.tensor_tensor(low[:, k, :], bank[6 + k][:, :], f32(high[:, k, :]),
                                          ALU.subtract).then_inc(self.lo, 1)

            def act(self, act, r, free, high=hH):
                free()
                for k in range(KT):
                    act.wait_ge(self.tp, r * KT + k + 1)
                    act.activation(high[:, k, :], bank[6 + k][:, :], ACT.Copy).then_inc(self.hi, 1)

            def pe(self, pe, r):
                pe.wait_ge(self.h, (r + 1) * 2)
                for k in range(KT):
                    for t in range(QT):
                        last = pe.transpose(bank[6 + k][:, t * P:(t + 1) * P], hN[:, t, k * P:(k + 1) * P],
                                            identf[:, :])
                    last.then_inc(self.tp, 1)

            def wait_ready(self, pe, r):
                pe.wait_ge(self.lo, (r + 1) * KT)

        norm_a0 = Norm("norm_a0", 0, CA, SA)
        norm_f0 = Norm("norm_f0", 0, CB, SB)
        norm_a1 = Norm("norm_a1", 1, CA, SA)
        norm_f1 = Norm("norm_f1", 1, CB, SB)

        loaded_c, loaded_w0, loaded_x, loaded_idx, loaded_misc = map(
            sem, ("loaded_c", "loaded_w0", "loaded_x", "loaded_idx", "loaded_misc"))
        loaded_m0, loaded_m, loaded_x0, consts, q_hi, k_hi = map(
            sem, ("loaded_m0", "loaded_m", "loaded_x0", "consts", "q_hi", "k_hi"))
        silu_c, cb_ready, mod_pe, mod_raw, mod_done = map(
            sem, ("silu_c", "cb_ready", "mod_pe", "mod_raw", "mod_done"))
        w0_hi, w0_lo = sem("w0_hi"), sem("w0_lo")
        qkv_pe, q_scaled, q_split, q_stored, k_read, v_read = map(
            sem, ("qkv_pe", "q_scaled", "q_split", "q_stored", "k_read", "v_read"))
        dchain = [sem(f"dve_chain{i}") for i in range(6)]
        q_loaded = [sem(f"q_loaded{g}") for g in range(NG)]
        s0_pe, max0, exp0, t0_pe, ev0, pv0, oev0 = map(
            sem, ("scores0", "max0", "exp0", "turned0", "pT0_ready", "pv0", "o0_ready"))
        ot_pe, ot_hi, ot_lo, y0_pe, x0_add = map(sem, ("oT_pe", "oT_hi", "oT_lo", "y0_pe", "x0_added"))
        r_pe, r_nmax, r_exp, r_w, r_tp, r_wT, r_y = map(
            sem, ("route_pe", "route_max", "route_exp", "route_w", "route_tp", "route_wT", "route_y"))
        h1_stored = sem("h1_stored")
        gat, gat_dma = sem("gathered"), sem("gathered_dma")
        w1_loaded, w1_hi, w1_lo, h1_loaded, gqk_ready = map(
            sem, ("w1_loaded", "w1_hi", "w1_lo", "h1_loaded", "gqk_ready"))
        p1_pe, p1_act, p1_dve, qk_norm = map(
            sem, ("proj1", "proj1_copied", "proj1_stats", "qk_normed"))
        tr_pe, tr_act = sem("qkT_pe"), sem("qkT_ready")
        s1_pe, max1, exp1, nrm1, t1_pe, ev1, pv1, o1_hi, o1_lo, y1_pe, x1_add = map(
            sem, ("scores1", "max1", "exp1", "normed1", "turned1", "pT1_ready", "pv1", "o1_hi", "o1_lo",
                  "y1_pe", "x1_added"))
        rsum0, y2_gated = sem("rsum0"), sem("y2_gated")
        y1_gated, rsum1 = sem("y1_gated"), sem("rsum1")
        f_loaded, f_zero, f_hi, f_lo = map(sem, ("f_loaded", "f_zero", "f_hi", "f_lo"))
        gu_pe, f_silu, f_h, f_hhi, f_hlo, y2_pe, x2_add, stored = map(
            sem, ("gateup_pe", "silu", "f_h", "f_h_hi", "f_h_lo", "y2_pe", "x2_added", "stored"))

        carriers = [0]

        def vector_carrier(dve):
            dve.memset(pad[:, carriers[0]:carriers[0] + 1], 0.0)
            carriers[0] += 1

        def tensor_carrier(pe, o):
            pe.matmul(o, identb[:, :], identb[:, :], start=True, stop=True)

        block = top.enter_context(nc.Block())

        @block.sync
        def _(sp):
            sp.dma_start(cT[:, :, :, :], a["cT"]).then_inc(loaded_c, 16)
            wm = [a[f"wmod{l}"].rearrange("(k p) n -> p k n", p=P) for l in range(2)]
            sp.dma_start(wmod[:, 0, :, 0:2 * D], wm[0][:, :, 0:2 * D]).then_inc(loaded_m0, 16)
            sp.dma_start(x[:, 0:QT, :], x_v[:, 0:QT, :]).then_inc(loaded_x0, 16)
            for name, cols in (("wq0", WQ), ("wk0", WK), ("wv0", WV), ("wo0", WO), ("wr", WR)):
                sp.dma_start(w0[:, :, cols], a[name].rearrange("(k p) n -> p k n", p=P)).then_inc(loaded_w0, 16)
            sp.dma_start(x[:, QT:, :], x_v[:, QT:, :]).then_inc(loaded_x, 16)
            sp.dma_start(wmod[:, 0, :, 2 * D:], wm[0][:, :, 2 * D:]).then_inc(loaded_m, 16)
            sp.dma_start(wmod[:, 1, :, :], wm[1]).then_inc(loaded_m, 16)
            sp.dma_start(kmask[:, :], a["kmask"]).then_inc(loaded_misc, 16)
            sp.dma_start(gqk[:, 0:2], a["gqk"]).then_inc(gqk_ready, 16)
            sp.dma_start(ebias[:, :], a["ebias"]).then_inc(loaded_misc, 16)
            sp.dma_start(rbias[:, :], a["rbias"].to_broadcast([P, NE])).then_inc(loaded_misc, 16)
            with sp.Fori(0, NB) as b:
                for m in range(KT):
                    sp.wait_ge(q_split, (b * KT + m + 1) * 2)
                    for i, part in enumerate((qhi, qmi, qlo)):
                        sp.dma_start(q_parts[i, m * P:(m + 1) * P, bass.ds(b * SEQ, SEQ)],
                                     part[:, m, :]).then_inc(q_stored, 16)
            sp.wait_ge(k_read, NB)
            sp.wait_ge(q_stored, NB * KT * 3 * 16)
            def load_q(b, g):
                for s, part in enumerate(Q_SLOT):
                    sp.dma_start(qst[s * HD0:(s + 1) * HD0, g * HG * SEQ:(g + 1) * HG * SEQ].rearrange("d (h t) -> d h t", h=HG),
                                 q_parts[part].rearrange("(h d) t -> d h t", d=HD0)[:, g * HG:(g + 1) * HG, bass.ds(b * SEQ, SEQ)]
                                 ).then_inc(q_loaded[g], 16)

            for g in range(NG):
                load_q(0, g)
            with sp.Fori(1, NB) as b:
                for g in range(NG):
                    sp.wait_ge(s0_pe, (b - 1) * ITEMS0 + (g + 1) * ITEMS)
                    load_q(b, g)
            def load_w1(g):
                sp.dma_start(wg[:, :, :], a["wqkv"][g].rearrange("p (k n) -> p k n", k=3 * KT)).then_inc(w1_loaded, 16)
                sp.dma_start(wo[:, :, :], a["wo1"][g].rearrange("(h p) n -> p h n", p=P)).then_inc(w1_loaded, 16)

            def load_h1(b):
                sp.dma_start(f32(hH[:, :, :]).rearrange("p k t -> p (k t)"), h1_saved[b, :, 0:KT * SEQ]).then_inc(h1_loaded, 16)
                sp.dma_start(f32(hL[:, :, :]).rearrange("p k t -> p (k t)"), h1_saved[b, :, KT * SEQ:]).then_inc(h1_loaded, 16)

            sp.wait_ge(s0_pe, NB * ITEMS0)
            load_w1(0)
            sp.wait_ge(r_pe, NB)
            sp.wait_ge(h1_stored, (NB - 1) * 32)
            load_h1(0)
            sp.wait_ge(h1_stored, NB * 32)
            def load_later_h1(g):
                with sp.Fori(1, NB) as b:
                    sp.wait_ge(p1_pe, (g * NB + b) * 3 * QT)
                    load_h1(b)

            with sp.Fori(0, NG - 1) as g:
                load_later_h1(g)
                sp.wait_ge(w1_lo, (g + 1) * (3 * KT + HG))
                load_w1(g + 1)
                sp.wait_ge(p1_pe, (g + 1) * NB * 3 * QT)
                load_h1(0)
            load_later_h1(NG - 1)
            with sp.Fori(0, NB) as b:
                for t2 in range(2):
                    sp.wait_ge(x2_add, b * 2 + t2 + 1)
                    sp.dma_start(out_v[:, bass.ds(b * QT + 2 * t2, 2), :], xb(b, 2 * t2, 2)).then_inc(stored, 16)
            sp.wait_ge(stored, NB * 2 * 16)

        @block.gpsimd
        def _(pool):
            pool.memset(identf[:, :], 0.0).then_inc(consts, 1)
            pool.memset(ones[:, :], 0.0).then_inc(consts, 1)
            pool.wait_ge(consts, 2)
            pool.affine_select(out=identf[:, :], in_=identf[:, :], compare_op=ALU.not_equal, fill=1.0, base=0,
                               pattern=[[-1, P]], channel_multiplier=1).then_inc(consts, 1)
            pool.affine_select(out=maskb[:, :], in_=ones[:, :], compare_op=ALU.is_ge, fill=NEG, base=0,
                               pattern=[[-1, P]], channel_multiplier=1).then_inc(consts, 1)
            pool.wait_ge(consts, 4)
            pool.tensor_copy(identb[:, :], identf[:, :]).then_inc(consts, 1)
            pool.memset(v0[:, :, :], 1.0).then_inc(consts, 1)
            pool.memset(ones[:, :], 1.0).then_inc(consts, 1)
            n = [0]

            def link(ins):
                n[0] += 1
                ins.then_inc(gat, 1)
                pool.wait_ge(gat, n[0])

            pool.dma_start(lut[:, :], a["lut"].to_broadcast([P, LUT])).then_inc(loaded_idx, 16)
            jobs = [(a[f"idx_{w}"].rearrange("(k p) n -> p k n", p=P), P, 0, KT * INTER, n * KT * INTER)
                    for n, w in enumerate(("gate", "up"))]
            jobs += [(a["idx_down"][0:(MT - 1) * P, :].rearrange("(m p) n -> p m n", p=P), P, 0, (MT - 1) * D,
                      2 * KT * INTER),
                     (a["idx_down"][(MT - 1) * P:, :], LAST, (MT - 1) * D, D, 2 * KT * INTER + (MT - 1) * D)]
            link(pool.memset(wf[:, :], 0.0))
            for i, (src, rows, o, cols, at) in enumerate(jobs):
                part = idx[0:rows, o:o + cols]
                if len(src.shape) == 3:
                    part = part.rearrange("p (k n) -> p k n", k=src.shape[1])
                pool.dma_start(part, src).then_inc(loaded_idx, 16)
                pool.wait_ge(loaded_idx, (i + 2) * 16)
                if i:
                    pool.wait_ge(gat_dma, i * 16)
                if i == 3:
                    link(pool.memset(wf[:, o:o + cols], 0.0))
                part, acc, tmp = idx[0:rows, o:o + cols], wf[0:rows, o:o + cols], wft[0:rows, o:o + cols]
                for j in range(LUT):
                    link(pool.tensor_scalar(tmp if j else acc, part, float(j), lut[0:rows, j:j + 1],
                                            ALU.is_equal, ALU.mult))
                    if j:
                        link(pool.tensor_tensor(acc, acc, tmp, ALU.add))
                pool.dma_start(wffn_saved[:, at:at + cols], wf[:, o:o + cols]).then_inc(gat_dma, 16)

            pool.wait_ge(h1_stored, NB * 32)
            pool.wait_ge(gat_dma, 4 * 16)
            pool.memset(f32(wguH[:, :, :, INTER:]), 0.0).then_inc(f_zero, 1)
            pool.wait_ge(w1_lo, NG * (3 * KT + HG))
            pool.memset(f32(wguL[:, :, :, INTER:]), 0.0).then_inc(f_zero, 1)
            strips = [((w * KT + k) * INTER, wguH[:, w, k, 0:INTER], wguL[:, w, k, 0:INTER])
                      for w in range(2) for k in range(KT)]
            strips += [(2 * KT * INTER + j * (MT * D // 2), wdH[:, j * MT // 2:(j + 1) * MT // 2, :],
                        wdL[:, j * MT // 2:(j + 1) * MT // 2, :]) for j in range(2)]
            for i, (at, hi, lo) in enumerate(strips):
                cols = INTER if i < 2 * KT else MT * D // 2
                raw = wraw[:, 0:cols]
                if i >= 2 * KT:
                    raw = raw.rearrange("p (m n) -> p m n", n=D)
                if i:
                    pool.wait_ge(f_lo, i)
                pool.dma_start(wraw[:, 0:cols], wffn_saved[:, at:at + cols]).then_inc(f_loaded, 16)
                pool.wait_ge(f_loaded, (i + 1) * 16)
                pool.tensor_copy(hi, raw).then_inc(f_hi, 1)
                pool.wait_ge(f_hi, i + 1)
                pool.tensor_tensor(lo, raw, f32(hi), ALU.subtract).then_inc(f_lo, 1)

        @block.scalar
        def _(act):
            act.wait_ge(loaded_c, 16)
            act.activation(sc[:, :, :, :], cT[:, :, :, :], ACT.Silu).then_inc(silu_c, 1)

            def copy_mod(u, o, l, b, c):
                act.wait_ge(mod_pe, u + 1)
                for j in range(2):
                    last = act.activation(mod[l][:, b, 2 * c + j, :], o[:, j * D:(j + 1) * D], ACT.Copy,
                                          bias=1.0 if 2 * c + j in (CA, CB) else 0.0)
                last.then_inc(mod_done, 1)

            for b in range(NB):
                copy_mod(b, bank[4 + b % 2], 0, b, 0)
            act.wait_ge(loaded_w0, 5 * 16)
            act.activation(w0H[:, :, :], w0[:, :, :], ACT.Copy).then_inc(w0_hi, 1)

            def qkv0(b, following):
                for m in range(KT):
                    act.wait_ge(qkv_pe, b * (KT + 2) + m + 1)
                    act.wait_ge(q_split, b * KT * 2)
                    act.activation(q32[:, m, :], bank[m][:, :], ACT.Copy, scale=HD0 ** -0.5).then_inc(q_scaled, 1)
                    act.wait_ge(q_scaled, b * KT + m + 1)
                    act.wait_ge(q_stored, b * KT * 3 * 16)
                    act.activation(qhi[:, m, :], q32[:, m, :], ACT.Copy).then_inc(q_hi, 1)
                act.wait_ge(qkv_pe, b * (KT + 2) + KT + 1)
                act.wait_ge(k_read, b)
                act.activation(qst[:, 0:SEQ], bank[2][:, :], ACT.Copy).then_inc(k_hi, 1)
                act.wait_ge(qkv_pe, (b + 1) * (KT + 2))
                act.activation(v0[:, bass.ds(b * QT, QT), 0:HD0], bank[3][:, 0:QT * HD0].rearrange("p (t d) -> p t d", d=HD0),
                               ACT.Copy).then_inc(v_read, 1)
                if following is not None:
                    norm_a0.act(act, following, lambda: act.wait_ge(qkv_pe, following * (KT + 2)))
                for j, (l, c) in enumerate(LATER_MODS):
                    copy_mod(NB + b * len(LATER_MODS) + j, bank[4 + j % 2], l, b, c)

            norm_a0.act(act, 0, lambda: None)
            with act.Fori(0, NB - 1) as b:
                qkv0(b, b + 1)
            qkv0(NB - 1, None)

            def after0(n, b, last=False):
                if n in (3, 4):
                    k = n - 3
                    act.wait_ge(ot_pe, b * KT + k + 1)
                    act.wait_ge(y0_pe, b * 2)
                    act.activation(oH0[:, k, :], bank[6 + k][:, :], ACT.Copy).then_inc(ot_hi, 1)
                elif n == 25:
                    norm_f0.act(act, b, lambda: act.wait_ge(h1_stored, b * 32))
                elif n == 30:
                    act.wait_ge(r_nmax, b + 1)
                    for t in range(QT):
                        act.activation(ex[:, t, :], lg[:, t, :], ACT.Exp, bias=rsm[:, 0, t:t + 1],
                                       accum_out=rsm[:, 1, t:t + 1]).then_inc(r_exp, 1)
                elif n == 38:
                    act.wait_ge(r_tp, b + 1)
                    act.activation(wT[:, :], bank[7][0:NE, :], ACT.Copy).then_inc(r_wT, 1)
                elif n == 58:
                    if last:
                        norm_a1.act(act, b, lambda: act.wait_ge(gat_dma, 4 * 16), hH2)
                    else:
                        norm_a1.act(act, b, lambda: act.wait_ge(r_pe, b + 1))
                elif n == 61:
                    act.wait_ge(norm_a1.lo, (b + 1) * KT)
                    high, low = (hH2, hL2) if last else (hH, hL)
                    act.dma_start(h1_saved[b, :, 0:KT * SEQ], f32(high[:, :, :]).rearrange("p k t -> p (k t)")).then_inc(h1_stored, 16)
                    act.dma_start(h1_saved[b, :, KT * SEQ:], f32(low[:, :, :]).rearrange("p k t -> p (k t)")).then_inc(h1_stored, 16)

            def attend0(b, after):
                for s in range(ITEMS0 + LAG):
                    if s < ITEMS0:
                        i, n = s, (s % QT + 1) * P
                        act.wait_ge(max0, b * ITEMS0 + i + 1)
                        act.wait_ge(t0_pe, b * ITEMS0 + max(i - 3, 0))
                        act.activation(probs[:, i % 4, 0:n], bank[i % 3][:, 0:n], ACT.Exp,
                                       bias=negmax[:, i:i + 1]).then_inc(exp0, 1)
                    i = s - LAG
                    if i >= 0:
                        n = (i % QT + 1) * P
                        act.wait_ge(t0_pe, b * ITEMS0 + i + 1)
                        act.wait_ge(pv0, b * ITEMS0 + max(i - 1, 0))
                        act.activation(pT0[:, i % 2, 0:n], bank[3 + i % 2][:, 0:n], ACT.Copy).then_inc(ev0, 1)
                    if after is not None and s < ITEMS0:
                        after0(s, after)

            attend0(0, None)
            with act.Fori(1, NB) as b:
                attend0(b, b - 1)

            def split_w1(g):
                act.wait_ge(w1_loaded, (g + 1) * 32)
                act.wait_ge(p1_pe, g * NB * 3 * QT)
                for c in range(3 * KT):
                    act.activation(wgH[:, c, :], wg[:, c, :], ACT.Copy).then_inc(w1_hi, 1)
                act.wait_ge(y1_pe, g * NB * 2)
                for c in range(HG):
                    act.activation(woH[:, c, :], wo[:, c, :], ACT.Copy).then_inc(w1_hi, 1)

            act.wait_ge(q_stored, NB * KT * 3 * 16)
            for n in range(ITEMS0):
                after0(n, NB - 1, True)
                if n == 31:
                    split_w1(0)

            act.wait_ge(gqk_ready, 16)
            act.activation(gqk[:, 2:3], gqk[:, 0:1], ACT.Copy, scale=gqk[:, 1:2]).then_inc(gqk_ready, 1)
            act.wait_ge(gqk_ready, 17)
            act.activation(gqk[:, 2:3], gqk[:, 2:3], ACT.Copy, scale=HD1 ** -0.5).then_inc(gqk_ready, 1)
            act.wait_ge(gqk_ready, 18)

            def rounds1(g):
                with act.Fori(0, NB) as b:
                    it = g * NB + b
                    act.wait_ge(tr_pe, it * 2 * QT)
                    act.wait_ge(pv1, it * HG)
                    for u in range(3 * QT):
                        act.wait_ge(p1_pe, it * 3 * QT + u + 1)
                        dst = qk[:, u // 2, u % 2, :] if u < 2 * QT else v1[:, u - 2 * QT, :]
                        act.activation(dst, bank[u % 3][:, :], ACT.Copy).then_inc(p1_act, 1)
                    for u in range(2 * QT):
                        act.wait_ge(tr_pe, it * 2 * QT + u + 1)
                        t = u // 2
                        dst = (qT, kT)[u % 2][:, :, t * P:(t + 1) * P]
                        act.activation(dst, bank[u % 3][:, :].rearrange("p (h t) -> p h t", h=HG), ACT.Copy,
                                       scale=1.0 if u % 2 else gqk[:, 2:3]).then_inc(tr_act, 1)
                    for s in range(ITEMS + LAG1 + 2):
                        if s < ITEMS:
                            i = s
                            n = (ORDER[i % QT] + 1) * P
                            act.wait_ge(max1, it * ITEMS + i + 1)
                            act.wait_ge(t1_pe, it * ITEMS + max(i - 3, 0))
                            act.activation(probs[:, i % 4, 0:n], bank[SCORE_BANKS[i % 3]][:, 0:n], ACT.Exp,
                                           bias=negmax[:, i:i + 1], accum_out=sums[:, i:i + 1]).then_inc(exp1, 1)
                        i = s - LAG1
                        if 0 <= i < ITEMS:
                            h, t = i // QT, ORDER[i % QT]
                            act.wait_ge(t1_pe, it * ITEMS + i + 1)
                            act.wait_ge(pv1, it * HG + max(h - 1, 0))
                            at = t * (t + 1) // 2 * P
                            act.activation(pT1[:, h % 2, at:at + (t + 1) * P], bank[5 + i % 2][:, 0:(t + 1) * P],
                                           ACT.Copy).then_inc(ev1, 1)
                        i = s - LAG1 - 2
                        if i >= 0 and i % QT == QT - 1:
                            h = i // QT
                            act.wait_ge(pv1, it * HG + h + 1)
                            act.wait_ge(y1_pe, it * 2)
                            act.activation(oH1[:, h, :], bank[7][:, :], ACT.Copy).then_inc(o1_hi, 1)

            with act.Fori(0, NG - 1) as g:
                rounds1(g)
                split_w1(g + 1)
            rounds1(NG - 1)

            def swiglu(b, following):
                for m in range(MT):
                    act.wait_ge(gu_pe, b * MT + m + 1)
                    act.wait_ge(f_h, b * MT + max(m - 1, 0))
                    act.activation(sg[:, m % 2, :], bank[2 * (m % 2)][:, :], ACT.Silu).then_inc(f_silu, 1)
                    act.wait_ge(f_h, b * MT + m + 1)
                    act.wait_ge(y2_pe, b * 2)
                    act.activation(hmH[:, m, :], hf[:, m % 2, :], ACT.Copy).then_inc(f_hhi, 1)
                if following is not None:
                    norm_f1.act(act, following, lambda: act.wait_ge(gu_pe, following * MT))

            norm_f1.act(act, 0, lambda: act.wait_ge(p1_pe, NG * NB * 3 * QT))
            act.wait_ge(y1_pe, NG * NB * 2)
            with act.Fori(0, NB - 1) as b:
                swiglu(b, b + 1)
            swiglu(NB - 1, None)

        @block.vector
        def _(dve):
            chains = [Chain(dve, s) for s in dchain]
            dve.wait_ge(consts, 7)
            dve.wait_ge(silu_c, 1)
            for k in range(KT):
                for b in range(NB):
                    last = dve.tensor_scalar(cB0[:, k, b, :], ones[:, :], sc[:, 0, k, b:b + 1], None, ALU.mult)
            last.then_inc(cb_ready, 1)

            norm_ch, ch = chains[1], chains[0]

            def norm_parts(b):
                norm_ch.begin(b * NORM_STEPS)
                for part in range(NORM_PARTS - 1):
                    norm_a0.dve_part(part, dve, norm_ch, b, b)
                assert norm_ch.n == NORM_STEPS, norm_ch.n

            def qkv0(b, following):
                dve.wait_ge(mod_pe, NB + b * len(LATER_MODS))
                dve.tensor_copy(cB[:, :, :, :, :], sc[:, :, :, bass.ds(b, 1)].rearrange(
                    "p l k (b one) -> p l k b one", one=1).to_broadcast([P, 2, KT, 1, P])).then_inc(cb_ready, 1)
                norm_a0.dve_part(NORM_PARTS - 1, dve, norm_ch, b, b)
                if following is not None:
                    norm_parts(following)
                ch.begin(b * QK0_STEPS)
                for m in range(KT):
                    dve.wait_ge(q_hi, b * KT + m + 1)
                    ch.step(dve.tensor_tensor(q32[:, m, :], q32[:, m, :], qhi[:, m, :], ALU.subtract))
                    dve.wait_ge(q_stored, b * KT * 3 * 16)
                    dve.tensor_copy(qmi[:, m, :], q32[:, m, :]).then_inc(q_split, 1)
                    dve.wait_ge(q_split, (b * KT + m) * 2 + 1)
                    dve.tensor_tensor(qlo[:, m, :], q32[:, m, :], qmi[:, m, :], ALU.subtract).then_inc(q_split, 1)
                dve.wait_ge(k_hi, b + 1)
                kb, lo = bank[2][:, :], probs[:, 2, :]
                hb, mb = qst[:, 0:SEQ], qst[:, SEQ:2 * SEQ]
                ch.step(dve.tensor_tensor(lo, kb, hb, ALU.subtract))
                ch.step(dve.tensor_copy(mb, lo))
                ch.step(dve.tensor_tensor(lo, lo, mb, ALU.subtract))
                ch.step(dve.tensor_scalar(lo, lo, kmask[:, 2:3], None, ALU.mult))
                ch.step(dve.scalar_tensor_tensor(out=lo, in0=mb, scalar=kmask[:, 1:2], in1=lo, op0=ALU.mult, op1=ALU.add))
                dve.scalar_tensor_tensor(out=kst[:, bass.ds(b * SEQ, SEQ)], in0=hb, scalar=kmask[:, 0:1], in1=lo,
                                         op0=ALU.mult, op1=ALU.add).then_inc(k_read, 1)
                assert ch.n == QK0_STEPS, ch.n

            dve.wait_ge(loaded_x0, 16)
            dve.wait_ge(mod_done, NB)
            norm_parts(0)
            dve.wait_ge(w0_hi, 1)
            dve.tensor_tensor(w0L[:, :, :], w0[:, :, :], f32(w0H[:, :, :]), ALU.subtract).then_inc(w0_lo, 1)
            dve.wait_ge(loaded_x, 16)
            dve.wait_ge(loaded_misc, 48)
            with dve.Fori(0, NB - 1) as b:
                qkv0(b, b + 1)
            qkv0(NB - 1, None)
            dve.wait_ge(mod_done, NB + NB * len(LATER_MODS))

            ch = chains[2]

            def after0(n, b, last=False):
                if n in (0, 2):
                    if n == 0:
                        ch.begin(b * NB0_STEPS)
                    g = mod[n // 2][:, bass.ds(b, 1), GA:GB + 1:GB - GA, :]
                    sign, mag = (w.rearrange("p (one c) d -> p one c d", one=1) for w in (sgn, ytmp[:, :, :]))
                    ch.step(dve.tensor_scalar(sign, g, 0.0, 2.0, ALU.is_ge, ALU.mult))
                    ch.step(dve.scalar_tensor_tensor(out=mag, in0=g, scalar=-1.0, in1=g, op0=ALU.mult, op1=ALU.max))
                    ch.step(dve.tensor_scalar(sign, sign, -1.0, None, ALU.add))
                    ch.step(dve.scalar_tensor_tensor(out=g, in0=mag, scalar=0.25, in1=sign, op0=ALU.max, op1=ALU.mult))
                elif n in (4, 5):
                    k = n - 4
                    dve.wait_ge(ot_hi, b * KT + k + 1)
                    dve.tensor_tensor(oL0[:, k, :], bank[6 + k][:, :], f32(oH0[:, k, :]), ALU.subtract).then_inc(ot_lo, 1)
                elif n in (9, 10):
                    t2 = n - 9
                    dve.wait_ge(y0_pe, b * 2 + t2 + 1)
                    ch.step(dve.tensor_tensor(ytmp[:, :, :], bank[6 + t2][:, :].rearrange("p (t d) -> p t d", d=D),
                                              modb(0, b, GA).to_broadcast([P, 2, D]), ALU.mult))
                    ch.step(dve.tensor_tensor(xb(b, 2 * t2, 2), xb(b, 2 * t2, 2), ytmp[:, :, :], ALU.add))
                elif 11 <= n < 10 + NORM_PARTS:
                    norm_f0.dve_part(n - 11, dve, ch, b, b)
                elif n == 26:
                    norm_f0.dve_part(NORM_PARTS - 1, dve, ch, b, b)
                elif n == 29:
                    dve.wait_ge(r_pe, b + 1)
                    ch.step(dve.tensor_tensor(lg[:, :, :], bank[6][:, 0:QT * NE].rearrange("p (t e) -> p t e", e=NE),
                                              rbias[:, :].rearrange("p (one e) -> p one e", one=1).to_broadcast([P, QT, NE]), ALU.add))
                    dve.tensor_reduce(rsm[:, 0, :], lg[:, :, :], AX.X, ALU.max, negate=True).then_inc(r_nmax, 1)
                elif n == 32:
                    dve.wait_ge(r_exp, (b + 1) * QT)
                    vector_carrier(dve)
                    for t in range(QT):
                        last = dve.max(top8[:, t, :], ex[:, t, :])
                    ch.step(last)
                elif n == 33:
                    vector_carrier(dve)
                    for t in range(QT):
                        last = dve.match_replace(rest[:, t, :], top8[:, t, :], ex[:, t, :], 0.0)
                    ch.step(last)
                elif n == 34:
                    ch.step(dve.tensor_tensor(ex[:, :, :], ex[:, :, :], rest[:, :, :], ALU.subtract))
                    ch.step(dve.reciprocal(rsm[:, 2, :], rsm[:, 1, :]))
                elif n == 35:
                    ch.step(dve.tensor_reduce(rsm[:, 3, :], ex[:, :, :], AX.X, ALU.add))
                    ch.step(dve.tensor_tensor(rsm[:, 3, :], rsm[:, 3, :], rsm[:, 2, :], ALU.mult))
                    dve.tensor_tensor(ex[:, :, :], ex[:, :, :], rsm[:, 2, :].rearrange("p (t one) -> p t one", one=1).to_broadcast([P, QT, NE]),
                                      ALU.mult).then_inc(r_w, 1)
                elif n == 41:
                    dve.wait_ge(r_y, b + 1)
                    for t in range(QT):
                        y = bank[6 + t // 2][:, (t % 2) * D:(t % 2 + 1) * D]
                        last = dve.scalar_tensor_tensor(out=hN[:, t, :], in0=hN[:, t, :], scalar=rsm[:, 3, t:t + 1], in1=y,
                                                        op0=ALU.mult, op1=ALU.add)
                    ch.step(last)
                elif n == 42:
                    ch.step(dve.tensor_tensor(hN[:, :, :], hN[:, :, :], modb(0, b, GB).to_broadcast([P, QT, D]), ALU.mult))
                elif n == 43:
                    ch.step(dve.tensor_tensor(xb(b, 0, QT), xb(b, 0, QT), hN[:, :, :], ALU.add))
                elif 44 <= n < 43 + NORM_PARTS:
                    norm_a1.dve_part(n - 44, dve, ch, b, b)
                elif n == 59:
                    norm_a1.dve_part(NORM_PARTS - 1, dve, ch, b, b, *((hH2, hL2) if last else ()))
                    assert ch.n == NB0_STEPS, ch.n

            def attend0(b, after):
                for s in range(ITEMS0 + LAG + 2):
                    if s < ITEMS0:
                        i, n = s, (s % QT + 1) * P
                        dve.wait_ge(s0_pe, b * ITEMS0 + i + 1)
                        dve.tensor_reduce(negmax[:, i:i + 1], bank[i % 3][:, 0:n], AX.X, ALU.max,
                                          negate=True).then_inc(max0, 1)
                    i = s - LAG - 1
                    if i >= 0 and i % ITEMS == ITEMS - 1:
                        g = i // ITEMS
                        dve.wait_ge(pv0, b * ITEMS0 + i + 1)
                        pv = bank[5][:, :].rearrange("p (i d) -> p i d", d=2 * HD0)
                        dve.reciprocal(rsum0_t[:, :, :], pv[:, :, HD0:HD0 + 1]).then_inc(rsum0, 1)
                        dve.wait_ge(rsum0, b * NG + g + 1)
                        if g == 0:
                            dve.wait_ge(ot_pe, b * KT)
                        dve.tensor_tensor(
                            oTok[:, :, g * HG * HD0:(g + 1) * HG * HD0].rearrange("p t (h d) -> p h t d", d=HD0),
                            pv[:, :, 0:HD0].rearrange("p (h t) d -> p h t d", h=HG),
                            rsum0_t[:, :, :].rearrange("p (h t) d -> p h t d", h=HG).to_broadcast([P, HG, QT, HD0]),
                            ALU.mult).then_inc(oev0, 1)
                    if after is not None and s < ITEMS0:
                        after0(s, after)

            attend0(0, None)
            with dve.Fori(1, NB) as b:
                attend0(b, b - 1)

            def split_w1(g, which):
                for c in range(3 * KT + HG)[which]:
                    dve.wait_ge(w1_hi, g * (3 * KT + HG) + c + 1)
                    whole, hi, lo = (w[:, c, :] for w in (wg, wgH, wgL)) if c < 3 * KT else (
                        w[:, c - 3 * KT, :] for w in (wo, woH, woL))
                    dve.tensor_tensor(lo, whole, f32(hi), ALU.subtract).then_inc(w1_lo, 1)

            for n in range(ITEMS0):
                after0(n, NB - 1, True)
                if n == 36:
                    split_w1(0, slice(0, 3 * KT))
                if n == 57:
                    split_w1(0, slice(3 * KT, 3 * KT + HG))

            ch = chains[3]

            def add_y1(it, b):
                for t2 in range(2):
                    dve.wait_ge(y1_pe, it * 2 + t2 + 1)
                    dve.tensor_tensor(ytmp[:, :, :], bank[5 + t2][:, :].rearrange("p (t d) -> p t d", d=D),
                                      modb(1, b, GA).to_broadcast([P, 2, D]), ALU.mult).then_inc(y1_gated, 1)
                    dve.wait_ge(y1_gated, it * 2 + t2 + 1)
                    dve.tensor_tensor(xb(b, 2 * t2, 2), xb(b, 2 * t2, 2), ytmp[:, :, :], ALU.add).then_inc(x1_add, 1)
                    dve.wait_ge(x1_add, it * 2 + t2 + 1)

            def round1(it, before):
                ch.begin(it * N1_STEPS)
                for u in range(2 * QT):
                    dve.wait_ge(p1_act, it * 3 * QT + u + 1)
                    vector_carrier(dve)
                    for h in range(HG):
                        last = dve.bn_stats(qkst[:, u * HG + h, :], qk[:, u // 2, u % 2, h * HD1:(h + 1) * HD1])
                    last.then_inc(p1_dve, 1)
                dve.wait_ge(p1_dve, (it + 1) * 2 * QT)
                v, w = sm[:, 0, :], sm[:, 2, :]
                me, mo = qkst[:, :, 1], qkst[:, :, 4]
                ch.step(dve.tensor_tensor(v, me, me, ALU.mult))
                ch.step(dve.tensor_tensor(w, mo, mo, ALU.mult))
                ch.step(dve.tensor_tensor(v, v, w, ALU.add))
                ch.step(dve.tensor_tensor(w, qkst[:, :, 2], qkst[:, :, 5], ALU.add))
                ch.step(dve.scalar_tensor_tensor(out=v, in0=w, scalar=2.0 / HD1, in1=v, op0=ALU.mult, op1=ALU.add))
                ch.step(dve.tensor_scalar(v, v, 0.5, EPS, ALU.mult, ALU.add))
                rsqrt_seed(dve, ch, w, sm[:, 1, :], v)
                for _ in range(NEWTON):
                    rsqrt_newton(dve, ch, w, sm[:, 1, :], v)
                ch.wait()
                for u in range(2 * QT):
                    rows = qk[:, u // 2, u % 2, :].rearrange("p (h d) -> p h d", d=HD1)
                    r = sm[:, 2, u * HG:(u + 1) * HG].rearrange("p (h one) -> p h one", one=1)
                    dve.tensor_tensor(rows, rows, r.to_broadcast([P, HG, HD1]), ALU.mult).then_inc(qk_norm, 1)
                if before is not None:
                    add_y1(it - 1, before)
                for s in range(ITEMS + LAG1 + 3):
                    if s < ITEMS:
                        i, n = s, (ORDER[s % QT] + 1) * P
                        dve.wait_ge(s1_pe, it * ITEMS + i + 1)
                        dve.tensor_reduce(negmax[:, i:i + 1], bank[SCORE_BANKS[i % 3]][:, 0:n], AX.X, ALU.max,
                                          negate=True).then_inc(max1, 1)
                    i = s - 1
                    if 0 <= i < ITEMS:
                        dve.wait_ge(exp1, it * ITEMS + i + 1)
                        dve.reciprocal(rsum[:, i:i + 1], sums[:, i:i + 1]).then_inc(rsum1, 1)
                    i = s - 2
                    if 0 <= i < ITEMS:
                        n = (ORDER[i % QT] + 1) * P
                        dve.wait_ge(rsum1, it * ITEMS + i + 1)
                        dve.tensor_scalar(probs[:, i % 4, 0:n], probs[:, i % 4, 0:n], rsum[:, i:i + 1], None,
                                          ALU.mult).then_inc(nrm1, 1)
                    i = s - LAG1 - 3
                    if i >= 0 and i % QT == QT - 1:
                        h = i // QT
                        dve.wait_ge(o1_hi, it * HG + h + 1)
                        dve.tensor_tensor(oL1[:, h, :], bank[7][:, :], f32(oH1[:, h, :]),
                                          ALU.subtract).then_inc(o1_lo, 1)
                assert ch.n == N1_STEPS, ch.n

            def rounds1(g):
                round1(g * NB, None)
                with dve.Fori(1, NB) as b:
                    round1(g * NB + b, b - 1)

            with dve.Fori(0, NG - 1) as g:
                rounds1(g)
                split_w1(g + 1, slice(0, 3 * KT))
                add_y1(g * NB + NB - 1, NB - 1)
                split_w1(g + 1, slice(3 * KT, 3 * KT + HG))
            rounds1(NG - 1)
            add_y1(NG * NB - 1, NB - 1)

            ch = chains[4]

            def swiglu(b, following):
                for m in range(MT):
                    dve.wait_ge(f_silu, b * MT + m + 1)
                    dve.wait_ge(f_hlo, b * MT + max(m - 1, 0))
                    dve.tensor_tensor(hf[:, m % 2, :], bank[2 * (m % 2) + 1][:, :], sg[:, m % 2, :], ALU.mult).then_inc(f_h, 1)
                    if following is not None:
                        if m == 0:
                            ch.begin(following * NORM_STEPS)
                        for part in range(NORM_PARTS - 1)[m * 3:(m + 1) * 3]:
                            norm_f1.dve_part(part, dve, ch, following, following)
                    dve.wait_ge(f_hhi, b * MT + m + 1)
                    dve.tensor_tensor(hmL[:, m, :], hf[:, m % 2, :], f32(hmH[:, m, :]), ALU.subtract).then_inc(f_hlo, 1)
                if following is not None:
                    norm_f1.dve_part(NORM_PARTS - 1, dve, ch, following, following)
                for t2 in range(2):
                    dve.wait_ge(y2_pe, b * 2 + t2 + 1)
                    dve.tensor_tensor(ytmp[:, :, :], bank[4 + t2][:, :].rearrange("p (t d) -> p t d", d=D),
                                      modb(1, b, GB).to_broadcast([P, 2, D]), ALU.mult).then_inc(y2_gated, 1)
                    dve.wait_ge(y2_gated, b * 2 + t2 + 1)
                    dve.tensor_tensor(xb(b, 2 * t2, 2), xb(b, 2 * t2, 2), ytmp[:, :, :], ALU.add).then_inc(x2_add, 1)
                    dve.wait_ge(x2_add, b * 2 + t2 + 1)

            ch.begin(0)
            norm_f1.dve(dve, ch, 0, 0)
            assert ch.n == NORM_STEPS, ch.n
            with dve.Fori(0, NB - 1) as b:
                swiglu(b, b + 1)
            swiglu(NB - 1, None)

        @block.tensor
        def _(pe):
            def modulation(o, c_rows, l, c):
                for k in range(KT):
                    last = pe.matmul(o, c_rows[k], wmod[:, l, k, c * 2 * D:(c + 1) * 2 * D],
                                     start=(k == 0), stop=(k == KT - 1))
                last.then_inc(mod_pe, 1)

            pe.wait_ge(cb_ready, 1)
            pe.wait_ge(loaded_m0, 16)
            for b in range(NB):
                if b >= 2:
                    pe.wait_ge(mod_done, b - 1)
                modulation(bank[4 + b % 2][:, :], [cB0[:, k, b, :] for k in range(KT)], 0, 0)
            norm_a0.pe(pe, 0)
            pe.wait_ge(w0_lo, 1)
            pe.wait_ge(loaded_m, 32)

            def qkv0(b, following):
                norm_a0.wait_ready(pe, b)
                for m in range(KT + 1):
                    if m < KT:
                        pe.wait_ge(q_scaled, b * KT)
                    else:
                        pe.wait_ge(k_read, b)
                    cols = slice(m * P, (m + 1) * P)
                    for k in range(KT):
                        last = mm3(pe, bank[m][:, :], w0H[:, k, cols], w0L[:, k, cols], hH[:, k, :], hL[:, k, :],
                                   k == 0, k == KT - 1)
                    last.then_inc(qkv_pe, 1)
                pe.wait_ge(v_read, b)
                for t in range(QT):
                    rows = slice(t * P, (t + 1) * P)
                    for k in range(KT):
                        last = mm3(pe, bank[3][:, t * HD0:(t + 1) * HD0], hH[:, k, rows], hL[:, k, rows],
                                   w0H[:, k, WV], w0L[:, k, WV], k == 0, k == KT - 1)
                last.then_inc(qkv_pe, 1)
                if following is not None:
                    norm_a0.pe(pe, following)
                pe.wait_ge(cb_ready, b + 2)
                for j, (l, c) in enumerate(LATER_MODS):
                    pe.wait_ge(mod_done, NB + b * len(LATER_MODS) + max(j - 1, 0))
                    modulation(bank[4 + j % 2][:, :], [cB[:, l, k, 0, :] for k in range(KT)], l, c)

            with pe.Fori(0, NB - 1) as b:
                qkv0(b, b + 1)
            qkv0(NB - 1, None)
            pe.wait_ge(mod_done, NB + NB * len(LATER_MODS))
            pe.wait_ge(k_read, NB)
            pe.wait_ge(v_read, NB)

            def after0(n, b):
                if n == 1:
                    pe.wait_ge(oev0, (b + 1) * NG)
                    for k in range(KT):
                        for t in range(QT):
                            last = pe.transpose(bank[6 + k][:, t * P:(t + 1) * P], oTok[:, t, k * P:(k + 1) * P], identf[:, :])
                        last.then_inc(ot_pe, 1)
                elif n == 7:
                    pe.wait_ge(ot_lo, (b + 1) * KT)
                    for t in range(QT):
                        rows = slice(t * P, (t + 1) * P)
                        for k in range(KT):
                            last = mm3(pe, bank[6 + t // 2][:, (t % 2) * D:(t % 2 + 1) * D], oH0[:, k, rows], oL0[:, k, rows],
                                       w0H[:, k, WO], w0L[:, k, WO], k == 0, k == KT - 1)
                        if t % 2:
                            last.then_inc(y0_pe, 1)
                elif n == 24:
                    norm_f0.pe(pe, b)
                elif n == 27:
                    norm_f0.wait_ready(pe, b)
                    for t in range(QT):
                        rows = slice(t * P, (t + 1) * P)
                        for k in range(KT):
                            last = mm3(pe, bank[6][:, t * NE:(t + 1) * NE], hH[:, k, rows], hL[:, k, rows],
                                       w0H[:, k, WR], w0L[:, k, WR], k == 0, k == KT - 1)
                    last.then_inc(r_pe, 1)
                elif n == 37:
                    pe.wait_ge(r_w, b + 1)
                    tensor_carrier(pe, bank[7][:, 0:P])
                    for t in range(QT):
                        last = pe.transpose(bank[7][0:NE, t * P:(t + 1) * P], ex[:, t, :], identf[:, :])
                    last.then_inc(r_tp, 1)
                elif n == 39:
                    pe.wait_ge(r_wT, b + 1)
                    for t in range(QT):
                        last = pe.matmul(bank[6 + t // 2][:, (t % 2) * D:(t % 2 + 1) * D], wT[:, t * P:(t + 1) * P], ebias[:, :],
                                         start=True, stop=True)
                    last.then_inc(r_y, 1)
                elif n == 57:
                    norm_a1.pe(pe, b)

            def attend0(b, after):
                for s in range(ITEMS0 + LAG + 1):
                    if s < ITEMS0:
                        i, h, t = s, s // QT, s % QT
                        n = (t + 1) * P
                        if i % ITEMS == 0:
                            pe.wait_ge(q_loaded[i // ITEMS], (b + 1) * SLOTS * 16)
                        pe.wait_ge(exp0, b * ITEMS0 + max(i - 2, 0))
                        pe.matmul(bank[i % 3][:, 0:n], qst[:, h * SEQ + t * P:h * SEQ + n],
                                  kst[:, bass.ds(b * SEQ, n)], start=True, stop=False)
                        pe.matmul(bank[i % 3][:, t * P:n], identb[:, :], maskb[:, :], start=False,
                                  stop=True).then_inc(s0_pe, 1)
                    i = s - LAG
                    if 0 <= i < ITEMS0:
                        t = i % QT
                        pe.wait_ge(exp0, b * ITEMS0 + i + 1)
                        pe.wait_ge(ev0, b * ITEMS0 + max(i - 1, 0))
                        for k in range(t + 1):
                            last = pe.transpose(bank[3 + i % 2][:, k * P:(k + 1) * P],
                                                probs[:, i % 4, k * P:(k + 1) * P], identf[:, :])
                        last.then_inc(t0_pe, 1)
                    i = s - LAG - 1
                    if i >= 0:
                        t = i % QT
                        pe.wait_ge(ev0, b * ITEMS0 + i + 1)
                        if i % ITEMS == 0:
                            pe.wait_ge(oev0, b * NG + i // ITEMS)
                        c = i % ITEMS * 2 * HD0
                        for k in range(t + 1):
                            last = pe.matmul(bank[5][:, c:c + 2 * HD0], pT0[:, i % 2, k * P:(k + 1) * P],
                                             v0[:, bass.ds(b * QT + k, 1), :], start=(k == 0), stop=(k == t))
                        last.then_inc(pv0, 1)
                    if after is not None and s < ITEMS0:
                        after0(s, after)

            attend0(0, None)
            with pe.Fori(1, NB) as b:
                attend0(b, b - 1)
            for n in range(ITEMS0):
                after0(n, NB - 1)

            def out_proj1(it):
                pe.wait_ge(o1_lo, (it + 1) * HG)
                for t in range(QT):
                    rows = slice(t * P, (t + 1) * P)
                    for h in range(HG):
                        last = mm3(pe, bank[5 + t // 2][:, (t % 2) * D:(t % 2 + 1) * D], oH1[:, h, rows], oL1[:, h, rows],
                                   woH[:, h, :], woL[:, h, :], h == 0, h == HG - 1)
                    if t % 2:
                        last.then_inc(y1_pe, 1)

            def round1(g, it, first):
                pe.wait_ge(w1_lo, g * (3 * KT + HG) + (3 * KT if first else 3 * KT + HG))
                pe.wait_ge(h1_loaded, (it + 1) * 32)
                pe.wait_ge(exp1, it * ITEMS)
                for u in range(3 * QT):
                    t, c = (u // 2, u % 2) if u < 2 * QT else (u - 2 * QT, 2)
                    if u >= 3:
                        pe.wait_ge(p1_act, it * 3 * QT + u - 2)
                    else:
                        pe.wait_ge(tr_act, it * 2 * QT)
                    rows = slice(t * P, (t + 1) * P)
                    for k in range(KT):
                        w = c * KT + k
                        last = mm3(pe, bank[u % 3][:, :], hH[:, k, rows], hL[:, k, rows], wgH[:, w, :], wgL[:, w, :],
                                   k == 0, k == KT - 1)
                    last.then_inc(p1_pe, 1)
                if not first:
                    out_proj1(it - 1)
                pe.wait_ge(p1_act, (it + 1) * 3 * QT)
                for u in range(2 * QT):
                    pe.wait_ge(qk_norm, it * 2 * QT + u + 1)
                    if u >= 3:
                        pe.wait_ge(tr_act, it * 2 * QT + u - 2)
                    for h in range(HG):
                        last = pe.transpose(bank[u % 3][:, h * P:(h + 1) * P],
                                            qk[:, u // 2, u % 2, h * HD1:(h + 1) * HD1], identf[:, :])
                    last.then_inc(tr_pe, 1)
                for s in range(ITEMS + LAG1 + 1):
                    if s < ITEMS:
                        i, h, t = s, s // QT, ORDER[s % QT]
                        n = (t + 1) * P
                        if i < QT:
                            pe.wait_ge(tr_act, it * 2 * QT + 2 * (t + 1))
                        pe.wait_ge(exp1, it * ITEMS + max(i - 2, 0))
                        pe.matmul(bank[SCORE_BANKS[i % 3]][:, 0:n], qT[:, h, t * P:n], kT[:, h, 0:n], start=True, stop=False)
                        pe.matmul(bank[SCORE_BANKS[i % 3]][:, t * P:n], identb[:, :], maskb[:, :], start=False,
                                  stop=True).then_inc(s1_pe, 1)
                    i = s - LAG1
                    if 0 <= i < ITEMS:
                        t = ORDER[i % QT]
                        if i == 0:
                            pe.wait_ge(x1_add, it * 2)
                        pe.wait_ge(nrm1, it * ITEMS + i + 1)
                        pe.wait_ge(ev1, it * ITEMS + max(i - 1, 0))
                        for k in range(t + 1):
                            last = pe.transpose(bank[5 + i % 2][:, k * P:(k + 1) * P],
                                                probs[:, i % 4, k * P:(k + 1) * P], identf[:, :])
                        last.then_inc(t1_pe, 1)
                    i = s - LAG1 - 1
                    if 0 <= i and i % QT == QT - 1:
                        h = i // QT
                        pe.wait_ge(ev1, it * ITEMS + i + 1)
                        pe.wait_ge(o1_lo, it * HG + h)
                        for t in range(QT):
                            for k in range(t + 1):
                                at = (t * (t + 1) // 2 + k) * P
                                last = pe.matmul(bank[7][:, t * P:(t + 1) * P], v1[:, k, h * HD1:(h + 1) * HD1],
                                                 pT1[:, h % 2, at:at + P], start=(k == 0), stop=(k == t))
                        last.then_inc(pv1, 1)

            with pe.Fori(0, NG) as g:
                round1(g, g * NB, True)
                with pe.Fori(1, NB) as b:
                    round1(g, g * NB + b, False)
                out_proj1(g * NB + NB - 1)

            def swiglu(b, following):
                norm_f1.wait_ready(pe, b)
                for m in range(MT):
                    pe.wait_ge(f_h, b * MT + max(m - 1, 0))
                    for w in range(2):
                        for k in range(KT):
                            last = mm3(pe, bank[2 * (m % 2) + w][:, :], wguH[:, w, k, m * P:(m + 1) * P],
                                       wguL[:, w, k, m * P:(m + 1) * P], hH[:, k, :], hL[:, k, :], k == 0, k == KT - 1)
                    last.then_inc(gu_pe, 1)
                if following is not None:
                    norm_f1.pe(pe, following)
                pe.wait_ge(f_hlo, (b + 1) * MT)
                pe.wait_ge(x2_add, b * 2)
                for t in range(QT):
                    rows = slice(t * P, (t + 1) * P)
                    for m in range(MT):
                        last = mm3(pe, bank[4 + t // 2][:, (t % 2) * D:(t % 2 + 1) * D], hmH[:, m, rows], hmL[:, m, rows],
                                   wdH[:, m, :], wdL[:, m, :], m == 0, m == MT - 1)
                    if t % 2:
                        last.then_inc(y2_pe, 1)

            pe.wait_ge(f_zero, 2)
            pe.wait_ge(f_lo, 2 * KT + 2)
            norm_f1.pe(pe, 0)
            with pe.Fori(0, NB - 1) as b:
                swiglu(b, b + 1)
            swiglu(NB - 1, None)


RSQRT_STEPS = 2 + 3 * NEWTON
NORM_STEPS = 2 + 2 + RSQRT_STEPS + 2 + 2
QK0_STEPS = KT + 5
NB0_STEPS = 2 * 4 + 4 + NORM_STEPS + 1 + 2 + 4 + 3 + NORM_STEPS
N1_STEPS = 5 + 1 + RSQRT_STEPS


def kernel(**inputs):
    import numpy as np
    import concourse.bacc as bacc
    from concourse.bass_utils import run_bass_kernel_spmd

    i = {k: np.asarray(v) for k, v in inputs.items()}
    kmask = np.zeros((P, 3), np.float32)
    for s, part in enumerate(K_SLOT):
        kmask[s * HD0:(s + 1) * HD0, part] = 1
    wk, wv = i["L0_attn_Wkv"][:HD0], i["L0_attn_Wkv"][HD0:]
    wqkv = np.stack([i[f"L1_attn_W{c}"].T for c in "qkv"]).reshape(3, KT, P, NG, HG * HD1)
    arrays = {
        "x": i["L0_attn_x"],
        "cT": np.stack([i[f"L{l}_c"].T for l in range(2)]).reshape(2, KT, P, NB).transpose(2, 0, 1, 3),
        "wmod0": i["L0_wmod"],
        "wmod1": i["L1_wmod"],
        "wq0": i["L0_attn_Wq"].T,
        "wk0": np.tile(wk.T, (1, SLOTS)),
        "wv0": wv.T,
        "wo0": i["L0_attn_Wo"].T,
        "wr": i["L0_ffn_router_weight"].T,
        "ebias": i["L0_ffn_expert_bias"],
        "rbias": i["L0_ffn_router_bias"].reshape(1, NE),
        "kmask": kmask,
        "wqkv": wqkv.transpose(3, 2, 0, 1, 4).reshape(NG, P, 3 * KT * HG * HD1),
        "wo1": i["L1_attn_Wo"].T.reshape(NG, HG * HD1, D),
        "gqk": np.stack([i["L1_attn_gq"], i["L1_attn_gk"]], axis=1),
        "lut": i["L1_ffn_lut"].reshape(1, LUT),
        "idx_gate": i["L1_ffn_gate_idx"].T,
        "idx_up": i["L1_ffn_up_idx"].T,
        "idx_down": i["L1_ffn_down_idx"].T,
    }
    arrays = {k: np.ascontiguousarray(v) for k, v in arrays.items()}
    nc = bacc.Bacc("TRN2", target_bir_lowering=False, num_devices=1)
    aps = {k: nc.dram_tensor(f"in_{k}", v.shape, mybir.dt.from_np(v.dtype), kind="ExternalInput").ap()
           for k, v in arrays.items()}
    out = nc.dram_tensor("out", (NB, SEQ, D), F32, kind="ExternalOutput").ap()
    build(nc, aps, out)
    r = run_bass_kernel_spmd(nc, [{f"in_{k}": v for k, v in arrays.items()}], core_ids=[0])
    return r.results[0]["out"]
```

```python
from contextlib import ExitStack

import concourse.bass as bass
from concourse import mybir

F32 = mybir.dt.float32
F32R = mybir.dt.float32r
BF16 = mybir.dt.bfloat16
I32 = mybir.dt.int32
ALU = mybir.AluOpType
ACT = mybir.ActivationFunctionType
AX = mybir.AxisListType

P = 128
NB = 4
SEQ = 512
QT = SEQ // P
D = 256
KT = D // P
NH = 16
HD0 = 16
HD1 = 128
HG = 4
NG = NH // HG
ITEMS = HG * QT
ITEMS0 = NH * QT
NE = 64
TOPK = 8
INTER = 688
MT = -(-INTER // P)
LAST = INTER - (MT - 1) * P
LUT = 16
NMOD = 6
SA, CA, GA, SB, CB, GB = range(NMOD)
LATER_MODS = ((0, 1), (0, 2), (1, 0), (1, 1), (1, 2))
NEWTON = 3
NORM_PARTS = 11 + NEWTON
EPS = 1e-5
NEG = -1e30
Q_SLOT = (0, 0, 0, 1, 1, 2)
K_SLOT = (0, 1, 2, 0, 1, 0)
SLOTS = len(Q_SLOT)
SHIFT = SLOTS * HD0
TURN = 29
VALUE = TURN + 2
AFTER = VALUE + 2
VW = 32
LAG1 = 3
SCORE_BANKS = (3, 4, 2)


class Chain:

    def __init__(self, eng, sem):
        self.eng, self.sem, self.base, self.n = eng, sem, 0, 0

    def begin(self, base):
        self.base, self.n = base, 0

    def mark(self, ins):
        self.n += 1
        ins.then_inc(self.sem, 1)

    def wait(self):
        self.eng.wait_ge(self.sem, self.base + self.n)

    def step(self, ins):
        self.mark(ins)
        self.wait()


def rsqrt_seed(dve, ch, y, t, v):
    ch.step(dve.tensor_scalar(t.bitcast(I32), v.bitcast(I32), 1, None, ALU.arith_shift_right))
    ch.mark(dve.tensor_scalar(y.bitcast(I32), t.bitcast(I32), -1.0, float(0x5F3759DF), ALU.mult, ALU.add))


def rsqrt_newton(dve, ch, y, t, v):
    ch.wait()
    ch.step(dve.tensor_tensor(t, y, y, ALU.mult))
    ch.step(dve.scalar_tensor_tensor(out=t, in0=t, scalar=-0.5, in1=v, op0=ALU.mult, op1=ALU.mult))
    ch.mark(dve.scalar_tensor_tensor(out=y, in0=t, scalar=1.5, in1=y, op0=ALU.add, op1=ALU.mult))


def at_step(n, lag, b, new, old):
    if n >= lag:
        return (n - lag, b) if new else (None, None)
    return (n - lag + ITEMS0, b - 1) if old else (None, None)


def f32(ap):
    return ap.bitcast(F32)


def build(nc, a, out):
    x_v = a["x"].rearrange("b (t p) d -> p (b t) d", p=P)
    out_v = out.rearrange("b (t p) d -> p (b t) d", p=P)
    q_parts = nc.dram_tensor("q_parts", (3, D, NB * SEQ), BF16).ap()
    h1_saved = nc.dram_tensor("h1_saved", (NB, P, 2 * KT * SEQ), F32).ap()
    wffn_saved = nc.dram_tensor("wffn_saved", (P, 2 * KT * INTER + MT * D), F32).ap()

    with ExitStack() as top:
        sems = {}

        def sem(name):
            if name not in sems:
                sems[name] = top.enter_context(nc.semaphore(name))
            return sems[name]

        def sb(stack, name, shape, dt=F32):
            return stack.enter_context(nc.sbuf_tensor(name, shape, dt))

        bank = [top.enter_context(nc.psum_tensor(f"bank{i}", [P, 512], F32)) for i in range(8)]

        x = sb(top, "x", [P, NB * QT, D])
        mod1 = sb(top, "mod1", [P, NB, NMOD, D])
        identf = sb(top, "identf", [P, P])
        identb = sb(top, "identb", [P, P], BF16)
        maskb = sb(top, "maskb", [P, P], BF16)
        maskT = sb(top, "maskT", [P, P], BF16)
        pad = sb(top, "pad", [P, 96])
        hN = sb(top, "hN", [P, QT, D])
        hH = sb(top, "hH", [P, KT, SEQ], F32R)
        hL = sb(top, "hL", [P, KT, SEQ], F32R)
        gqk = sb(top, "gqk", [P, 3])
        stats = sb(top, "stats", [P, QT, 6])
        mv = sb(top, "mv", [P, QT, 2])
        sm = sb(top, "sm", [P, 4, 2 * ITEMS])
        negmax = sb(top, "negmax", [P, ITEMS0])
        sums = sb(top, "sums", [P, ITEMS0])
        rsum = sb(top, "rsum", [P, ITEMS0])
        probs = sb(top, "probs", [P, 4, SEQ])
        ytmp = sb(top, "ytmp", [P, 2, D])

        s0 = ExitStack()
        wmod = sb(s0, "wmod", [P, 2, KT, NMOD * D])
        qhi = sb(s0, "qhi", [P, 2, SEQ], BF16)
        qmi = sb(s0, "qmi", [P, 2, SEQ], BF16)
        qlo = sb(s0, "qlo", [P, 2, SEQ], BF16)
        cB = sb(s0, "cB", [P, 2, KT, 1, P])
        qst = sb(s0, "qst", [P, NH * SEQ], BF16)
        mod = [sb(s0, "mod0", [P, NB, NMOD, D]), mod1]
        cT = sb(s0, "cT", [P, 2, KT, NB])
        sc = sb(s0, "sc", [P, 2, KT, NB])
        ones = sb(s0, "ones", [P, P])
        cB0 = sb(s0, "cB0", [P, KT, NB, P])
        W0N = D + P + HD0 + D + NE
        w0 = sb(s0, "w0", [P, KT, W0N])
        w0H = sb(s0, "w0H", [P, KT, W0N], F32R)
        w0L = sb(s0, "w0L", [P, KT, W0N], F32R)
        WQ, WK, WV, WO, WR = (slice(o, o + n) for o, n in
                              ((0, D), (D, P), (D + P, HD0), (D + P + HD0, D), (2 * D + P + HD0, NE)))
        ebias = sb(s0, "ebias", [NE, D])
        rbias = sb(s0, "rbias", [P, NE])
        kmask = sb(s0, "kmask", [P, 4 + QT])
        nmp = sb(s0, "nmp", [P, HG, P], BF16)
        nmr = sb(s0, "nmr", [P, HG, QT])
        q32 = probs[:, 0:KT, :]
        sgn = hN[:, 0:2, :]
        kst = sb(s0, "kst", [P, NB * SEQ], BF16)
        v0 = sb(s0, "v0", [P, NB * QT, HD0])
        vS = sb(s0, "vS", [P, QT, VW])
        rsum0_t = sb(s0, "rsum0_t", [P, QT, HG, 1])
        oRaw = sb(s0, "oRaw", [P, SEQ])
        oTok = sb(s0, "oTok", [P, QT, D])
        oH0 = sb(s0, "oH0", [P, KT, SEQ], F32R)
        oL0 = sb(s0, "oL0", [P, KT, SEQ], F32R)
        lg = sb(s0, "lg", [P, QT, NE])
        ex = sb(s0, "ex", [P, QT, NE])
        rest = sb(s0, "rest", [P, QT, NE])
        top8 = sb(s0, "top8", [P, QT, TOPK])
        rsm = sb(s0, "rsm", [P, 4, QT])
        wT = sb(s0, "wT", [NE, SEQ])
        lut = sb(s0, "lut", [P, LUT])
        idx = sb(s0, "idx", [P, MT * D], I32)
        wf = sb(s0, "wf", [P, MT * D])
        wft = sb(s0, "wft", [P, MT * D])
        hH2, hL2 = (w[:, 0:KT * SEQ].bitcast(F32R).rearrange("p (k t) -> p k t", k=KT) for w in (wf, wft))
        s0.close()

        s1 = ExitStack()
        wgH = sb(s1, "wgH", [P, 3 * KT, HG * HD1], F32R)
        wgL = sb(s1, "wgL", [P, 3 * KT, HG * HD1], F32R)
        woH = sb(s1, "woH", [P, HG, D], F32R)
        woL = sb(s1, "woL", [P, HG, D], F32R)
        wo = sb(s1, "wo", [P, HG, D])
        wg = sb(s1, "wg", [P, 3 * KT, HG * HD1])
        qk = sb(s1, "qk", [P, QT, 2, HG * HD1])
        qkst = sb(s1, "qkst", [P, QT * 2 * HG, 6])
        qT = sb(s1, "qT", [P, HG, SEQ])
        kT = sb(s1, "kT", [P, HG, SEQ])
        v1 = sb(s1, "v1", [P, QT, HG * HD1])
        pT1 = sb(s1, "pT1", [P, 2, QT * (QT + 1) // 2 * P])
        oH1 = sb(s1, "oH1", [P, HG, SEQ], F32R)
        oL1 = sb(s1, "oL1", [P, HG, SEQ], F32R)
        wguH = sb(s1, "wguH", [P, 2, KT, MT * P], F32R)
        wdH = sb(s1, "wdH", [P, MT, D], F32R)
        wdL = sb(s1, "wdL", [P, MT, D], F32R)
        wraw = sb(s1, "wraw", [P, max(INTER, MT * D // 2)])
        s1.close()

        s2 = ExitStack()
        sg = sb(s2, "sg", [P, 2, SEQ])
        hf = sb(s2, "hf", [P, 2, SEQ])
        hmH = sb(s2, "hmH", [P, MT, SEQ], F32R)
        hmL = sb(s2, "hmL", [P, MT, SEQ], F32R)
        sb(s2, "as_wo", [P, HG, D])
        wguL = sb(s2, "wguL", [P, 2, KT, MT * P], F32R)
        s2.close()

        def xb(b, t, n=1):
            return x[:, bass.ds(b * QT + t, n), :]

        def modb(l, b, c):
            return mod[l][:, bass.ds(b, 1), c, :]

        def mm3(pe, o, wH, wL, mH, mL, start, stop):
            pe.matmul(o, wL, mH, start=start, stop=False)
            pe.matmul(o, wH, mL, start=False, stop=False)
            return pe.matmul(o, wH, mH, start=False, stop=stop)

        class Norm:
            def __init__(self, name, layer, c, s):
                self.layer, self.c, self.s = layer, c, s
                self.h, self.tp, self.hi, self.lo = (sem(f"{name}_{w}") for w in ("h", "tp", "hi", "lo"))

            def dve(self, dve, ch, b, r):
                for part in range(NORM_PARTS):
                    self.dve_part(part, dve, ch, b, r)

            def dve_part(self, part, dve, ch, b, r, high=hH, low=hL):
                m, s = modb(self.layer, b, self.c), modb(self.layer, b, self.s)
                v, t, y = sm[:, 0, 0:QT], sm[:, 1, 0:QT], sm[:, 2, 0:QT]
                half = lambda i: slice(i * QT // 2, (i + 1) * QT // 2)
                if part < 2:
                    vector_carrier(dve)
                    for i in range(QT)[half(part)]:
                        last = dve.bn_stats(stats[:, i, :], xb(b, i))
                    ch.mark(last)
                elif part == 2:
                    ch.wait()
                    vector_carrier(dve)
                    for i in range(QT):
                        last = dve.bn_aggr(mv[:, i, :], stats[:, i, :])
                    ch.step(last)
                    ch.mark(dve.tensor_scalar(v, mv[:, :, 1], EPS, None, ALU.add))
                elif part == 3:
                    ch.wait()
                    rsqrt_seed(dve, ch, y, t, v)
                elif part < 4 + NEWTON:
                    rsqrt_newton(dve, ch, y, t, v)
                elif part < 6 + NEWTON:
                    ch.wait()
                    for i in range(QT)[half(part - 4 - NEWTON)]:
                        last = dve.tensor_scalar(hN[:, i, :], xb(b, i), mv[:, i, 0:1], sm[:, 2, i:i + 1],
                                                 ALU.subtract, ALU.mult)
                    ch.mark(last)
                elif part < 8 + NEWTON:
                    ch.wait()
                    h = hN[:, half(part - 6 - NEWTON), :]
                    ch.mark(dve.tensor_tensor(h, h, m.to_broadcast([P, QT // 2, D]), ALU.mult))
                elif part < 10 + NEWTON:
                    ch.wait()
                    h = hN[:, half(part - 8 - NEWTON), :]
                    ins = dve.tensor_tensor(h, h, s.to_broadcast([P, QT // 2, D]), ALU.add)
                    ins.then_inc(self.h, 1)
                else:
                    for k in range(KT):
                        dve.wait_ge(self.hi, r * KT + k + 1)
                        dve.tensor_tensor(low[:, k, :], bank[6 + k][:, :], f32(high[:, k, :]),
                                          ALU.subtract).then_inc(self.lo, 1)

            def act(self, act, r, free, high=hH):
                free()
                for k in range(KT):
                    act.wait_ge(self.tp, r * KT + k + 1)
                    act.activation(high[:, k, :], bank[6 + k][:, :], ACT.Copy).then_inc(self.hi, 1)

            def pe(self, pe, r):
                pe.wait_ge(self.h, (r + 1) * 2)
                for k in range(KT):
                    for t in range(QT):
                        last = pe.transpose(bank[6 + k][:, t * P:(t + 1) * P], hN[:, t, k * P:(k + 1) * P],
                                            identf[:, :])
                    last.then_inc(self.tp, 1)

            def wait_ready(self, pe, r):
                pe.wait_ge(self.lo, (r + 1) * KT)

        norm_a0 = Norm("norm_a0", 0, CA, SA)
        norm_f0 = Norm("norm_f0", 0, CB, SB)
        norm_a1 = Norm("norm_a1", 1, CA, SA)
        norm_f1 = Norm("norm_f1", 1, CB, SB)

        loaded_c, loaded_w0, loaded_x, loaded_idx, loaded_misc = map(
            sem, ("loaded_c", "loaded_w0", "loaded_x", "loaded_idx", "loaded_misc"))
        loaded_m0, loaded_m, loaded_x0, consts, q_hi, k_hi = map(
            sem, ("loaded_m0", "loaded_m", "loaded_x0", "consts", "q_hi", "k_hi"))
        silu_c, cb_ready, mod_pe, mod_done = map(
            sem, ("silu_c", "cb_ready", "mod_pe", "mod_done"))
        w0_hi, w0_lo = sem("w0_hi"), sem("w0_lo")
        qkv_pe, q_scaled, q_split, q_stored, k_read, v_read = map(
            sem, ("qkv_pe", "q_scaled", "q_split", "q_stored", "k_read", "v_read"))
        dchain = [sem(f"dve_chain{i}") for i in range(6)]
        q_loaded = [sem(f"q_loaded{g}") for g in range(NG)]
        s0_pe, max0, nm_split, nm_pe, nm_ready, st_pe, exp0, pv0, v_moved, o_copied, o_turned, oev0 = map(
            sem, ("scores0", "max0", "negmax_split", "negmax_turned", "negmax_ready", "scoresT0", "exp0", "pv0",
                  "v_moved", "o_copied", "o_turned", "o0_ready"))
        ot_pe, ot_hi, ot_lo, y0_pe = map(sem, ("oT_pe", "oT_hi", "oT_lo", "y0_pe"))
        r_pe, r_nmax, r_exp, r_w, r_tp, r_wT, r_y = map(
            sem, ("route_pe", "route_max", "route_exp", "route_w", "route_tp", "route_wT", "route_y"))
        h1_stored = sem("h1_stored")
        gat, gat_dma = sem("gathered"), sem("gathered_dma")
        w1_loaded, w1_hi, w1_lo, h1_loaded, gqk_ready = map(
            sem, ("w1_loaded", "w1_hi", "w1_lo", "h1_loaded", "gqk_ready"))
        p1_pe, p1_act, p1_dve, qk_norm = map(
            sem, ("proj1", "proj1_copied", "proj1_stats", "qk_normed"))
        tr_pe, tr_act = sem("qkT_pe"), sem("qkT_ready")
        s1_pe, max1, exp1, nrm1, t1_pe, ev1, pv1, o1_hi, o1_lo, y1_pe, x1_add = map(
            sem, ("scores1", "max1", "exp1", "normed1", "turned1", "pT1_ready", "pv1", "o1_hi", "o1_lo",
                  "y1_pe", "x1_added"))
        rsum0, y2_gated = sem("rsum0"), sem("y2_gated")
        y1_gated, rsum1 = sem("y1_gated"), sem("rsum1")
        f_loaded, f_zero, f_hi, f_lo = map(sem, ("f_loaded", "f_zero", "f_hi", "f_lo"))
        gu_pe, f_silu, f_h, f_hhi, f_hlo, y2_pe, x2_add, stored = map(
            sem, ("gateup_pe", "silu", "f_h", "f_h_hi", "f_h_lo", "y2_pe", "x2_added", "stored"))

        carriers = [0]

        def vector_carrier(dve):
            dve.memset(pad[:, carriers[0]:carriers[0] + 1], 0.0)
            carriers[0] += 1

        def tensor_carrier(pe, o):
            pe.matmul(o, identb[:, :], identb[:, :], start=True, stop=True)

        block = top.enter_context(nc.Block())

        @block.sync
        def _(sp):
            sp.dma_start(cT[:, :, :, :], a["cT"]).then_inc(loaded_c, 16)
            wm = [a[f"wmod{l}"].rearrange("(k p) n -> p k n", p=P) for l in range(2)]
            sp.dma_start(wmod[:, 0, :, 0:2 * D], wm[0][:, :, 0:2 * D]).then_inc(loaded_m0, 16)
            sp.dma_start(x[:, 0:QT, :], x_v[:, 0:QT, :]).then_inc(loaded_x0, 16)
            for name, cols in (("wq0", WQ), ("wk0", WK), ("wv0", WV), ("wo0", WO), ("wr", WR)):
                sp.dma_start(w0[:, :, cols], a[name].rearrange("(k p) n -> p k n", p=P)).then_inc(loaded_w0, 16)
            sp.dma_start(x[:, QT:, :], x_v[:, QT:, :]).then_inc(loaded_x, 16)
            sp.dma_start(wmod[:, 0, :, 2 * D:], wm[0][:, :, 2 * D:]).then_inc(loaded_m, 16)
            sp.dma_start(wmod[:, 1, :, :], wm[1]).then_inc(loaded_m, 16)
            sp.dma_start(kmask[:, :], a["kmask"]).then_inc(loaded_misc, 16)
            sp.dma_start(gqk[:, 0:2], a["gqk"]).then_inc(gqk_ready, 16)
            sp.dma_start(ebias[:, :], a["ebias"]).then_inc(loaded_misc, 16)
            sp.dma_start(rbias[:, :], a["rbias"].to_broadcast([P, NE])).then_inc(loaded_misc, 16)
            with sp.Fori(0, NB) as b:
                for m in range(KT):
                    sp.wait_ge(q_split, (b * KT + m + 1) * 2)
                    for i, part in enumerate((qhi, qmi, qlo)):
                        sp.dma_start(q_parts[i, m * P:(m + 1) * P, bass.ds(b * SEQ, SEQ)],
                                     part[:, m, :]).then_inc(q_stored, 16)
            sp.wait_ge(k_read, NB)
            sp.wait_ge(q_stored, NB * KT * 3 * 16)

            def load_q(b, g):
                for s, part in enumerate(Q_SLOT):
                    sp.dma_start(qst[s * HD0:(s + 1) * HD0, g * HG * SEQ:(g + 1) * HG * SEQ].rearrange("d (h t) -> d h t", h=HG),
                                 q_parts[part].rearrange("(h d) t -> d h t", d=HD0)[:, g * HG:(g + 1) * HG, bass.ds(b * SEQ, SEQ)]
                                 ).then_inc(q_loaded[g], 16)

            for g in range(NG):
                load_q(0, g)
            with sp.Fori(1, NB) as b:
                for g in range(NG):
                    sp.wait_ge(st_pe, (b - 1) * ITEMS0 + (g + 1) * ITEMS)
                    load_q(b, g)

            def load_w1(g):
                sp.dma_start(wg[:, :, :], a["wqkv"][g].rearrange("p (k n) -> p k n", k=3 * KT)).then_inc(w1_loaded, 16)
                sp.dma_start(wo[:, :, :], a["wo1"][g].rearrange("(h p) n -> p h n", p=P)).then_inc(w1_loaded, 16)

            def load_h1(b):
                sp.dma_start(f32(hH[:, :, :]).rearrange("p k t -> p (k t)"), h1_saved[b, :, 0:KT * SEQ]).then_inc(h1_loaded, 16)
                sp.dma_start(f32(hL[:, :, :]).rearrange("p k t -> p (k t)"), h1_saved[b, :, KT * SEQ:]).then_inc(h1_loaded, 16)

            sp.wait_ge(st_pe, NB * ITEMS0)
            load_w1(0)
            sp.wait_ge(r_pe, NB)
            sp.wait_ge(h1_stored, (NB - 1) * 32)
            load_h1(0)
            sp.wait_ge(h1_stored, NB * 32)

            def load_later_h1(g):
                with sp.Fori(1, NB) as b:
                    sp.wait_ge(p1_pe, (g * NB + b) * 3 * QT)
                    load_h1(b)

            with sp.Fori(0, NG - 1) as g:
                load_later_h1(g)
                sp.wait_ge(w1_lo, (g + 1) * (3 * KT + HG))
                load_w1(g + 1)
                sp.wait_ge(p1_pe, (g + 1) * NB * 3 * QT)
                load_h1(0)
            load_later_h1(NG - 1)
            with sp.Fori(0, NB) as b:
                for t2 in range(2):
                    sp.wait_ge(x2_add, b * 2 + t2 + 1)
                    sp.dma_start(out_v[:, bass.ds(b * QT + 2 * t2, 2), :], xb(b, 2 * t2, 2)).then_inc(stored, 16)
            sp.wait_ge(stored, NB * 2 * 16)

        @block.gpsimd
        def _(pool):
            pool.memset(identf[:, :], 0.0).then_inc(consts, 1)
            pool.memset(ones[:, :], 0.0).then_inc(consts, 1)
            pool.wait_ge(consts, 2)
            pool.affine_select(out=identf[:, :], in_=identf[:, :], compare_op=ALU.not_equal, fill=1.0, base=0,
                               pattern=[[-1, P]], channel_multiplier=1).then_inc(consts, 1)
            pool.affine_select(out=maskb[:, :], in_=ones[:, :], compare_op=ALU.is_ge, fill=NEG, base=0,
                               pattern=[[-1, P]], channel_multiplier=1).then_inc(consts, 1)
            pool.affine_select(out=maskT[:, :], in_=ones[:, :], compare_op=ALU.is_ge, fill=NEG, base=0,
                               pattern=[[1, P]], channel_multiplier=-1).then_inc(consts, 1)
            pool.memset(nmp[:, :, :], 0.0).then_inc(consts, 1)
            pool.wait_ge(consts, 6)
            pool.tensor_copy(identb[:, :], identf[:, :]).then_inc(consts, 1)
            pool.memset(vS[:, :, :], 1.0).then_inc(consts, 1)
            pool.memset(ones[:, :], 1.0).then_inc(consts, 1)
            n = [0]

            def link(ins):
                n[0] += 1
                ins.then_inc(gat, 1)
                pool.wait_ge(gat, n[0])

            pool.dma_start(lut[:, :], a["lut"].to_broadcast([P, LUT])).then_inc(loaded_idx, 16)
            jobs = [(a[f"idx_{w}"].rearrange("(k p) n -> p k n", p=P), P, 0, KT * INTER, n * KT * INTER)
                    for n, w in enumerate(("gate", "up"))]
            jobs += [(a["idx_down"][0:(MT - 1) * P, :].rearrange("(m p) n -> p m n", p=P), P, 0, (MT - 1) * D,
                      2 * KT * INTER),
                     (a["idx_down"][(MT - 1) * P:, :], LAST, (MT - 1) * D, D, 2 * KT * INTER + (MT - 1) * D)]
            link(pool.memset(wf[:, :], 0.0))
            for i, (src, rows, o, cols, at) in enumerate(jobs):
                part = idx[0:rows, o:o + cols]
                if len(src.shape) == 3:
                    part = part.rearrange("p (k n) -> p k n", k=src.shape[1])
                pool.dma_start(part, src).then_inc(loaded_idx, 16)
                pool.wait_ge(loaded_idx, (i + 2) * 16)
                if i:
                    pool.wait_ge(gat_dma, i * 16)
                if i == 3:
                    link(pool.memset(wf[:, o:o + cols], 0.0))
                part, acc, tmp = idx[0:rows, o:o + cols], wf[0:rows, o:o + cols], wft[0:rows, o:o + cols]
                for j in range(LUT):
                    link(pool.tensor_scalar(tmp if j else acc, part, float(j), lut[0:rows, j:j + 1],
                                            ALU.is_equal, ALU.mult))
                    if j:
                        link(pool.tensor_tensor(acc, acc, tmp, ALU.add))
                pool.dma_start(wffn_saved[:, at:at + cols], wf[:, o:o + cols]).then_inc(gat_dma, 16)

            pool.wait_ge(h1_stored, NB * 32)
            pool.wait_ge(gat_dma, 4 * 16)
            pool.memset(f32(wguH[:, :, :, INTER:]), 0.0).then_inc(f_zero, 1)
            pool.wait_ge(w1_lo, NG * (3 * KT + HG))
            pool.memset(f32(wguL[:, :, :, INTER:]), 0.0).then_inc(f_zero, 1)
            strips = [((w * KT + k) * INTER, wguH[:, w, k, 0:INTER], wguL[:, w, k, 0:INTER])
                      for w in range(2) for k in range(KT)]
            strips += [(2 * KT * INTER + j * (MT * D // 2), wdH[:, j * MT // 2:(j + 1) * MT // 2, :],
                        wdL[:, j * MT // 2:(j + 1) * MT // 2, :]) for j in range(2)]
            for i, (at, hi, lo) in enumerate(strips):
                cols = INTER if i < 2 * KT else MT * D // 2
                raw = wraw[:, 0:cols]
                if i >= 2 * KT:
                    raw = raw.rearrange("p (m n) -> p m n", n=D)
                if i:
                    pool.wait_ge(f_lo, i)
                pool.dma_start(wraw[:, 0:cols], wffn_saved[:, at:at + cols]).then_inc(f_loaded, 16)
                pool.wait_ge(f_loaded, (i + 1) * 16)
                pool.tensor_copy(hi, raw).then_inc(f_hi, 1)
                pool.wait_ge(f_hi, i + 1)
                pool.tensor_tensor(lo, raw, f32(hi), ALU.subtract).then_inc(f_lo, 1)

        @block.scalar
        def _(act):
            act.wait_ge(loaded_c, 16)
            act.activation(sc[:, :, :, :], cT[:, :, :, :], ACT.Silu).then_inc(silu_c, 1)

            def copy_mod(u, o, l, b, c):
                act.wait_ge(mod_pe, u + 1)
                for j in range(2):
                    last = act.activation(mod[l][:, b, 2 * c + j, :], o[:, j * D:(j + 1) * D], ACT.Copy,
                                          bias=1.0 if 2 * c + j in (CA, CB) else 0.0)
                last.then_inc(mod_done, 1)

            for b in range(NB):
                copy_mod(b, bank[4 + b % 2], 0, b, 0)
            act.wait_ge(loaded_w0, 5 * 16)
            act.activation(w0H[:, :, :], w0[:, :, :], ACT.Copy).then_inc(w0_hi, 1)

            def qkv0(b, following):
                for m in range(KT):
                    act.wait_ge(qkv_pe, b * (KT + 2) + m + 1)
                    act.wait_ge(q_split, b * KT * 2)
                    act.activation(q32[:, m, :], bank[m][:, :], ACT.Copy, scale=HD0 ** -0.5).then_inc(q_scaled, 1)
                    act.wait_ge(q_scaled, b * KT + m + 1)
                    act.wait_ge(q_stored, b * KT * 3 * 16)
                    act.activation(qhi[:, m, :], q32[:, m, :], ACT.Copy).then_inc(q_hi, 1)
                act.wait_ge(qkv_pe, b * (KT + 2) + KT + 1)
                act.wait_ge(k_read, b)
                act.activation(qst[:, 0:SEQ], bank[2][:, :], ACT.Copy).then_inc(k_hi, 1)
                act.wait_ge(qkv_pe, (b + 1) * (KT + 2))
                act.activation(v0[:, bass.ds(b * QT, QT), :], bank[3][:, 0:QT * HD0].rearrange("p (t d) -> p t d", d=HD0),
                               ACT.Copy).then_inc(v_read, 1)
                if following is not None:
                    norm_a0.act(act, following, lambda: act.wait_ge(qkv_pe, following * (KT + 2)))
                for j, (l, c) in enumerate(LATER_MODS):
                    copy_mod(NB + b * len(LATER_MODS) + j, bank[4 + j % 2], l, b, c)

            norm_a0.act(act, 0, lambda: None)
            with act.Fori(0, NB - 1) as b:
                qkv0(b, b + 1)
            qkv0(NB - 1, None)

            def after0(n, b, last):
                if n == 31 and last:
                    act.wait_ge(q_stored, NB * KT * 3 * 16)
                    split_w1(0)
                if n in (3, 4):
                    k = n - 3
                    act.wait_ge(ot_pe, b * KT + k + 1)
                    act.wait_ge(y0_pe, b * 2)
                    act.activation(oH0[:, k, :], bank[6 + k][:, :], ACT.Copy).then_inc(ot_hi, 1)
                elif n == 25:
                    norm_f0.act(act, b, lambda: act.wait_ge(h1_stored, b * 32))
                elif n == 30:
                    act.wait_ge(r_nmax, b + 1)
                    for t in range(QT):
                        act.activation(ex[:, t, :], lg[:, t, :], ACT.Exp, bias=rsm[:, 0, t:t + 1],
                                       accum_out=rsm[:, 1, t:t + 1]).then_inc(r_exp, 1)
                elif n == 38:
                    act.wait_ge(r_tp, b + 1)
                    act.activation(wT[:, :], bank[7][0:NE, :], ACT.Copy).then_inc(r_wT, 1)
                elif n == 60:
                    if last:
                        norm_a1.act(act, b, lambda: act.wait_ge(gat_dma, 4 * 16), hH2)
                    else:
                        norm_a1.act(act, b, lambda: act.wait_ge(r_pe, b + 1))
                elif n == 62:
                    act.wait_ge(norm_a1.lo, (b + 1) * KT)
                    high, low = (hH2, hL2) if last else (hH, hL)
                    act.dma_start(h1_saved[b, :, 0:KT * SEQ], f32(high[:, :, :]).rearrange("p k t -> p (k t)")).then_inc(h1_stored, 16)
                    act.dma_start(h1_saved[b, :, KT * SEQ:], f32(low[:, :, :]).rearrange("p k t -> p (k t)")).then_inc(h1_stored, 16)

            def split_w1(g):
                act.wait_ge(w1_loaded, (g + 1) * 32)
                act.wait_ge(p1_pe, g * NB * 3 * QT)
                for c in range(3 * KT):
                    act.activation(wgH[:, c, :], wg[:, c, :], ACT.Copy).then_inc(w1_hi, 1)
                act.wait_ge(y1_pe, g * NB * 2)
                for c in range(HG):
                    act.activation(woH[:, c, :], wo[:, c, :], ACT.Copy).then_inc(w1_hi, 1)

            def steps0(b, scores=False, values=False, after=False, end=False):
                for n in range(ITEMS0):
                    i, batch = at_step(n, TURN, b, scores, values)
                    if i is not None:
                        w = SEQ - i % QT * P
                        act.wait_ge(st_pe, batch * ITEMS0 + i + 1)
                        act.wait_ge(pv0, batch * ITEMS0 + max(i - 3, 0))
                        act.activation(probs[:, i % 4, 0:w], bank[2 + i % 2][:, 0:w], ACT.Exp).then_inc(exp0, 1)
                    for t in range(QT):
                        i, batch = at_step(n, 4 + t, b, scores, values)
                        if i is not None and i % ITEMS == ITEMS - 1:
                            g = i // ITEMS
                            act.wait_ge(nm_pe, batch * NG + g + 1)
                            to = qst[SHIFT:P, g * HG * SEQ:(g + 1) * HG * SEQ].rearrange("p (h t q) -> p h t q", h=HG, t=QT)
                            act.activation(to[:, :, t, :], bank[4][SHIFT:P, :].rearrange("p (h q) -> p h q", h=HG),
                                           ACT.Copy, scale=kmask[SHIFT:P, 4 + t:5 + t]).then_inc(nm_ready, 1)
                    i, batch = at_step(n, VALUE, b, scores, values)
                    if i == 0:
                        act.wait_ge(pv0, batch * ITEMS0)
                        act.activation(vS[:, :, 0:HD0], v0[:, bass.ds(batch * QT, QT), :], ACT.Copy).then_inc(v_moved, 1)
                    i, batch = at_step(n, VALUE + 1, b, scores, values)
                    if i is not None and i % ITEMS == ITEMS - 1:
                        act.wait_ge(pv0, batch * ITEMS0 + i + 1)
                        act.wait_ge(o_turned, batch * NG + i // ITEMS)
                        act.activation(oRaw[:, :], bank[5][:, :], ACT.Copy).then_inc(o_copied, 1)
                    i, batch = at_step(n, AFTER, b - 1, after, end)
                    if i is not None:
                        after0(i, batch, isinstance(batch, int) and batch == NB - 1)

            steps0(0, scores=True)
            steps0(1, scores=True, values=True, after=True)
            with act.Fori(2, NB) as b:
                steps0(b, scores=True, values=True, after=True, end=True)
            steps0(NB, values=True, after=True, end=True)
            steps0(NB + 1, end=True)

            act.wait_ge(gqk_ready, 16)
            act.activation(gqk[:, 2:3], gqk[:, 0:1], ACT.Copy, scale=gqk[:, 1:2]).then_inc(gqk_ready, 1)
            act.wait_ge(gqk_ready, 17)
            act.activation(gqk[:, 2:3], gqk[:, 2:3], ACT.Copy, scale=HD1 ** -0.5).then_inc(gqk_ready, 1)
            act.wait_ge(gqk_ready, 18)

            def rounds1(g):
                with act.Fori(0, NB) as b:
                    it = g * NB + b
                    act.wait_ge(tr_pe, it * 2 * QT)
                    act.wait_ge(pv1, it * HG)
                    for u in range(3 * QT):
                        act.wait_ge(p1_pe, it * 3 * QT + u + 1)
                        dst = qk[:, u // 2, u % 2, :] if u < 2 * QT else v1[:, u - 2 * QT, :]
                        act.activation(dst, bank[u % 3][:, :], ACT.Copy).then_inc(p1_act, 1)
                    for u in range(2 * QT):
                        act.wait_ge(tr_pe, it * 2 * QT + u + 1)
                        t = u // 2
                        dst = (qT, kT)[u % 2][:, :, t * P:(t + 1) * P]
                        act.activation(dst, bank[u % 3][:, :].rearrange("p (h t) -> p h t", h=HG), ACT.Copy,
                                       scale=1.0 if u % 2 else gqk[:, 2:3]).then_inc(tr_act, 1)
                    for s in range(ITEMS + LAG1 + 2):
                        i = s - LAG1
                        if 0 <= i < ITEMS:
                            h, t = i // QT, i % QT
                            act.wait_ge(t1_pe, it * ITEMS + i + 1)
                            act.wait_ge(pv1, it * HG + max(h - 1, 0))
                            at = t * (t + 1) // 2 * P
                            act.activation(pT1[:, h % 2, at:at + (t + 1) * P], bank[5 + i % 2][:, 0:(t + 1) * P],
                                           ACT.Copy).then_inc(ev1, 1)
                        if s < ITEMS:
                            i = s
                            n = (i % QT + 1) * P
                            act.wait_ge(max1, it * ITEMS + i + 1)
                            act.wait_ge(t1_pe, it * ITEMS + max(i - 3, 0))
                            act.activation(probs[:, i % 4, 0:n], bank[SCORE_BANKS[i % 3]][:, 0:n], ACT.Exp,
                                           bias=negmax[:, i:i + 1], accum_out=sums[:, i:i + 1]).then_inc(exp1, 1)
                        i = s - LAG1 - 2
                        if i >= 0 and i % QT == QT - 1:
                            h = i // QT
                            act.wait_ge(pv1, it * HG + h + 1)
                            act.wait_ge(y1_pe, it * 2)
                            act.activation(oH1[:, h, :], bank[7][:, :], ACT.Copy).then_inc(o1_hi, 1)

            with act.Fori(0, NG - 1) as g:
                rounds1(g)
                split_w1(g + 1)
            rounds1(NG - 1)

            def swiglu(b, following):
                for m in range(MT):
                    act.wait_ge(gu_pe, b * MT + m + 1)
                    act.wait_ge(f_h, b * MT + max(m - 1, 0))
                    act.activation(sg[:, m % 2, :], bank[2 * (m % 2)][:, :], ACT.Silu).then_inc(f_silu, 1)
                    act.wait_ge(f_h, b * MT + m + 1)
                    act.wait_ge(y2_pe, b * 2)
                    act.activation(hmH[:, m, :], hf[:, m % 2, :], ACT.Copy).then_inc(f_hhi, 1)
                if following is not None:
                    norm_f1.act(act, following, lambda: act.wait_ge(gu_pe, following * MT))

            norm_f1.act(act, 0, lambda: act.wait_ge(p1_pe, NG * NB * 3 * QT))
            act.wait_ge(y1_pe, NG * NB * 2)
            with act.Fori(0, NB - 1) as b:
                swiglu(b, b + 1)
            swiglu(NB - 1, None)

        @block.vector
        def _(dve):
            chains = [Chain(dve, s) for s in dchain]
            dve.wait_ge(consts, 9)
            dve.wait_ge(silu_c, 1)
            for k in range(KT):
                for b in range(NB):
                    last = dve.tensor_scalar(cB0[:, k, b, :], ones[:, :], sc[:, 0, k, b:b + 1], None, ALU.mult)
            last.then_inc(cb_ready, 1)

            norm_ch, ch = chains[1], chains[0]

            def norm_parts(b):
                norm_ch.begin(b * NORM_STEPS)
                for part in range(NORM_PARTS - 1):
                    norm_a0.dve_part(part, dve, norm_ch, b, b)
                assert norm_ch.n == NORM_STEPS, norm_ch.n

            def qkv0(b, following):
                dve.wait_ge(mod_pe, NB + b * len(LATER_MODS))
                dve.tensor_copy(cB[:, :, :, :, :], sc[:, :, :, bass.ds(b, 1)].rearrange(
                    "p l k (b one) -> p l k b one", one=1).to_broadcast([P, 2, KT, 1, P])).then_inc(cb_ready, 1)
                norm_a0.dve_part(NORM_PARTS - 1, dve, norm_ch, b, b)
                if following is not None:
                    norm_parts(following)
                ch.begin(b * QK0_STEPS)
                for m in range(KT):
                    dve.wait_ge(q_hi, b * KT + m + 1)
                    ch.step(dve.tensor_tensor(q32[:, m, :], q32[:, m, :], qhi[:, m, :], ALU.subtract))
                    dve.wait_ge(q_stored, b * KT * 3 * 16)
                    dve.tensor_copy(qmi[:, m, :], q32[:, m, :]).then_inc(q_split, 1)
                    dve.wait_ge(q_split, (b * KT + m) * 2 + 1)
                    dve.tensor_tensor(qlo[:, m, :], q32[:, m, :], qmi[:, m, :], ALU.subtract).then_inc(q_split, 1)
                dve.wait_ge(k_hi, b + 1)
                kb, lo = bank[2][:, :], probs[:, 2, :]
                hb, mb = qst[:, 0:SEQ], qst[:, SEQ:2 * SEQ]
                ch.step(dve.tensor_tensor(lo, kb, hb, ALU.subtract))
                ch.step(dve.tensor_copy(mb, lo))
                ch.step(dve.tensor_tensor(lo, lo, mb, ALU.subtract))
                ch.step(dve.tensor_scalar(lo, lo, kmask[:, 2:3], kmask[:, 3:4], ALU.mult, ALU.add))
                ch.step(dve.scalar_tensor_tensor(out=lo, in0=mb, scalar=kmask[:, 1:2], in1=lo, op0=ALU.mult, op1=ALU.add))
                dve.scalar_tensor_tensor(out=kst[:, bass.ds(b * SEQ, SEQ)], in0=hb, scalar=kmask[:, 0:1], in1=lo,
                                         op0=ALU.mult, op1=ALU.add).then_inc(k_read, 1)
                assert ch.n == QK0_STEPS, ch.n

            dve.wait_ge(loaded_x0, 16)
            dve.wait_ge(mod_done, NB)
            norm_parts(0)
            dve.wait_ge(w0_hi, 1)
            dve.tensor_tensor(w0L[:, :, :], w0[:, :, :], f32(w0H[:, :, :]), ALU.subtract).then_inc(w0_lo, 1)
            dve.wait_ge(loaded_x, 16)
            dve.wait_ge(loaded_misc, 48)
            with dve.Fori(0, NB - 1) as b:
                qkv0(b, b + 1)
            qkv0(NB - 1, None)
            dve.wait_ge(mod_done, NB + NB * len(LATER_MODS))

            ch = chains[2]

            def after0(n, b, last):
                if n == 36 and last:
                    split_w1(0, slice(0, 3 * KT))
                if n == 59 and last:
                    split_w1(0, slice(3 * KT, 3 * KT + HG))
                if n in (0, 2):
                    if n == 0:
                        ch.begin(b * NB0_STEPS)
                    g = mod[n // 2][:, bass.ds(b, 1), GA:GB + 1:GB - GA, :]
                    sign, mag = (w.rearrange("p (one c) d -> p one c d", one=1) for w in (sgn, ytmp[:, :, :]))
                    ch.step(dve.tensor_scalar(sign, g, 0.0, 2.0, ALU.is_ge, ALU.mult))
                    ch.step(dve.scalar_tensor_tensor(out=mag, in0=g, scalar=-1.0, in1=g, op0=ALU.mult, op1=ALU.max))
                    ch.step(dve.tensor_scalar(sign, sign, -1.0, None, ALU.add))
                    ch.step(dve.scalar_tensor_tensor(out=g, in0=mag, scalar=0.25, in1=sign, op0=ALU.max, op1=ALU.mult))
                elif n in (4, 5):
                    k = n - 4
                    dve.wait_ge(ot_hi, b * KT + k + 1)
                    dve.tensor_tensor(oL0[:, k, :], bank[6 + k][:, :], f32(oH0[:, k, :]), ALU.subtract).then_inc(ot_lo, 1)
                elif n in (9, 10):
                    t2 = n - 9
                    dve.wait_ge(y0_pe, b * 2 + t2 + 1)
                    ch.step(dve.tensor_tensor(ytmp[:, :, :], bank[6 + t2][:, :].rearrange("p (t d) -> p t d", d=D),
                                              modb(0, b, GA).to_broadcast([P, 2, D]), ALU.mult))
                    ch.step(dve.tensor_tensor(xb(b, 2 * t2, 2), xb(b, 2 * t2, 2), ytmp[:, :, :], ALU.add))
                elif 11 <= n < 10 + NORM_PARTS:
                    norm_f0.dve_part(n - 11, dve, ch, b, b)
                elif n == 26:
                    norm_f0.dve_part(NORM_PARTS - 1, dve, ch, b, b)
                elif n == 29:
                    dve.wait_ge(r_pe, b + 1)
                    ch.step(dve.tensor_tensor(lg[:, :, :], bank[6][:, 0:QT * NE].rearrange("p (t e) -> p t e", e=NE),
                                              rbias[:, :].rearrange("p (one e) -> p one e", one=1).to_broadcast([P, QT, NE]), ALU.add))
                    dve.tensor_reduce(rsm[:, 0, :], lg[:, :, :], AX.X, ALU.max, negate=True).then_inc(r_nmax, 1)
                elif n == 32:
                    dve.wait_ge(r_exp, (b + 1) * QT)
                    vector_carrier(dve)
                    for t in range(QT):
                        last = dve.max(top8[:, t, :], ex[:, t, :])
                    ch.step(last)
                elif n == 33:
                    vector_carrier(dve)
                    for t in range(QT):
                        last = dve.match_replace(rest[:, t, :], top8[:, t, :], ex[:, t, :], 0.0)
                    ch.step(last)
                elif n == 34:
                    ch.step(dve.tensor_tensor(ex[:, :, :], ex[:, :, :], rest[:, :, :], ALU.subtract))
                    ch.step(dve.reciprocal(rsm[:, 2, :], rsm[:, 1, :]))
                elif n == 35:
                    ch.step(dve.tensor_reduce(rsm[:, 3, :], ex[:, :, :], AX.X, ALU.add))
                    ch.step(dve.tensor_tensor(rsm[:, 3, :], rsm[:, 3, :], rsm[:, 2, :], ALU.mult))
                    dve.tensor_tensor(ex[:, :, :], ex[:, :, :], rsm[:, 2, :].rearrange("p (t one) -> p t one", one=1).to_broadcast([P, QT, NE]),
                                      ALU.mult).then_inc(r_w, 1)
                elif n == 41:
                    dve.wait_ge(r_y, b + 1)
                    for t in range(QT):
                        y = bank[6 + t // 2][:, (t % 2) * D:(t % 2 + 1) * D]
                        last = dve.scalar_tensor_tensor(out=hN[:, t, :], in0=hN[:, t, :], scalar=rsm[:, 3, t:t + 1], in1=y,
                                                        op0=ALU.mult, op1=ALU.add)
                    ch.step(last)
                elif n in (42, 43):
                    h = hN[:, 2 * (n - 42):2 * (n - 42) + 2, :]
                    ch.mark(dve.tensor_tensor(h, h, modb(0, b, GB).to_broadcast([P, 2, D]), ALU.mult))
                elif n in (44, 45):
                    ch.wait()
                    x2 = xb(b, 2 * (n - 44), 2)
                    ch.mark(dve.tensor_tensor(x2, x2, hN[:, 2 * (n - 44):2 * (n - 44) + 2, :], ALU.add))
                    if n == 45:
                        ch.wait()
                elif 46 <= n < 45 + NORM_PARTS:
                    norm_a1.dve_part(n - 46, dve, ch, b, b)
                elif n == 61:
                    norm_a1.dve_part(NORM_PARTS - 1, dve, ch, b, b, *((hH2, hL2) if last else ()))
                    assert ch.n == NB0_STEPS, ch.n

            def split_w1(g, which):
                for c in range(3 * KT + HG)[which]:
                    dve.wait_ge(w1_hi, g * (3 * KT + HG) + c + 1)
                    whole, hi, lo = (w[:, c, :] for w in (wg, wgH, wgL)) if c < 3 * KT else (
                        w[:, c - 3 * KT, :] for w in (wo, woH, woL))
                    dve.tensor_tensor(lo, whole, f32(hi), ALU.subtract).then_inc(w1_lo, 1)

            def steps0(b, scores=False, values=False, after=False, end=False):
                for n in range(ITEMS0):
                    if scores:
                        w = (n % QT + 1) * P
                        dve.wait_ge(s0_pe, b * ITEMS0 + n + 1)
                        dve.tensor_reduce(negmax[:, n:n + 1], bank[n % 2][:, 0:w], AX.X, ALU.max,
                                          negate=True).then_inc(max0, 1)
                    i, batch = at_step(n, 1, b, scores, values)
                    if i is not None and i % ITEMS == ITEMS - 1:
                        g = i // ITEMS
                        nm = negmax[:, g * ITEMS:(g + 1) * ITEMS].rearrange("p (h t) -> p h t", t=QT)
                        hi, mi, lo = (nmp[:, :, SHIFT + j * QT:SHIFT + (j + 1) * QT] for j in range(3))
                        nm_ch.begin((batch * NG + g) * 3)
                        dve.wait_ge(max0, batch * ITEMS0 + i + 1)
                        dve.wait_ge(nm_pe, batch * NG + g)
                        nm_ch.step(dve.tensor_copy(hi, nm))
                        nm_ch.mark(dve.tensor_tensor(nmr[:, :, :], nm, hi, ALU.subtract))
                    i, batch = at_step(n, 2, b, scores, values)
                    if i is not None and i % ITEMS == ITEMS - 1:
                        nm_ch.wait()
                        nm_ch.step(dve.tensor_copy(mi, nmr[:, :, :]))
                        dve.tensor_tensor(lo, nmr[:, :, :], mi, ALU.subtract).then_inc(nm_split, 1)
                    i, batch = at_step(n, VALUE + 2, b, scores, values)
                    if i is not None and i % ITEMS == ITEMS - 1:
                        g = i // ITEMS
                        dve.wait_ge(o_turned, batch * NG + g + 1)
                        pv = bank[4][:, :].rearrange("p (t h d) -> p t h d", t=QT, d=VW)
                        dve.reciprocal(rsum0_t[:, :, :, :], pv[:, :, :, HD0:HD0 + 1]).then_inc(rsum0, 1)
                        dve.wait_ge(rsum0, batch * NG + g + 1)
                        if g == 0:
                            dve.wait_ge(ot_pe, batch * KT)
                        dve.tensor_tensor(
                            oTok[:, :, g * HG * HD0:(g + 1) * HG * HD0].rearrange("p t (h d) -> p t h d", d=HD0),
                            pv[:, :, :, 0:HD0], rsum0_t[:, :, :, :].to_broadcast([P, QT, HG, HD0]),
                            ALU.mult).then_inc(oev0, 1)
                    i, batch = at_step(n, AFTER, b - 1, after, end)
                    if i is not None:
                        if i == ITEMS0 - AFTER:
                            resume.setdefault(i, ch.n)
                            ch.begin(batch * NB0_STEPS)
                            ch.n = resume[i]
                        after0(i, batch, isinstance(batch, int) and batch == NB - 1)

            resume, nm_ch = {}, chains[4]

            steps0(0, scores=True)
            steps0(1, scores=True, values=True, after=True)
            with dve.Fori(2, NB) as b:
                steps0(b, scores=True, values=True, after=True, end=True)
            steps0(NB, values=True, after=True, end=True)
            steps0(NB + 1, end=True)

            ch = chains[3]

            def add_y1(it, b):
                for t2 in range(2):
                    dve.wait_ge(y1_pe, it * 2 + t2 + 1)
                    dve.tensor_tensor(ytmp[:, :, :], bank[5 + t2][:, :].rearrange("p (t d) -> p t d", d=D),
                                      modb(1, b, GA).to_broadcast([P, 2, D]), ALU.mult).then_inc(y1_gated, 1)
                    dve.wait_ge(y1_gated, it * 2 + t2 + 1)
                    dve.tensor_tensor(xb(b, 2 * t2, 2), xb(b, 2 * t2, 2), ytmp[:, :, :], ALU.add).then_inc(x1_add, 1)
                    dve.wait_ge(x1_add, it * 2 + t2 + 1)

            def round1(it, before):
                ch.begin(it * N1_STEPS)
                for u in range(2 * QT):
                    dve.wait_ge(p1_act, it * 3 * QT + u + 1)
                    vector_carrier(dve)
                    for h in range(HG):
                        last = dve.bn_stats(qkst[:, u * HG + h, :], qk[:, u // 2, u % 2, h * HD1:(h + 1) * HD1])
                    last.then_inc(p1_dve, 1)
                dve.wait_ge(p1_dve, (it + 1) * 2 * QT)
                v, w = sm[:, 0, :], sm[:, 2, :]
                me, mo = qkst[:, :, 1], qkst[:, :, 4]
                ch.step(dve.tensor_tensor(v, me, me, ALU.mult))
                ch.step(dve.tensor_tensor(w, mo, mo, ALU.mult))
                ch.step(dve.tensor_tensor(v, v, w, ALU.add))
                ch.step(dve.tensor_tensor(w, qkst[:, :, 2], qkst[:, :, 5], ALU.add))
                ch.step(dve.scalar_tensor_tensor(out=v, in0=w, scalar=2.0 / HD1, in1=v, op0=ALU.mult, op1=ALU.add))
                ch.step(dve.tensor_scalar(v, v, 0.5, EPS, ALU.mult, ALU.add))
                rsqrt_seed(dve, ch, w, sm[:, 1, :], v)
                for _ in range(NEWTON):
                    rsqrt_newton(dve, ch, w, sm[:, 1, :], v)
                ch.wait()
                for u in range(2 * QT):
                    rows = qk[:, u // 2, u % 2, :].rearrange("p (h d) -> p h d", d=HD1)
                    r = sm[:, 2, u * HG:(u + 1) * HG].rearrange("p (h one) -> p h one", one=1)
                    dve.tensor_tensor(rows, rows, r.to_broadcast([P, HG, HD1]), ALU.mult).then_inc(qk_norm, 1)
                if before is not None:
                    add_y1(it - 1, before)
                for s in range(ITEMS + LAG1 + 4):
                    i = s - 2
                    if 0 <= i < ITEMS:
                        n = (i % QT + 1) * P
                        dve.wait_ge(rsum1, it * ITEMS + i + 1)
                        dve.tensor_scalar(probs[:, i % 4, 0:n], probs[:, i % 4, 0:n], rsum[:, i:i + 1], None,
                                          ALU.mult).then_inc(nrm1, 1)
                    if s < ITEMS:
                        i, n = s, (s % QT + 1) * P
                        dve.wait_ge(s1_pe, it * ITEMS + i + 1)
                        dve.tensor_reduce(negmax[:, i:i + 1], bank[SCORE_BANKS[i % 3]][:, 0:n], AX.X, ALU.max,
                                          negate=True).then_inc(max1, 1)
                    i = s - 1
                    if 0 <= i < ITEMS:
                        dve.wait_ge(exp1, it * ITEMS + i + 1)
                        dve.reciprocal(rsum[:, i:i + 1], sums[:, i:i + 1]).then_inc(rsum1, 1)
                    i = s - LAG1 - 3
                    if i >= 0 and i % QT == QT - 1:
                        h = i // QT
                        dve.wait_ge(o1_hi, it * HG + h + 1)
                        dve.tensor_tensor(oL1[:, h, :], bank[7][:, :], f32(oH1[:, h, :]),
                                          ALU.subtract).then_inc(o1_lo, 1)
                assert ch.n == N1_STEPS, ch.n

            def rounds1(g):
                round1(g * NB, None)
                with dve.Fori(1, NB) as b:
                    round1(g * NB + b, b - 1)

            with dve.Fori(0, NG - 1) as g:
                rounds1(g)
                split_w1(g + 1, slice(0, 3 * KT))
                add_y1(g * NB + NB - 1, NB - 1)
                split_w1(g + 1, slice(3 * KT, 3 * KT + HG))
            rounds1(NG - 1)
            add_y1(NG * NB - 1, NB - 1)

            ch = chains[5]

            def swiglu(b, following):
                for m in range(MT):
                    dve.wait_ge(f_silu, b * MT + m + 1)
                    dve.wait_ge(f_hlo, b * MT + max(m - 1, 0))
                    dve.tensor_tensor(hf[:, m % 2, :], bank[2 * (m % 2) + 1][:, :], sg[:, m % 2, :], ALU.mult).then_inc(f_h, 1)
                    if following is not None:
                        if m == 0:
                            ch.begin(following * NORM_STEPS)
                        for part in range(NORM_PARTS - 1)[m * 3:(m + 1) * 3]:
                            norm_f1.dve_part(part, dve, ch, following, following)
                    dve.wait_ge(f_hhi, b * MT + m + 1)
                    dve.tensor_tensor(hmL[:, m, :], hf[:, m % 2, :], f32(hmH[:, m, :]), ALU.subtract).then_inc(f_hlo, 1)
                if following is not None:
                    norm_f1.dve_part(NORM_PARTS - 1, dve, ch, following, following)
                for t2 in range(2):
                    dve.wait_ge(y2_pe, b * 2 + t2 + 1)
                    dve.tensor_tensor(ytmp[:, :, :], bank[4 + t2][:, :].rearrange("p (t d) -> p t d", d=D),
                                      modb(1, b, GB).to_broadcast([P, 2, D]), ALU.mult).then_inc(y2_gated, 1)
                    dve.wait_ge(y2_gated, b * 2 + t2 + 1)
                    dve.tensor_tensor(xb(b, 2 * t2, 2), xb(b, 2 * t2, 2), ytmp[:, :, :], ALU.add).then_inc(x2_add, 1)
                    dve.wait_ge(x2_add, b * 2 + t2 + 1)

            ch.begin(0)
            norm_f1.dve(dve, ch, 0, 0)
            assert ch.n == NORM_STEPS, ch.n
            with dve.Fori(0, NB - 1) as b:
                swiglu(b, b + 1)
            swiglu(NB - 1, None)

        @block.tensor
        def _(pe):
            def modulation(o, c_rows, l, c):
                for k in range(KT):
                    last = pe.matmul(o, c_rows[k], wmod[:, l, k, c * 2 * D:(c + 1) * 2 * D],
                                     start=(k == 0), stop=(k == KT - 1))
                last.then_inc(mod_pe, 1)

            pe.wait_ge(cb_ready, 1)
            pe.wait_ge(loaded_m0, 16)
            for b in range(NB):
                if b >= 2:
                    pe.wait_ge(mod_done, b - 1)
                modulation(bank[4 + b % 2][:, :], [cB0[:, k, b, :] for k in range(KT)], 0, 0)
            norm_a0.pe(pe, 0)
            pe.wait_ge(w0_lo, 1)
            pe.wait_ge(loaded_m, 32)

            def qkv0(b, following):
                norm_a0.wait_ready(pe, b)
                for m in range(KT + 1):
                    if m < KT:
                        pe.wait_ge(q_scaled, b * KT)
                    else:
                        pe.wait_ge(k_read, b)
                    cols = slice(m * P, (m + 1) * P)
                    for k in range(KT):
                        last = mm3(pe, bank[m][:, :], w0H[:, k, cols], w0L[:, k, cols], hH[:, k, :], hL[:, k, :],
                                   k == 0, k == KT - 1)
                    last.then_inc(qkv_pe, 1)
                pe.wait_ge(v_read, b)
                for t in range(QT):
                    rows = slice(t * P, (t + 1) * P)
                    for k in range(KT):
                        last = mm3(pe, bank[3][:, t * HD0:(t + 1) * HD0], hH[:, k, rows], hL[:, k, rows],
                                   w0H[:, k, WV], w0L[:, k, WV], k == 0, k == KT - 1)
                last.then_inc(qkv_pe, 1)
                if following is not None:
                    norm_a0.pe(pe, following)
                pe.wait_ge(cb_ready, b + 2)
                for j, (l, c) in enumerate(LATER_MODS):
                    pe.wait_ge(mod_done, NB + b * len(LATER_MODS) + max(j - 1, 0))
                    modulation(bank[4 + j % 2][:, :], [cB[:, l, k, 0, :] for k in range(KT)], l, c)

            with pe.Fori(0, NB - 1) as b:
                qkv0(b, b + 1)
            qkv0(NB - 1, None)
            pe.wait_ge(mod_done, NB + NB * len(LATER_MODS))
            pe.wait_ge(k_read, NB)
            pe.wait_ge(v_read, NB)

            def after0(n, b):
                if n == 1:
                    pe.wait_ge(oev0, (b + 1) * NG)
                    for k in range(KT):
                        for t in range(QT):
                            last = pe.transpose(bank[6 + k][:, t * P:(t + 1) * P], oTok[:, t, k * P:(k + 1) * P], identf[:, :])
                        last.then_inc(ot_pe, 1)
                elif n == 7:
                    pe.wait_ge(ot_lo, (b + 1) * KT)
                    for t in range(QT):
                        rows = slice(t * P, (t + 1) * P)
                        for k in range(KT):
                            last = mm3(pe, bank[6 + t // 2][:, (t % 2) * D:(t % 2 + 1) * D], oH0[:, k, rows], oL0[:, k, rows],
                                       w0H[:, k, WO], w0L[:, k, WO], k == 0, k == KT - 1)
                        if t % 2:
                            last.then_inc(y0_pe, 1)
                elif n == 24:
                    norm_f0.pe(pe, b)
                elif n == 27:
                    norm_f0.wait_ready(pe, b)
                    for t in range(QT):
                        rows = slice(t * P, (t + 1) * P)
                        for k in range(KT):
                            last = mm3(pe, bank[6][:, t * NE:(t + 1) * NE], hH[:, k, rows], hL[:, k, rows],
                                       w0H[:, k, WR], w0L[:, k, WR], k == 0, k == KT - 1)
                    last.then_inc(r_pe, 1)
                elif n == 37:
                    pe.wait_ge(r_w, b + 1)
                    tensor_carrier(pe, bank[7][:, 0:P])
                    for t in range(QT):
                        last = pe.transpose(bank[7][0:NE, t * P:(t + 1) * P], ex[:, t, :], identf[:, :])
                    last.then_inc(r_tp, 1)
                elif n == 39:
                    pe.wait_ge(r_wT, b + 1)
                    for t in range(QT):
                        last = pe.matmul(bank[6 + t // 2][:, (t % 2) * D:(t % 2 + 1) * D], wT[:, t * P:(t + 1) * P], ebias[:, :],
                                         start=True, stop=True)
                    last.then_inc(r_y, 1)
                elif n == 59:
                    norm_a1.pe(pe, b)

            def steps0(b, scores=False, values=False, after=False, end=False):
                for n in range(ITEMS0):
                    i, batch = at_step(n, 3, b, scores, values)
                    if i is not None and i % ITEMS == ITEMS - 1:
                        g = i // ITEMS
                        pe.wait_ge(nm_split, batch * NG + g + 1)
                        if not isinstance(batch, int) or batch * NG + g > 0:
                            pe.wait_ge(oev0, batch * NG + g - 1)
                        for h in range(HG):
                            last = pe.matmul(bank[4][:, h * P:(h + 1) * P], nmp[:, h, :], identb[:, :], start=True, stop=True)
                        last.then_inc(nm_pe, 1)
                    i, batch = at_step(n, TURN, b, scores, values)
                    if i is not None:
                        h, k = i // QT, i % QT
                        w = SEQ - k * P
                        if i % ITEMS == 0:
                            pe.wait_ge(nm_ready, (batch * NG + i // ITEMS + 1) * QT)
                        pe.wait_ge(exp0, batch * ITEMS0 + max(i - 1, 0))
                        pe.matmul(bank[2 + i % 2][:, 0:w], kst[:, bass.ds(batch * SEQ + k * P, P)],
                                  qst[:, h * SEQ + k * P:(h + 1) * SEQ], start=True, stop=False)
                        pe.matmul(bank[2 + i % 2][:, 0:P], identb[:, :], maskT[:, :], start=False,
                                  stop=True).then_inc(st_pe, 1)
                    if scores:
                        h, t = n // QT, n % QT
                        w = (t + 1) * P
                        if n % ITEMS == 0:
                            pe.wait_ge(q_loaded[n // ITEMS], (b + 1) * SLOTS * 16)
                        pe.wait_ge(max0, b * ITEMS0 + max(n - 1, 0))
                        pe.matmul(bank[n % 2][:, 0:w], qst[0:SHIFT, h * SEQ + t * P:h * SEQ + w],
                                  kst[0:SHIFT, bass.ds(b * SEQ, w)], start=True, stop=False)
                        pe.matmul(bank[n % 2][:, t * P:w], identb[:, :], maskb[:, :], start=False,
                                  stop=True).then_inc(s0_pe, 1)
                    i, batch = at_step(n, VALUE, b, scores, values)
                    if i is not None:
                        h, k = i // QT, i % QT
                        rows = slice(h % HG * VW, (h % HG + 1) * VW)
                        if i == 0:
                            pe.wait_ge(v_moved, batch + 1)
                        if i % ITEMS == 0:
                            pe.wait_ge(o_copied, batch * NG + i // ITEMS)
                        pe.wait_ge(exp0, batch * ITEMS0 + i + 1)
                        pe.matmul(bank[5][rows, k * P:], vS[:, k, :], probs[:, i % 4, 0:SEQ - k * P],
                                  start=(k == 0), stop=(k == QT - 1)).then_inc(pv0, 1)
                    i, batch = at_step(n, VALUE + 2, b, scores, values)
                    if i is not None and i % ITEMS == ITEMS - 1:
                        pe.wait_ge(o_copied, batch * NG + i // ITEMS + 1)
                        for t in range(QT):
                            last = pe.transpose(bank[4][:, t * P:(t + 1) * P], oRaw[:, t * P:(t + 1) * P], identf[:, :])
                        last.then_inc(o_turned, 1)
                    i, batch = at_step(n, AFTER, b - 1, after, end)
                    if i is not None:
                        after0(i, batch)

            steps0(0, scores=True)
            steps0(1, scores=True, values=True, after=True)
            with pe.Fori(2, NB) as b:
                steps0(b, scores=True, values=True, after=True, end=True)
            steps0(NB, values=True, after=True, end=True)
            steps0(NB + 1, end=True)

            def out_proj1(it):
                for t in range(QT):
                    rows = slice(t * P, (t + 1) * P)
                    for h in range(HG):
                        if t == 0:
                            pe.wait_ge(o1_lo, it * HG + h + 1)
                        last = mm3(pe, bank[5 + t // 2][:, (t % 2) * D:(t % 2 + 1) * D], oH1[:, h, rows], oL1[:, h, rows],
                                   woH[:, h, :], woL[:, h, :], h == 0, h == HG - 1)
                    if t % 2:
                        last.then_inc(y1_pe, 1)

            def round1(g, it, first):
                pe.wait_ge(w1_lo, g * (3 * KT + HG) + (3 * KT if first else 3 * KT + HG))
                pe.wait_ge(h1_loaded, (it + 1) * 32)
                pe.wait_ge(exp1, it * ITEMS)
                for u in range(3 * QT):
                    t, c = (u // 2, u % 2) if u < 2 * QT else (u - 2 * QT, 2)
                    if u >= 3:
                        pe.wait_ge(p1_act, it * 3 * QT + u - 2)
                    else:
                        pe.wait_ge(tr_act, it * 2 * QT)
                    rows = slice(t * P, (t + 1) * P)
                    for k in range(KT):
                        w = c * KT + k
                        last = mm3(pe, bank[u % 3][:, :], hH[:, k, rows], hL[:, k, rows], wgH[:, w, :], wgL[:, w, :],
                                   k == 0, k == KT - 1)
                    last.then_inc(p1_pe, 1)
                if not first:
                    out_proj1(it - 1)
                pe.wait_ge(p1_act, (it + 1) * 3 * QT)
                for u in range(2 * QT):
                    pe.wait_ge(qk_norm, it * 2 * QT + u + 1)
                    if u >= 3:
                        pe.wait_ge(tr_act, it * 2 * QT + u - 2)
                    for h in range(HG):
                        last = pe.transpose(bank[u % 3][:, h * P:(h + 1) * P],
                                            qk[:, u // 2, u % 2, h * HD1:(h + 1) * HD1], identf[:, :])
                    last.then_inc(tr_pe, 1)
                for s in range(ITEMS + LAG1 + 1):
                    if s < ITEMS:
                        i, h, t = s, s // QT, s % QT
                        n = (t + 1) * P
                        if i < QT:
                            pe.wait_ge(tr_act, it * 2 * QT + 2 * (t + 1))
                        pe.wait_ge(exp1, it * ITEMS + max(i - 2, 0))
                        pe.matmul(bank[SCORE_BANKS[i % 3]][:, 0:n], qT[:, h, t * P:n], kT[:, h, 0:n], start=True, stop=False)
                        pe.matmul(bank[SCORE_BANKS[i % 3]][:, t * P:n], identb[:, :], maskb[:, :], start=False,
                                  stop=True).then_inc(s1_pe, 1)
                    i = s - LAG1
                    if 0 <= i < ITEMS:
                        t = i % QT
                        if i == 0:
                            pe.wait_ge(x1_add, it * 2)
                        pe.wait_ge(nrm1, it * ITEMS + i + 1)
                        pe.wait_ge(ev1, it * ITEMS + max(i - 1, 0))
                        for k in range(t + 1):
                            last = pe.transpose(bank[5 + i % 2][:, k * P:(k + 1) * P],
                                                probs[:, i % 4, k * P:(k + 1) * P], identf[:, :])
                        last.then_inc(t1_pe, 1)
                    i = s - LAG1 - 1
                    if 0 <= i and i % QT == QT - 1:
                        h = i // QT
                        pe.wait_ge(ev1, it * ITEMS + i + 1)
                        pe.wait_ge(o1_lo, it * HG + h)
                        for t in range(QT):
                            for k in range(t + 1):
                                at = (t * (t + 1) // 2 + k) * P
                                last = pe.matmul(bank[7][:, t * P:(t + 1) * P], v1[:, k, h * HD1:(h + 1) * HD1],
                                                 pT1[:, h % 2, at:at + P], start=(k == 0), stop=(k == t))
                        last.then_inc(pv1, 1)

            with pe.Fori(0, NG) as g:
                round1(g, g * NB, True)
                with pe.Fori(1, NB) as b:
                    round1(g, g * NB + b, False)
                out_proj1(g * NB + NB - 1)

            def swiglu(b, following):
                norm_f1.wait_ready(pe, b)
                for m in range(MT):
                    pe.wait_ge(f_h, b * MT + max(m - 1, 0))
                    for w in range(2):
                        for k in range(KT):
                            last = mm3(pe, bank[2 * (m % 2) + w][:, :], wguH[:, w, k, m * P:(m + 1) * P],
                                       wguL[:, w, k, m * P:(m + 1) * P], hH[:, k, :], hL[:, k, :], k == 0, k == KT - 1)
                    last.then_inc(gu_pe, 1)
                if following is not None:
                    norm_f1.pe(pe, following)
                pe.wait_ge(x2_add, b * 2)
                for t in range(QT):
                    rows = slice(t * P, (t + 1) * P)
                    for m in range(MT):
                        if t == 0:
                            pe.wait_ge(f_hlo, b * MT + m + 1)
                        last = mm3(pe, bank[4 + t // 2][:, (t % 2) * D:(t % 2 + 1) * D], hmH[:, m, rows], hmL[:, m, rows],
                                   wdH[:, m, :], wdL[:, m, :], m == 0, m == MT - 1)
                    if t % 2:
                        last.then_inc(y2_pe, 1)

            pe.wait_ge(f_zero, 2)
            pe.wait_ge(f_lo, 2 * KT + 2)
            norm_f1.pe(pe, 0)
            with pe.Fori(0, NB - 1) as b:
                swiglu(b, b + 1)
            swiglu(NB - 1, None)


RSQRT_STEPS = 2 + 3 * NEWTON
NORM_STEPS = 2 + 2 + RSQRT_STEPS + 2 + 2
QK0_STEPS = KT + 5
NB0_STEPS = 2 * 4 + 4 + NORM_STEPS + 1 + 2 + 4 + 1 + 4 + NORM_STEPS
N1_STEPS = 5 + 1 + RSQRT_STEPS


def kernel(**inputs):
    import numpy as np
    import concourse.bacc as bacc
    from concourse.bass_utils import run_bass_kernel_spmd

    i = {k: np.asarray(v) for k, v in inputs.items()}
    kmask = np.zeros((P, 4 + QT), np.float32)
    kmask[SHIFT:, 3] = 1
    for part in range(3):
        for t in range(QT):
            kmask[SHIFT + part * QT + t, 4 + t] = 1
    for s, part in enumerate(K_SLOT):
        kmask[s * HD0:(s + 1) * HD0, part] = 1
    wk, wv = i["L0_attn_Wkv"][:HD0], i["L0_attn_Wkv"][HD0:]
    wqkv = np.stack([i[f"L1_attn_W{c}"].T for c in "qkv"]).reshape(3, KT, P, NG, HG * HD1)
    arrays = {
        "x": i["L0_attn_x"],
        "cT": np.stack([i[f"L{l}_c"].T for l in range(2)]).reshape(2, KT, P, NB).transpose(2, 0, 1, 3),
        "wmod0": i["L0_wmod"],
        "wmod1": i["L1_wmod"],
        "wq0": i["L0_attn_Wq"].T,
        "wk0": np.tile(wk.T, (1, P // HD0)),
        "wv0": wv.T,
        "wo0": i["L0_attn_Wo"].T,
        "wr": i["L0_ffn_router_weight"].T,
        "ebias": i["L0_ffn_expert_bias"],
        "rbias": i["L0_ffn_router_bias"].reshape(1, NE),
        "kmask": kmask,
        "wqkv": wqkv.transpose(3, 2, 0, 1, 4).reshape(NG, P, 3 * KT * HG * HD1),
        "wo1": i["L1_attn_Wo"].T.reshape(NG, HG * HD1, D),
        "gqk": np.stack([i["L1_attn_gq"], i["L1_attn_gk"]], axis=1),
        "lut": i["L1_ffn_lut"].reshape(1, LUT),
        "idx_gate": i["L1_ffn_gate_idx"].T,
        "idx_up": i["L1_ffn_up_idx"].T,
        "idx_down": i["L1_ffn_down_idx"].T,
    }
    arrays = {k: np.ascontiguousarray(v) for k, v in arrays.items()}
    nc = bacc.Bacc("TRN2", target_bir_lowering=False, num_devices=1)
    aps = {k: nc.dram_tensor(f"in_{k}", v.shape, mybir.dt.from_np(v.dtype), kind="ExternalInput").ap()
           for k, v in arrays.items()}
    out = nc.dram_tensor("out", (NB, SEQ, D), F32, kind="ExternalOutput").ap()
    build(nc, aps, out)
    r = run_bass_kernel_spmd(nc, [{f"in_{k}": v for k, v in arrays.items()}], core_ids=[0])
    return r.results[0]["out"]
```
